# Optimizing a Trainium2 kernel written in Bass

```python
import numpy as np
import jax
import jax.numpy as jnp

def _softmax(x, axis=-1):
    return jax.nn.softmax(x, axis=axis)

def _gelu(x):
    return jax.nn.gelu(x, approximate=True)

def _silu(x):
    return jax.nn.silu(x)

def _sigmoid(x):
    return jax.nn.sigmoid(x)

def _layernorm(x, axis=-1, eps=1e-05):
    m = jnp.mean(x, axis=axis, keepdims=True)
    v = jnp.var(x, axis=axis, keepdims=True)
    return (x - m) / jnp.sqrt(v + eps)

def _scatter_add(tgt, idx, src, axis=0):
    return tgt.at[idx].add(src)

def _segment_sum(src, seg, n):
    return jax.ops.segment_sum(src, seg, n)
kernel_name = 'mk_gnn_ffn_d2_gnn_r32_519d69'

def setup_inputs(seed: int=0):
    np.random.seed(seed)
    _w = jnp.asarray

    def _rec_inputs():
        import jax
        import jax.numpy as jnp
        _gk = jax.random.key(seed)
        x = -0.0002117 + 1 * jax.random.normal(jax.random.fold_in(_gk, 1), (3125, 256), jnp.float32)
        src = jax.random.randint(jax.random.fold_in(_gk, 2), (50000,), 0, 3125, jnp.int32)
        dst = jnp.minimum((3125 * jax.random.uniform(jax.random.fold_in(_gk, 3), (50000,)) ** 2.0).astype(jnp.int32), 99999)
        _o = jnp.argsort(dst, stable=True)
        src = src[_o]
        dst = dst[_o]
        edge_weight = jax.random.uniform(jax.random.fold_in(_gk, 13), (50000,), jnp.float32, 0.0, 1)
        return (x, src, dst, edge_weight)
    x, src, dst, edge_weight = _rec_inputs()

    def _L0_gnn_setup():
        import jax, jax.numpy as jnp
        import numpy as np
        N_NODES = 3125
        N_EDGES = 100000
        IN_C = 256
        OUT_C = 256
        key = jax.random.key(seed)
        k1, k2, k3, k4, k5 = jax.random.split(key, 5)
        limit = float(np.sqrt(6.0 / (IN_C + OUT_C)))
        W = jax.random.uniform(k2, (IN_C, OUT_C), jnp.float32, -limit, limit)
        return {'x': jax.random.normal(k1, (N_NODES, IN_C), jnp.float32), 'W': W, 'bias': jnp.zeros((OUT_C,), jnp.float32), 'edge_row': jax.random.randint(k3, (N_EDGES,), 0, N_NODES, jnp.int32), 'edge_col': jax.random.randint(k4, (N_EDGES,), 0, N_NODES, jnp.int32), 'edge_val': jax.random.uniform(k5, (N_EDGES,), jnp.float32)}
    _L0_gnn_all = _L0_gnn_setup()
    _L0_gnn_in = {k: v for k, v in _L0_gnn_all.items() if k in ('W', 'bias')}
    del _L0_gnn_all

    def _L0_ffn_setup():
        import jax, jax.numpy as jnp
        import numpy as np
        NUM_EXPERTS = 8
        TOP_K = 2
        B, S, D = (8, 256, 256)

        def _moe(tokens, router_w, w1, b1, w2, b2):
            N = tokens.shape[0]
            E = router_w.shape[0]
            logits = tokens.astype(jnp.float32) @ router_w.astype(jnp.float32).T
            probs = jax.nn.softmax(logits, axis=-1)
            rw, re = jax.lax.top_k(probs, TOP_K)
            if TOP_K > 1:
                rw = rw / jnp.maximum(rw.sum(-1, keepdims=True), 1e-12)
            rw = rw.astype(tokens.dtype)
            combine = jnp.zeros((N, E), tokens.dtype).at[jnp.arange(N)[:, None], re].set(rw)
            out = tokens
            for e in range(E):
                h = jax.nn.gelu(tokens @ w1[e] + b1[e], approximate=False)
                y = h @ w2[e] + b2[e]
                out = out + combine[:, e:e + 1] * y
            return out
        key = jax.random.key(seed)
        ks = jax.random.split(key, 4)
        scale = 1.0 / np.sqrt(D).astype(np.float32)
        return {'input_embeddings': jax.random.normal(ks[0], (B, S, D), jnp.float32), 'router_w': jax.random.normal(ks[1], (NUM_EXPERTS, D), jnp.float32) * scale, 'w1': jax.random.normal(ks[2], (NUM_EXPERTS, D, D), jnp.float32) * scale, 'b1': jnp.zeros((NUM_EXPERTS, D), jnp.float32), 'w2': jax.random.normal(ks[3], (NUM_EXPERTS, D, D), jnp.float32) * scale, 'b2': jnp.zeros((NUM_EXPERTS, D), jnp.float32)}
    _L0_ffn_all = _L0_ffn_setup()
    _L0_ffn_in = {k: v for k, v in _L0_ffn_all.items() if k in ('router_w', 'w1', 'b1', 'w2', 'b2')}
    del _L0_ffn_all

    def _L1_gnn_setup():
        import jax, jax.numpy as jnp
        import numpy as np
        N_NODES = 3125
        D = 256
        N_LAYERS = 3
        N_EDGES = 100000
        BN_EPS = 1e-05

        def _bn_train(x, gamma, beta):
            m = jnp.mean(x, axis=0)
            v = jnp.var(x, axis=0)
            return gamma * (x - m) * jax.lax.rsqrt(v + BN_EPS) + beta
        key = jax.random.key(seed)
        ks = jax.random.split(key, 16)
        s = 1.0 / np.sqrt(D)
        inp = {'x': jax.random.normal(ks[0], (N_NODES, D), dtype=jnp.float32), 'edge_index': jax.random.randint(ks[1], (2, N_EDGES), 0, N_NODES, dtype=jnp.int64 if jax.config.jax_enable_x64 else jnp.int32), 'edge_weight': jax.random.uniform(ks[2], (N_EDGES,), dtype=jnp.float32), 'W_in': jax.random.uniform(ks[3], (D, D), jnp.float32, -s, s), 'b_in': jax.random.uniform(ks[4], (D,), jnp.float32, -s, s), 'W1': jax.random.uniform(ks[5], (N_LAYERS, D, D), jnp.float32, -s, s), 'b1': jax.random.uniform(ks[6], (N_LAYERS, D), jnp.float32, -s, s), 'g1': jnp.ones((N_LAYERS, D), jnp.float32), 'be1': jnp.zeros((N_LAYERS, D), jnp.float32), 'W2': jax.random.uniform(ks[7], (N_LAYERS, D, D), jnp.float32, -s, s), 'b2': jax.random.uniform(ks[8], (N_LAYERS, D), jnp.float32, -s, s), 'g_out': jnp.ones((N_LAYERS, D), jnp.float32), 'b_out': jnp.zeros((N_LAYERS, D), jnp.float32)}
        return inp
    _L1_gnn_all = _L1_gnn_setup()
    _L1_gnn_in = {k: v for k, v in _L1_gnn_all.items() if k in ('W_in', 'b_in', 'W1', 'b1', 'g1', 'be1', 'W2', 'b2', 'g_out', 'b_out')}
    del _L1_gnn_all

    def _L1_ffn_setup():
        import jax, jax.numpy as jnp
        import numpy as np
        B, S, D, F, E, K = (8, 64, 256, 1024, 8, 2)
        key = jax.random.key(seed)
        ks = jax.random.split(key, 10)
        s = 0.02
        return {'x': jax.random.normal(ks[0], (B, S, D), dtype=jnp.float32), 'Wr': jax.random.normal(ks[1], (D, E), dtype=jnp.float32) * s, 'W1s': jax.random.normal(ks[2], (D, F), dtype=jnp.float32) * s, 'b1s': jnp.zeros((F,), dtype=jnp.float32), 'W2s': jax.random.normal(ks[3], (F, D), dtype=jnp.float32) * s, 'b2s': jnp.zeros((D,), dtype=jnp.float32), 'W1p': jax.random.normal(ks[4], (E, D, F), dtype=jnp.float32) * s, 'b1p': jnp.zeros((E, F), dtype=jnp.float32), 'W2p': jax.random.normal(ks[5], (E, F, D), dtype=jnp.float32) * s, 'b2p': jnp.zeros((E, D), dtype=jnp.float32)}
    _L1_ffn_all = _L1_ffn_setup()
    _L1_ffn_in = {k: v for k, v in _L1_ffn_all.items() if k in ('Wr', 'W1s', 'b1s', 'W2s', 'b2s', 'W1p', 'b1p', 'W2p', 'b2p')}
    del _L1_ffn_all
    return {'x': x, 'src': src, 'dst': dst, 'edge_weight': edge_weight, 'L0_gnn_W': _L0_gnn_in['W'], 'L0_gnn_bias': _L0_gnn_in['bias'], 'L0_ffn_router_w': _L0_ffn_in['router_w'], 'L0_ffn_w1': _L0_ffn_in['w1'], 'L0_ffn_b1': _L0_ffn_in['b1'], 'L0_ffn_w2': _L0_ffn_in['w2'], 'L0_ffn_b2': _L0_ffn_in['b2'], 'L1_gnn_W_in': _L1_gnn_in['W_in'], 'L1_gnn_b_in': _L1_gnn_in['b_in'], 'L1_gnn_W1': _L1_gnn_in['W1'], 'L1_gnn_b1': _L1_gnn_in['b1'], 'L1_gnn_g1': _L1_gnn_in['g1'], 'L1_gnn_be1': _L1_gnn_in['be1'], 'L1_gnn_W2': _L1_gnn_in['W2'], 'L1_gnn_b2': _L1_gnn_in['b2'], 'L1_gnn_g_out': _L1_gnn_in['g_out'], 'L1_gnn_b_out': _L1_gnn_in['b_out'], 'L1_ffn_Wr': _L1_ffn_in['Wr'], 'L1_ffn_W1s': _L1_ffn_in['W1s'], 'L1_ffn_b1s': _L1_ffn_in['b1s'], 'L1_ffn_W2s': _L1_ffn_in['W2s'], 'L1_ffn_b2s': _L1_ffn_in['b2s'], 'L1_ffn_W1p': _L1_ffn_in['W1p'], 'L1_ffn_b1p': _L1_ffn_in['b1p'], 'L1_ffn_W2p': _L1_ffn_in['W2p'], 'L1_ffn_b2p': _L1_ffn_in['b2p']}

def reference(x, src, dst, edge_weight, L0_gnn_W, L0_gnn_bias, L0_ffn_router_w, L0_ffn_w1, L0_ffn_b1, L0_ffn_w2, L0_ffn_b2, L1_gnn_W_in, L1_gnn_b_in, L1_gnn_W1, L1_gnn_b1, L1_gnn_g1, L1_gnn_be1, L1_gnn_W2, L1_gnn_b2, L1_gnn_g_out, L1_gnn_b_out, L1_ffn_Wr, L1_ffn_W1s, L1_ffn_b1s, L1_ffn_W2s, L1_ffn_b2s, L1_ffn_W1p, L1_ffn_b1p, L1_ffn_W2p, L1_ffn_b2p):
    import jax
    import jax.numpy as jnp

    def _L0_gnn_ref(x, W, bias, edge_row, edge_col, edge_val):
        import jax, jax.numpy as jnp
        import numpy as np
        N_NODES = 3125
        N_EDGES = 100000
        IN_C = 256
        OUT_C = 256
        h = x @ W
        msgs = h[edge_col] * edge_val[:, None]
        agg = jax.ops.segment_sum(msgs, edge_row, num_segments=N_NODES)
        return agg + bias

    def _L0_ffn_ref(input_embeddings, router_w, w1, b1, w2, b2):
        import jax, jax.numpy as jnp
        import numpy as np
        NUM_EXPERTS = 8
        TOP_K = 2
        B, S, D = (8, 256, 256)

        def _moe(tokens, router_w, w1, b1, w2, b2):
            N = tokens.shape[0]
            E = router_w.shape[0]
            logits = tokens.astype(jnp.float32) @ router_w.astype(jnp.float32).T
            probs = jax.nn.softmax(logits, axis=-1)
            rw, re = jax.lax.top_k(probs, TOP_K)
            if TOP_K > 1:
                rw = rw / jnp.maximum(rw.sum(-1, keepdims=True), 1e-12)
            rw = rw.astype(tokens.dtype)
            combine = jnp.zeros((N, E), tokens.dtype).at[jnp.arange(N)[:, None], re].set(rw)
            out = tokens
            for e in range(E):
                h = jax.nn.gelu(tokens @ w1[e] + b1[e], approximate=False)
                y = h @ w2[e] + b2[e]
                out = out + combine[:, e:e + 1] * y
            return out
        b, s, d = input_embeddings.shape
        tokens = input_embeddings.reshape(b * s, d)
        return _moe(tokens, router_w, w1, b1, w2, b2).reshape(b, s, d)

    def _L1_gnn_ref(x, edge_index, edge_weight, W_in, b_in, W1, b1, g1, be1, W2, b2, g_out, b_out):
        import jax, jax.numpy as jnp
        import numpy as np
        N_NODES = 3125
        D = 256
        N_LAYERS = 3
        N_EDGES = 100000
        BN_EPS = 1e-05

        def _bn_train(x, gamma, beta):
            m = jnp.mean(x, axis=0)
            v = jnp.var(x, axis=0)
            return gamma * (x - m) * jax.lax.rsqrt(v + BN_EPS) + beta
        row, col = (edge_index[0], edge_index[1])
        h = x @ W_in + b_in
        for l in range(N_LAYERS):
            msgs = edge_weight[:, None] * h[col]
            pooled = jax.ops.segment_sum(msgs, row, num_segments=N_NODES) + h
            hid = jax.nn.relu(_bn_train(pooled @ W1[l] + b1[l], g1[l], be1[l]))
            rep = hid @ W2[l] + b2[l]
            h = jax.nn.relu(_bn_train(rep, g_out[l], b_out[l]))
        return h

    def _L1_ffn_ref(x, Wr, W1s, b1s, W2s, b2s, W1p, b1p, W2p, b2p):
        import jax, jax.numpy as jnp
        import numpy as np
        B, S, D, F, E, K = (8, 64, 256, 1024, 8, 2)
        gelu = lambda t: jax.nn.gelu(t, approximate=False)
        shared = gelu(x @ W1s + b1s) @ W2s + b2s
        rw = jax.nn.softmax(x @ Wr, axis=-1)
        topw, topi = jax.lax.top_k(rw, K)
        topw = topw / jnp.sum(topw, axis=-1, keepdims=True)
        mask = jnp.sum(jax.nn.one_hot(topi, E, dtype=topw.dtype) * topw[..., None], axis=-2)
        h = gelu(jnp.einsum('bsd,edf->bsef', x, W1p) + b1p)
        priv = jnp.einsum('bsef,efd->bsed', h, W2p) + b2p
        routed = jnp.einsum('bsed,bse->bsd', priv, mask)
        return shared + routed
    edge_index = jnp.stack([src, dst])
    x = x + _L0_gnn_ref(_layernorm(x, axis=-1), L0_gnn_W, L0_gnn_bias, src, dst, edge_weight)
    x = x + _L0_ffn_ref(_layernorm(x, axis=-1)[None], L0_ffn_router_w, L0_ffn_w1, L0_ffn_b1, L0_ffn_w2, L0_ffn_b2)[0]
    x = x + _L1_gnn_ref(_layernorm(x, axis=-1), edge_index, edge_weight, L1_gnn_W_in, L1_gnn_b_in, L1_gnn_W1, L1_gnn_b1, L1_gnn_g1, L1_gnn_be1, L1_gnn_W2, L1_gnn_b2, L1_gnn_g_out, L1_gnn_b_out)
    x = x + _L1_ffn_ref(_layernorm(x, axis=-1)[None], L1_ffn_Wr, L1_ffn_W1s, L1_ffn_b1s, L1_ffn_W2s, L1_ffn_b2s, L1_ffn_W1p, L1_ffn_b1p, L1_ffn_W2p, L1_ffn_b2p)[0]
    return x

_drawn_inputs = setup_inputs


def setup_inputs(seed=0):
    import zlib

    import numpy as np

    out = dict(_drawn_inputs(seed))
    spreads = {'L0_gnn_bias': (0.0, 0.1),
     'L0_ffn_b1': (0.0, 0.5),
     'L0_ffn_b2': (0.0, 0.345),
     'L1_gnn_g1': (1.0, 0.2),
     'L1_gnn_be1': (0.0, 0.1),
     'L1_gnn_g_out': (1.0, 0.2),
     'L1_gnn_b_out': (0.0, 0.1),
     'L1_ffn_b1s': (0.0, 0.8),
     'L1_ffn_b2s': (0.0, 0.296),
     'L1_ffn_b1p': (0.0, 0.8),
     'L1_ffn_b2p': (0.0, 0.403)}
    factors = {'L1_gnn_b_in': 2.944, 'L1_gnn_b1': 8.0, 'L1_gnn_b2': 8.0}
    for name, (base, spread) in spreads.items():
        noise = np.random.default_rng([zlib.crc32(name.encode()), seed]).standard_normal(out[name].shape)
        drawn = base * np.exp(spread * noise) if base else spread * noise
        out[name] = jnp.asarray(drawn.astype(out[name].dtype))
    for name, factor in factors.items():
        out[name] = (out[name] * factor).astype(out[name].dtype)
    return out
```

```python
import concourse.bass as bass
from concourse import mybir
from contextlib import ExitStack, contextmanager

fp32 = mybir.dt.float32
int32 = mybir.dt.int32
ALU = mybir.AluOpType
ACT = mybir.ActivationFunctionType
AXIS = mybir.AxisListType

N = 3125
D = 256
P = 125
NT = N // P
KD = D // 128
E = 50000
EJ = E // P
TOP = 2
NX = 8
SLOT = 128
EDGE_TILES = (E + NT * (SLOT - 1)) // SLOT
ROUND = 16
EDGE_PAD = -(-EDGE_TILES // ROUND) * ROUND
BANKS = 8
MOE_TILES = (TOP * N + NX * (SLOT - 1)) // SLOT
SHARED_TILES = -(-N // SLOT)
LN_EPS = 1e-5
BN_EPS = 1e-5
U = 5
CH = 500
CHUNKS = [(s, min(CH, N - s)) for s in range(0, N, CH)]


class Program:

    def __init__(self, nc, ctx):
        self.nc, self.ctx = nc, ctx
        self.own_sems, self.used_sems = [], []
        self.pool_sems = [self.sem(f"arrived{k}") for k in range(ROUND)]
        self.pool_count = [0] * ROUND

    def sb(self, name, shape, dt=fp32, ctx=None):
        return (ctx or self.ctx).enter_context(self.nc.sbuf_tensor(name, shape, dt))

    def arrivals(self, n, total):
        taken = [Arrival(self.pool_sems[k], self.pool_count[k]) for k in range(n)]
        for k in range(n):
            self.pool_count[k] += total[k] if isinstance(total, list) else total
        return taken

    def sem(self, name, ctx=None):
        handle = (ctx or self.ctx).enter_context(self.nc.semaphore(name))
        if ctx is not None:
            self.own_sems.append(handle.num)
        return handle

    @contextmanager
    def block(self):
        with self.nc.Block() as block:
            yield block
        self.used_sems, self.own_sems = self.own_sems, []

    def clear_used(self, pool):
        nums, self.used_sems = sorted(self.used_sems), []
        while nums:
            n = next((k for k in range(1, len(nums)) if nums[k] != nums[0] + k), len(nums))
            pool.sem_clear(range(nums[0], nums[0] + n))
            nums = nums[n:]


class Arrival:

    def __init__(self, sem, base):
        self.sem, self.base = sem, base

    def wait(self, eng, value):
        eng.wait_ge(self.sem, value + self.base)


class Chain:

    def __init__(self, eng, sem):
        self.eng, self.sem, self.n = eng, sem, 0

    def __call__(self, ins):
        self.n += 1
        ins.then_inc(self.sem, 1)
        self.eng.wait_ge(self.sem, self.n)


def load_weight_chunks(eng, dst, src, sem):
    eng.dma_start(dst, src.rearrange("(k p) m -> p k m", p=128)).then_inc(sem, 16)


def bucket_slots(nc, step, dve, oh, cum, J, B, buf, tot_ready, tot_done, slots):
    flat = "p b j -> p (b j)"
    step(nc.vector.tensor_tensor_scan(cum.rearrange(flat), oh.rearrange(flat), oh.rearrange(flat),
                                      0.0, ALU.add, ALU.max))
    last = cum[:, :, J - 1]
    before, total = buf["before"], buf["total"]
    step(nc.vector.memset(before[:, 0:1], 0.0))
    step(nc.vector.tensor_copy(before[:, 1:B], last[:, 0:B - 1]))
    nc.vector.tensor_tensor(total[:, 0:B], last, before[:, 0:B], ALU.subtract).then_inc(tot_ready, 1)
    dve.wait_ge(tot_done, 1)
    ti, tf, start, base = buf["ti"], buf["tf"], buf["start"], buf["base"]
    step(nc.vector.tensor_scalar(ti[:, 0:B], buf["ps_all"], float(SLOT - 1), None, ALU.add))
    step(nc.vector.tensor_scalar(ti[:, 0:B], ti[:, 0:B], 7, None, ALU.arith_shift_right))
    step(nc.vector.tensor_copy(tf[:, 1:B + 1], ti[:, 0:B]))
    step(nc.vector.memset(tf[:, 0:1], 0.0))
    step(nc.vector.memset(buf["zero"][:, 0:B], 0.0))
    step(nc.vector.tensor_tensor_scan(start[:, 0:B], tf[:, 0:B], buf["zero"][:, 0:B], 0.0,
                                      ALU.add, ALU.add))
    step(nc.vector.tensor_scalar(base[:, 0:B], start[0:P, 0:B], float(SLOT), -1.0, ALU.mult, ALU.add))
    step(nc.vector.tensor_tensor(base[:, 0:B], base[:, 0:B], before[:, 0:B], ALU.subtract))
    step(nc.vector.tensor_tensor(base[:, 0:B], base[:, 0:B], buf["ps_pre"], ALU.add))
    step(nc.vector.tensor_tensor(cum, cum, base[:, 0:B].unsqueeze(2).to_broadcast([P, B, J]), ALU.add))
    step(nc.vector.tensor_tensor(cum, cum, oh, ALU.mult))
    step(nc.vector.tensor_reduce(slots, cum.rearrange("p b j -> p j b"), AXIS.X, ALU.add))


def slot_buffers(pg, ctx, tag, B):
    sb = lambda n, s, d=fp32: pg.sb(f"{tag}_{n}", s, d, ctx)
    return {"before": sb("before", [P, B]), "total": sb("total", [P, B]),
            "ti": sb("ti", [128, B], int32), "tf": sb("tf", [128, B + 1]), "zero": sb("zero", [128, B]),
            "start": sb("start", [128, B]), "base": sb("base", [P, B]),
            "ps_all": pg.ps[:, 7, 0:B], "ps_pre": pg.ps[0:P, 7, 64:64 + B]}


def bucket_totals(nc, pe, pg, buf, B, tot_ready, tot_done):
    pe.wait_ge(tot_ready, 1)
    nc.tensor.matmul(buf["ps_all"], pg.ones[0:P, :], buf["total"][:, 0:B], start=True, stop=True)
    nc.tensor.matmul(buf["ps_pre"], pg.tri[0:P, 0:P], buf["total"][:, 0:B],
                     start=True, stop=True).then_inc(tot_done, 1)


def owner_table(nc, step, row_t, start, B, count, acc):
    step(nc.vector.memset(acc, 0.0))
    for b in range(1, B):
        step(nc.vector.scalar_tensor_tensor(acc, row_t[0:1, 0:count], start[0:1, b:b + 1], acc,
                                            ALU.is_ge, ALU.add))


class Norm:

    def __init__(self, pg, ctx, tag, use, weight=None, dram=None, features=None, logits=None):
        self.pg, self.use, self.weight, self.dram = pg, use, weight, dram
        self.features, self.logits = features, logits
        sb = lambda n, s, d=fp32: pg.sb(f"{tag}_{n}", s, d, ctx)
        sem = lambda n: pg.sem(f"{tag}_{n}", ctx)
        self.st = sb("stats", [P, NT, 6])
        self.mean, self.var = sb("mean", [P, NT]), sb("var", [P, NT])
        self.dif, self.rstd = sb("dif", [P, NT]), sb("rstd", [P, NT])
        self.ring = sb("xn_ring", [P, U, D])
        self.xt = sb("xn_t", [128, U, KD, P])
        self.rows = sb("rows", [P, U, D]) if use == "rows" else None
        self.s_stat, self.s_var, self.s_std = sem("stat"), sem("var"), sem("std")
        self.s_xn, self.s_ring, self.s_tr, self.s_xt = sem("xn"), sem("ring"), sem("tr"), sem("xt")
        self.s_mm, self.s_out = sem("mm"), sem("out")
        self.s_st = [sem(f"stored{s}") for s in range(U)]
        self.s_ch = sem("chain")

    def vector(self, dve, x_ready=None):
        nc, pg = self.pg.nc, self.pg
        step = Chain(dve, self.s_ch)
        if x_ready is not None:
            dve.wait_ge(*x_ready)
        dve.sem_inc(self.s_xt, U)
        if self.use == "router":
            dve.sem_inc(self.s_out, U)
        with dve.Fori(0, NT) as j:
            nc.vector.bn_stats(self.st[:, bass.ds(j, 1), :], pg.X[:, bass.ds(j, 1), :]).then_inc(self.s_stat, 1)
        dve.wait_ge(self.s_stat, NT)
        st = self.st
        step(nc.vector.tensor_tensor(self.dif[:], st[:, :, 1], st[:, :, 4], ALU.subtract))
        step(nc.vector.tensor_tensor(self.mean[:], st[:, :, 1], st[:, :, 4], ALU.add))
        step(nc.vector.tensor_scalar(self.mean[:], self.mean[:], 0.5, None, ALU.mult))
        step(nc.vector.tensor_tensor(self.var[:], st[:, :, 2], st[:, :, 5], ALU.add))
        step(nc.vector.tensor_scalar(self.var[:], self.var[:], 1.0 / D, LN_EPS, ALU.mult, ALU.add))
        step(nc.vector.tensor_tensor(self.dif[:], self.dif[:], self.dif[:], ALU.mult))
        nc.vector.scalar_tensor_tensor(self.var[:], self.dif[:], 0.25, self.var[:],
                                       ALU.mult, ALU.add).then_inc(self.s_var, 1)
        dve.wait_ge(self.s_std, 1)
        step(nc.vector.reciprocal(self.rstd[:], self.rstd[:]))
        with dve.Fori(0, NT // U) as i:
            for s in range(U):
                j = i * U + s
                nc.vector.tensor_scalar(pg.XN[:, bass.ds(j, 1), :], pg.X[:, bass.ds(j, 1), :],
                                        self.mean[:, bass.ds(j, 1)], self.rstd[:, bass.ds(j, 1)],
                                        ALU.subtract, ALU.mult).then_inc(self.s_xn, 1)
            for s in range(U):
                j = i * U + s
                dve.wait_ge(self.s_tr, U + 1 + j)
                if self.use != "features":
                    dve.wait_ge(self.s_mm, j + 1)
                out = (self.features[:, :, bass.ds(j * P, P)] if self.use == "features"
                       else self.xt[:, s, :, :])
                nc.vector.tensor_copy(out, self.t_psum(s)).then_inc(self.s_xt, 1)
            if self.use == "router":
                for s in range(U):
                    j = i * U + s
                    dve.wait_ge(self.s_mm, U + 1 + j)
                    nc.vector.tensor_copy(self.logits[:, bass.ds(j, 1), :],
                                          pg.ps[0:P, s:s + 1, 256:256 + NX]).then_inc(self.s_out, 1)

    def t_psum(self, s):
        return self.pg.ps[:, s, 0:256].rearrange("p (k q) -> p k q", k=KD)[:, :, 0:P]

    def scalar(self, act):
        nc, pg = self.pg.nc, self.pg
        if self.use == "rows":
            act.sem_inc(self.s_out, U)
            for s in range(U):
                act.sem_inc(self.s_st[s], 16)
        act.wait_ge(self.s_var, 1)
        nc.scalar.activation(self.rstd[:], self.var[:], ACT.Sqrt).then_inc(self.s_std, 1)
        with act.Fori(0, NT // U) as i:
            for s in range(U):
                j = i * U + s
                act.wait_ge(self.s_xn, j + 1)
                act.wait_ge(self.s_tr, i * U + U)
                nc.scalar.copy(self.ring[:, s:s + 1, :], pg.XN[:, bass.ds(j, 1), :]).then_inc(self.s_ring, 1)
            if self.use == "rows":
                for s in range(U):
                    j = i * U + s
                    act.wait_ge(self.s_mm, U + 1 + j)
                    act.wait_ge(self.s_st[s], i * 16 + 16)
                    nc.scalar.copy(self.rows[:, s, :], pg.ps[0:P, s, 256:512]).then_inc(self.s_out, 1)
                for s in range(U):
                    j = i * U + s
                    act.wait_ge(self.s_out, U + 1 + j)
                    act.dma_start(self.dram[bass.ds(j * P, P), :], self.rows[:, s, :]).then_inc(self.s_st[s], 16)
        if self.use == "rows":
            for s in range(U):
                act.wait_ge(self.s_st[s], 16 * (NT // U) + 16)

    def tensor(self, pe, w_ready=None):
        nc, pg = self.pg.nc, self.pg
        if w_ready is not None:
            pe.wait_ge(*w_ready)
        if self.use != "features":
            pe.sem_inc(self.s_mm, U)
        pe.sem_inc(self.s_tr, U)

        def transposes(i, s):
            j = i * U + s
            pe.wait_ge(self.s_ring, j + 1)
            pe.wait_ge(self.s_xt, i * U + U)
            if self.use != "features":
                pe.wait_ge(self.s_out, i * U + U)
            for k in range(KD):
                last = nc.tensor.transpose(pg.ps[:, s, k * 128:k * 128 + P],
                                           self.ring[:, s, k * 128:(k + 1) * 128], pg.ident[0:P, 0:P])
            last.then_inc(self.s_tr, 1)

        def product(i, s):
            pe.wait_ge(self.s_xt, U + 1 + i * U + s)
            width = NX if self.use == "router" else D
            for k in range(KD):
                last = nc.tensor.matmul(pg.ps[0:P, s, 256:256 + width], self.xt[:, s, k, :],
                                        self.weight[:, k, :], start=(k == 0), stop=(k == KD - 1))
            last.then_inc(self.s_mm, 1)

        with pe.Fori(0, NT // U) as i:
            for s in range(U):
                transposes(i, s)
            if self.use != "features":
                for s in range(U):
                    product(i, s)


def stage_prepare(pg, x, src, dst, edge_weight, w_l0, bias_l0):
    nc = pg.nc
    with ExitStack() as ctx:
        sb = lambda n, s, d=fp32: pg.sb(n, s, d, ctx)
        sem = lambda n: pg.sem(n, ctx)
        src_i, dst_i = sb("src_i", [P, EJ], int32), sb("dst_i", [P, EJ], int32)
        src_f, blk = sb("src_f", [P, EJ]), sb("blk", [P, EJ])
        pay = sb("pay", [P, EJ, 4])
        slot_f, row_f = sb("slot_f", [P, EJ]), sb("row_f", [P, EJ])
        slot_i, low_i = sb("slot_i", [P, EJ], int32), sb("low_i", [P, EJ], int32)
        oh, cum = sb("oh", [P, NT, EJ]), sb("cum", [P, NT, EJ])
        iota_b = sb("iota_b", [P, NT])
        W = sb("w_l0_gnn", [128, KD, D])
        bias = sb("bias_l0", [P, D])
        zero = sb("zero", [128, EDGE_PAD * 4])
        pay_st, idx_st = sb("pay_st", [P, 2, 8, 4]), sb("idx_st", [P, 2, 8], int32)
        owner = sb("owner", [1, EDGE_PAD])
        buf = slot_buffers(pg, ctx, "edges", NT)
        ld_edge, ld_x, ld_w, s_ch, s_const, tri_ok = (sem(n) for n in (
            "ld_edge", "ld_x", "ld_w", "sort_chain", "consts", "tri_ok"))
        tot_ready, tot_done, rows_ok, zeroed, cleared = (sem(n) for n in (
            "tot_ready", "tot_done", "slots_ok", "zeroed", "cleared"))
        s_tick, s_back, s_pool = (sem(n) for n in ("tick", "payload_back", "pool_chain"))
        staged = [sem(f"staged{h}") for h in range(2)]
        wiped = pg.arrivals(16, 16)
        scat = pg.arrivals(16, 16 * (EJ // 16))
        norm = Norm(pg, ctx, "ln0", "rows", weight=W, dram=pg.H)
        CLEARS = 2

        with pg.block() as block:
            @block.sync
            def _(sp):
                sp.dma_start(src_i[:], src.rearrange("(p j) -> p j", p=P)).then_inc(ld_edge, 16)
                sp.dma_start(dst_i[:], dst.rearrange("(p j) -> p j", p=P)).then_inc(ld_edge, 16)
                sp.dma_start(slot_f[:], edge_weight.rearrange("(p j) -> p j", p=P)).then_inc(ld_edge, 16)
                sp.dma_start(pg.X[:], x.rearrange("(j p) d -> p j d", p=P)).then_inc(ld_x, 16)
                load_weight_chunks(sp, W[:], w_l0, ld_w)
                sp.dma_start(bias[:], bias_l0.partition_broadcast(P)).then_inc(ld_w, 16)
                sp.wait_ge(zeroed, 1)
                for rows, n in ((pg.XS0, MOE_TILES), (pg.XS1, SHARED_TILES + MOE_TILES)):
                    sp.dma_start(rows.rearrange("(t p) d -> p t d", p=128),
                                 zero[:, 0:D].unsqueeze(1).to_broadcast([128, n, D])).then_inc(cleared, 16)
                sp.wait_ge(rows_ok, 1)
                with sp.Fori(0, EJ // 16) as i:
                    for h in range(2):
                        for k in range(8):
                            scat[8 * h + k].wait(sp, 16 * i)
                        cols = bass.ds(i * 16 + 8 * h, 8)
                        sp.dma_start(pay_st[:, h, :, :], pay[:, cols, :]).then_inc(staged[h], 16)
                        sp.dma_start(idx_st[:, h, :], slot_i[:, cols]).then_inc(staged[h], 16)
                for k in range(16):
                    scat[k].wait(sp, 16 * (EJ // 16))
                sp.dma_start(pg.slots[:].rearrange("p c f -> p (c f)"),
                             pg.pay_dram.rearrange("(p c) f -> p (c f)", p=128)).then_inc(s_back, 16)
                sp.wait_ge(s_back, 16)

            @block.gpsimd
            def _(pool):
                pg.clear_used(pool)
                step = Chain(pool, s_pool)
                g = nc.gpsimd
                step(g.memset(zero[:], 0.0))
                pool.sem_inc(zeroed, 1)
                f = {"allow_small_or_imprecise_dtypes": True}
                step(g.iota(pg.col[:], [[1, 128]], base=0, channel_multiplier=0, **f))
                step(g.iota(pg.tiles[:], [[1, EDGE_PAD]], base=0, channel_multiplier=0, **f))
                step(g.iota(pg.part[:], [[1, 1]], base=0, channel_multiplier=1, **f))
                step(g.iota(iota_b[:], [[1, NT]], base=0, channel_multiplier=0, **f))
                step(g.iota(pg.prio[:], [[-1, NX]], base=NX, channel_multiplier=0, **f))
                step(g.memset(pg.ones[:], 1.0))
                pool.sem_inc(s_const, 1)
                piece = 128 // 16
                for k in range(16):
                    rows = slice(k * piece * EDGE_PAD, (k + 1) * piece * EDGE_PAD)
                    pool.dma_start(pg.pay_dram[rows, :].rearrange("(p c) f -> p (c f)", p=piece),
                                   zero[k * piece:(k + 1) * piece, :]).then_inc(wiped[k].sem, 16)
                for k in range(16):
                    wiped[k].wait(pool, 16)
                pool.wait_ge(cleared, 16 * CLEARS)
                with pool.Fori(0, EJ // 16) as i:
                    for h in range(2):
                        pool.wait_ge(staged[h], 32 * i + 32)
                        pool.sem_inc(s_tick, 1)
                        for k in range(8):
                            g.indirect_dma_start(
                                pg.pay_dram, bass.IndirectOffsetOnAxis(ap=idx_st[:, h, k:k + 1], axis=0),
                                pay_st[:, h, k, :], None).then_inc(scat[8 * h + k].sem, 16)

            @block.vector
            def _(dve):
                step = Chain(dve, s_ch)
                v = nc.vector
                dve.wait_ge(s_const, 1)
                step(v.tensor_scalar(pg.ident[:], pg.col[:], pg.part[:, 0:1], None, ALU.is_equal))
                v.tensor_scalar(pg.tri[:], pg.col[:], pg.part[:, 0:1], None, ALU.is_gt).then_inc(tri_ok, 1)
                dve.wait_ge(ld_edge, 48)
                step(v.tensor_copy(src_f[:], src_i[:]))
                step(v.tensor_copy(pay[:, :, 2], dst_i[:]))
                step(v.tensor_copy(pay[:, :, 1], slot_f[:]))
                step(v.memset(pay[:, :, 3], 0.0))
                step(v.tensor_scalar(blk[:], src_f[:], float(P), None, ALU.is_ge))
                for b in range(2, NT):
                    step(v.scalar_tensor_tensor(blk[:], src_f[:], float(P * b), blk[:], ALU.is_ge, ALU.add))
                step(v.scalar_tensor_tensor(pay[:, :, 0], blk[:], -float(P), src_f[:], ALU.mult, ALU.add))
                step(v.tensor_tensor(oh[:], blk[:].unsqueeze(1).to_broadcast([P, NT, EJ]),
                                     iota_b[:].unsqueeze(2).to_broadcast([P, NT, EJ]), ALU.is_equal))
                bucket_slots(nc, step, dve, oh[:], cum[:], EJ, NT, buf, tot_ready, tot_done, slot_f[:])
                step(v.tensor_copy(slot_i[:], slot_f[:]))
                step(v.tensor_scalar(low_i[:], slot_i[:], SLOT - 1, None, ALU.bitwise_and))
                step(v.tensor_scalar(slot_i[:], slot_i[:], 7, None, ALU.arith_shift_right))
                step(v.tensor_copy(slot_f[:], slot_i[:]))
                step(v.tensor_copy(row_f[:], low_i[:]))
                step(v.scalar_tensor_tensor(row_f[:], row_f[:], float(EDGE_PAD), slot_f[:], ALU.mult, ALU.add))
                step(v.tensor_copy(slot_i[:], row_f[:]))
                dve.sem_inc(rows_ok, 1)
                owner_table(nc, step, pg.tiles, buf["start"], NT, EDGE_PAD, owner[:])
                step(v.tensor_scalar(pg.owner_n[:], owner[:], float(P), None, ALU.mult))
                step(v.tensor_copy(pg.owner_t[:], owner[:]))
                norm.vector(dve, (ld_x, 16))
                dve.wait_ge(ld_w, 32)
                step(v.tensor_tensor(pg.X[:], pg.X[:], bias[:].unsqueeze(1).to_broadcast([P, NT, D]), ALU.add))

            @block.tensor
            def _(pe):
                pe.wait_ge(s_const, 1)
                pe.wait_ge(tri_ok, 1)
                bucket_totals(nc, pe, pg, buf, NT, tot_ready, tot_done)
                norm.tensor(pe, (ld_w, 32))

            @block.scalar
            def _(act):
                norm.scalar(act)


class Aggregate:

    def __init__(self, pg, ctx, tag, by, acc):
        self.pg, self.by, self.acc = pg, by, acc
        sb = lambda n, s, d=fp32: pg.sb(f"{tag}_{n}", s, d, ctx)
        sem = lambda n: pg.sem(f"{tag}_{n}", ctx)
        self.G = sb("gathered", [128, ROUND, D])
        self.S = sb("onehot", [128, ROUND, P])
        self.key = sb("key", [128, ROUND, 2])
        self.idx = sb("idx", [128, ROUND], int32)
        self.s_got = pg.arrivals(ROUND, 16 * (EDGE_PAD // ROUND))
        self.s_key, self.s_hot, self.s_mm, self.s_acc, self.s_tick = (
            sem(n) for n in ("key", "hot", "mm", "acc", "tick"))

    def scalar(self, act):
        nc = self.pg.nc
        with act.Fori(0, EDGE_PAD // ROUND) as i:
            for h in range(2):
                for k in range(8 * h, 8 * h + 8):
                    self.s_got[k].wait(act, 16 * i)
                act.wait_ge(self.s_hot, ROUND * i + 8 * (h + 1))
                cols = bass.ds(i * ROUND + 8 * h, 8)
                half = slice(8 * h, 8 * h + 8)
                nc.scalar.copy(self.idx[:, half], self.pg.slots[:, cols, 2])
                nc.scalar.copy(self.key[:, half, :], self.pg.slots[:, cols, 0:2]).then_inc(self.s_key, 1)

    def gpsimd(self, pool):
        nc = self.pg.nc
        self.pg.clear_used(pool)
        with pool.Fori(0, EDGE_PAD // ROUND) as i:
            for h in range(2):
                pool.wait_ge(self.s_key, 2 * i + h + 1)
                pool.wait_ge(self.s_mm, ROUND * i + 8 * (h + 1))
                pool.sem_inc(self.s_tick, 1)
                for k in range(8 * h, 8 * h + 8):
                    nc.gpsimd.indirect_dma_start(
                        self.G[:, k, :], None, self.pg.H,
                        bass.IndirectOffsetOnAxis(ap=self.idx[:, k:k + 1], axis=0)).then_inc(self.s_got[k].sem, 16)

    def target(self, k):
        b = k % BANKS
        if self.by == "node":
            return self.pg.ps[0:P, b, 0:D]
        return self.pg.ps[:, b, 0:KD * P].rearrange("p (k q) -> p k q", k=KD)

    def tensor(self, pe):
        nc = self.pg.nc
        pe.sem_inc(self.s_mm, ROUND)
        with pe.Fori(0, EDGE_PAD // ROUND) as i:
            for k in range(ROUND):
                self.s_got[k].wait(pe, 16 * i + 16)
                pe.wait_ge(self.s_hot, ROUND * i + ROUND + k + 1)
                pe.wait_ge(self.s_acc, ROUND * i + k + 1)
                out = self.target(k)
                if self.by == "node":
                    last = nc.tensor.matmul(out, self.S[:, k, :], self.G[:, k, :], start=True, stop=True)
                else:
                    for c in range(KD):
                        last = nc.tensor.matmul(out[:, c, :], self.G[:, k, c * 128:(c + 1) * 128],
                                                self.S[:, k, :], start=True, stop=True)
                last.then_inc(self.s_mm, 1)

    def onehot(self, dve, i, k):
        if k % 8 == 0:
            dve.wait_ge(self.s_key, 2 * i + k // 8 + 1)
        dve.wait_ge(self.s_mm, ROUND * i + k + 1)
        self.pg.nc.vector.tensor_scalar(self.S[:, k, :], self.pg.col[:, 0:P], self.key[:, k, 0:1],
                                        self.key[:, k, 1:2], ALU.is_equal, ALU.mult).then_inc(self.s_hot, 1)

    def owners(self, i, h):
        table = self.pg.owner_t if self.by == "node" else self.pg.owner_n
        _, own = self.pg.nc.values_load_multi_w_load_instructions(
            table[0:1, bass.ds(ROUND * i + 8 * h, 8)], engines=(mybir.EngineType.DVE,),
            min_val=0, max_val=NT - 1 if self.by == "node" else N - P)
        return own

    def add(self, dve, i, k, own):
        nc, t = self.pg.nc, ROUND * i + k
        dve.wait_ge(self.s_mm, ROUND + t + 1)
        dve.wait_ge(self.s_acc, BANKS + t)
        if self.by == "node":
            a, p = self.acc[:, bass.ds(own, 1), :], self.target(k).unsqueeze(1)
        else:
            a, p = self.acc[:, :, bass.ds(own, P)], self.target(k)
        nc.vector.tensor_tensor(a, a, p, ALU.add).then_inc(self.s_acc, 1)

    def vector(self, dve):
        dve.sem_inc(self.s_hot, ROUND)
        dve.sem_inc(self.s_acc, BANKS)
        for k in range(8):
            self.onehot(dve, 0, k)
        last = EDGE_PAD // ROUND - 1
        with dve.Fori(0, last) as i:
            own = self.owners(i, 0)
            for k in range(8):
                self.add(dve, i, k, own[k])
                self.onehot(dve, i, k + 8)
            own = self.owners(i, 1)
            for k in range(8):
                self.add(dve, i, k + 8, own[k])
                self.onehot(dve, i + 1, k)
        own = self.owners(last, 0)
        for k in range(8):
            self.add(dve, last, k, own[k])
            self.onehot(dve, last, k + 8)
        own = self.owners(last, 1)
        for k in range(8):
            self.add(dve, last, k + 8, own[k])


def stage_aggregate_nodes(pg):
    nc = pg.nc
    with ExitStack() as ctx:
        agg = Aggregate(pg, ctx, "agg0", "node", pg.X)
        with pg.block() as block:
            block.scalar(agg.scalar)
            block.gpsimd(agg.gpsimd)
            block.tensor(agg.tensor)
            block.vector(agg.vector)


def rolled(eng, first, end, unroll, body):
    n = (end - first) // unroll
    if n > 1:
        with eng.Fori(0, n) as i:
            for u in range(unroll):
                body(i * unroll + (first + u), (first + u) % unroll)
    else:
        n = 0
    for t in range(first + n * unroll, end):
        body(t, t % unroll)


class Experts:

    def __init__(self, pg, ctx, tag, F, shared, XS, YS):
        self.pg, self.tag, self.F, self.FK, self.shared, self.XS, self.YS = pg, tag, F, F // 128, shared, XS, YS
        self.T = shared + MOE_TILES
        self.NE = NX + (1 if shared else 0)
        sb = lambda n, s, d=fp32: pg.sb(f"{tag}_{n}", s, d, ctx)
        self.W1 = sb("w1", [128, self.NE, KD, F])
        self.W2 = sb("w2", [128, self.NE, self.FK, D])
        self.b1 = sb("b1", [128, self.NE, self.FK])
        self.b2 = sb("b2", [128, self.NE, D])
        self.wr = sb("wr", [128, KD, NX])
        self.slot_i = sb("slot_i", [P, TOP * NT], int32)
        self.gate = sb("gate", [P, TOP, NT])
        self.owner = sb("owner", [1, self.T], int32)
        self.s_w = pg.sem(f"{tag}_weights")
        self.loads = 16 * (KD + 2 + 2 * NX + (4 if shared else 0))

    def load(self, eng, dst, src):
        with self.pg.nc.allow_non_contiguous_dma(reason="a few vectors, one value a partition"):
            eng.dma_start(dst, src).then_inc(self.s_w, 16)

    def load_weights(self, eng, wr, w1, b1, w2, b2, shared=None):
        for k in range(KD):
            self.load(eng, self.wr[:, k, :], wr(k))
        self.load(eng, self.b1[:, 0:NX, :], b1.rearrange("e (k p) -> p e k", p=128))
        self.load(eng, self.b2[:, 0:NX, :], b2.partition_broadcast(128))
        for e in range(NX):
            self.load(eng, self.W1[:, e, :, :], w1[e].rearrange("(k p) f -> p k f", p=128))
            self.load(eng, self.W2[:, e, :, :], w2[e].rearrange("(k p) f -> p k f", p=128))
        if shared:
            v1, c1, v2, c2 = shared
            self.load(eng, self.W1[:, NX, :, :], v1.rearrange("(k p) f -> p k f", p=128))
            self.load(eng, self.W2[:, NX, :, :], v2.rearrange("(k p) f -> p k f", p=128))
            self.load(eng, self.b1[:, NX, :], c1.rearrange("(k p) -> p k", p=128))
            self.load(eng, self.b2[:, NX, :], c2.partition_broadcast(128))


def stage_route(pg, ex, keep_x=None, load=None):
    nc = pg.nc
    B, J = NX, TOP * NT
    with ExitStack() as ctx:
        sb = lambda n, s, d=fp32: pg.sb(f"{ex.tag}_{n}", s, d, ctx)
        sem = lambda n: pg.sem(f"{ex.tag}_{n}", ctx)
        logit, prob = sb("logit", [P, NT, NX]), sb("prob", [P, NT, NX])
        cand = sb("cand", [P, NT, NX])
        top, best = sb("top", [P, TOP, NT]), sb("best", [P, NT])
        oh, cum = sb("oh", [P, B, J]), sb("cum", [P, B, J])
        slot_f, own = sb("slot_f", [P, J]), sb("own", [1, ex.T])
        buf = slot_buffers(pg, ctx, ex.tag, B)
        s_ch, s_log, s_exp, tot_ready, tot_done, s_kept = (
            sem(n) for n in ("route_chain", "logits", "exp", "tot_ready", "tot_done", "kept"))
        norm = Norm(pg, ctx, ex.tag, "router", weight=ex.wr, logits=logit)
        with pg.block() as block:
            @block.sync
            def _(sp):
                if keep_x is not None:
                    sp.dma_start(keep_x.rearrange("(j p) d -> p j d", p=P), pg.X[:]).then_inc(s_kept, 16)
                if load:
                    load(sp)
                if keep_x is not None:
                    sp.wait_ge(s_kept, 16)

            @block.gpsimd
            def _(pool):
                pg.clear_used(pool)

            @block.tensor
            def _(pe):
                norm.tensor(pe, (ex.s_w, ex.loads))
                bucket_totals(nc, pe, pg, buf, B, tot_ready, tot_done)

            @block.scalar
            def _(act):
                norm.scalar(act)
                act.wait_ge(s_log, 1)
                nc.scalar.activation(prob[:], logit[:], ACT.Exp).then_inc(s_exp, 1)

            @block.vector
            def _(dve):
                v = nc.vector
                step = Chain(dve, s_ch)
                wide = lambda a: a.unsqueeze(2).to_broadcast([P, NT, NX])
                prio = pg.prio[:].unsqueeze(1).to_broadcast([P, NT, NX])
                norm.vector(dve, (s_kept, 16) if keep_x is not None else None)
                dve.wait_ge(norm.s_out, NT + U)
                step(v.tensor_reduce(best[:], logit[:], AXIS.X, ALU.max))
                v.tensor_tensor(logit[:], logit[:], wide(best[:]), ALU.subtract).then_inc(s_log, 1)
                dve.wait_ge(s_exp, 1)
                step(v.tensor_reduce(best[:], prob[:], AXIS.X, ALU.add))
                step(v.reciprocal(best[:], best[:]))
                step(v.tensor_tensor(prob[:], prob[:], wide(best[:]), ALU.mult))
                for c in range(TOP):
                    picked = oh[:, :, c * NT:(c + 1) * NT].rearrange("p e j -> p j e")
                    step(v.tensor_reduce(top[:, c, :], prob[:], AXIS.X, ALU.max))
                    step(v.tensor_tensor(cand[:], prob[:], wide(top[:, c, :]), ALU.is_equal))
                    step(v.tensor_tensor(cand[:], cand[:], prio, ALU.mult))
                    step(v.tensor_reduce(best[:], cand[:], AXIS.X, ALU.max))
                    step(v.tensor_tensor(picked, cand[:], wide(best[:]), ALU.is_equal))
                    if c + 1 < TOP:
                        step(v.scalar_tensor_tensor(prob[:], picked, -2.0, prob[:], ALU.mult, ALU.add))
                step(v.tensor_tensor(best[:], top[:, 0, :], top[:, 1, :], ALU.add))
                step(v.tensor_scalar(best[:], best[:], 1e-12, None, ALU.max))
                step(v.reciprocal(best[:], best[:]))
                for c in range(TOP):
                    step(v.tensor_tensor(ex.gate[:, c, :], top[:, c, :], best[:], ALU.mult))
                bucket_slots(nc, step, dve, oh[:], cum[:], J, B, buf, tot_ready, tot_done, slot_f[:])
                if ex.shared:
                    step(v.tensor_scalar(slot_f[:], slot_f[:], float(ex.shared * SLOT), None, ALU.add))
                    step(v.memset(own[:, 0:ex.shared], float(NX)))
                step(v.tensor_copy(ex.slot_i[:], slot_f[:]))
                owner_table(nc, step, pg.tiles, buf["start"], B, MOE_TILES, own[:, ex.shared:])
                step(v.tensor_copy(ex.owner[:], own[:]))


def stage_experts(pg, ex, residual=None):
    nc = pg.nc
    F, FK, T = ex.F, ex.FK, ex.T
    R = 2
    NB = -(-F // 512)
    with ExitStack() as ctx:
        sb = lambda n, s, d=fp32: pg.sb(f"{ex.tag}_{n}", s, d, ctx)
        sem = lambda n: pg.sem(f"{ex.tag}_{n}", ctx)
        xs, xt = sb("xs", [128, R, D]), sb("xt", [128, R, KD, 128])
        hid, ht = sb("hid", [128, F]), sb("ht", [128, R, FK, 128])
        y = sb("y", [128, R, D])
        s_sh, s_ch, s_tick = sem("shared_rows"), sem("chain2"), sem("tick")
        s_sc, *s_st = pg.arrivals(1 + R, [16 * TOP * NT] + [16 * ((T - r + R - 1) // R) for r in range(R)])
        s_ld = [sem(f"loaded{r}") for r in range(R)]
        s_a, s_xt, s_b, s_h, s_c, s_g, s_d, s_y = (sem(n) for n in (
            "x_transposed", "xt_ok", "fc1", "hid_ok", "h_transposed", "gelu", "fc2", "y_ok"))
        ps_x, ps_h = pg.ps[:, 0, 0:D], pg.ps[:, 1:1 + NB, :]
        ps_t, ps_y = pg.ps[:, 3:3 + NB, :], pg.ps[:, 5, 0:D]
        tile_rows = lambda ap, t: ap[bass.ds(t * SLOT, SLOT), :]

        def times16(t, r):
            return (t - r) * (16 // R) + 16

        def stored16(t, r):
            return (t - r) * (16 // R)

        with pg.block() as block:
            @block.gpsimd
            def _(pool):
                pg.clear_used(pool)
                for c in range(TOP):
                    for j in range(NT):
                        nc.gpsimd.indirect_dma_start(
                            ex.XS, bass.IndirectOffsetOnAxis(ap=ex.slot_i[:, c * NT + j:c * NT + j + 1], axis=0),
                            pg.XN[:, j, :], None).then_inc(s_sc.sem, 16)

                def store(t, r):
                    pool.wait_ge(s_y, t + 2)
                    pool.sem_inc(s_tick, 1)
                    pool.dma_start(tile_rows(ex.YS, t), y[:, r, :]).then_inc(s_st[r].sem, 16)

                rolled(pool, 0, T, R, store)
                for r in range(R):
                    s_st[r].wait(pool, 16 * ((T - r + R - 1) // R))

            @block.sync
            def _(sp):
                def load(t, r):
                    sp.wait_ge(s_a, t + 1)
                    sp.dma_start(xs[:, r, :], tile_rows(ex.XS, t)).then_inc(s_ld[r], 16)

                if ex.shared:
                    sp.dma_start(ex.XS[0:N, :].rearrange("(j p) d -> p j d", p=P), pg.XN[:]).then_inc(s_sh, 16)
                    sp.wait_ge(s_sh, 16)
                    rolled(sp, 0, ex.shared, R, load)
                s_sc.wait(sp, 16 * TOP * NT)
                rolled(sp, ex.shared, T, R, load)

            @block.tensor
            def _(pe):
                pe.sem_inc(s_a, R)
                pe.wait_ge(ex.s_w, ex.loads)

                def expert(t):
                    return nc.tensor.value_load(ex.owner[0:1, bass.ds(t, 1)], min_val=0, max_val=ex.NE - 1)

                def x_transpose(t, r):
                    pe.wait_ge(s_ld[r], times16(t, r))
                    pe.wait_ge(s_xt, t + 1)
                    for k in range(KD):
                        last = nc.tensor.transpose(ps_x[:, k * 128:(k + 1) * 128],
                                                   xs[:, r, k * 128:(k + 1) * 128], pg.ident[:])
                    last.then_inc(s_a, 1)

                def fc1(t, r):
                    e = expert(t)
                    pe.wait_ge(s_xt, t + 2)
                    pe.wait_ge(s_h, t + 1)
                    for n in range(NB):
                        w = min(512, F)
                        for k in range(KD):
                            last = nc.tensor.matmul(ps_h[:, n, 0:w], xt[:, r, k, :],
                                                    ex.W1[:, bass.ds(e, 1), k, n * 512:n * 512 + w]
                                                    .rearrange("p o w -> p (o w)"),
                                                    start=(k == 0), stop=(k == KD - 1))
                    last.then_inc(s_b, 1)

                def h_transpose(t, r):
                    pe.wait_ge(s_h, t + 2)
                    pe.wait_ge(s_g, t + 1)
                    for k in range(FK):
                        last = nc.tensor.transpose(ps_t[:, k // 4, (k % 4) * 128:(k % 4) * 128 + 128],
                                                   hid[:, k * 128:(k + 1) * 128], pg.ident[:])
                    last.then_inc(s_c, 1)

                def fc2(t, r):
                    e = expert(t)
                    pe.wait_ge(s_g, t + 2)
                    pe.wait_ge(s_y, t + 1)
                    for k in range(FK):
                        last = nc.tensor.matmul(ps_y, ht[:, r, k, :], ex.W2[:, bass.ds(e, 1), k, :]
                                                .rearrange("p o w -> p (o w)"),
                                                start=(k == 0), stop=(k == FK - 1))
                    last.then_inc(s_d, 1)

                def body(t, r):
                    fc1(t + 1, (r + 1) % R)
                    h_transpose(t, r)
                    x_transpose(t + 2, r)
                    fc2(t - 1, (r + 1) % R)

                x_transpose(0, 0)
                fc1(0, 0)
                x_transpose(1, 1)
                fc1(1, 1)
                h_transpose(0, 0)
                x_transpose(2, 0)
                rolled(pe, 1, T - 2, R, body)
                t = T - 2
                fc1(t + 1, (t + 1) % R)
                h_transpose(t, t % R)
                fc2(t - 1, (t - 1) % R)
                h_transpose(t + 1, (t + 1) % R)
                fc2(t, t % R)
                fc2(t + 1, (t + 1) % R)

            @block.scalar
            def _(act):
                act.sem_inc(s_g, 1)

                def gelu(t, r):
                    e = nc.scalar.value_load(ex.owner[0:1, bass.ds(t, 1)], min_val=0, max_val=ex.NE - 1)
                    act.wait_ge(s_c, t + 1)
                    act.wait_ge(s_d, t + 1)
                    for k in range(FK):
                        last = nc.scalar.activation(
                            ht[:, r, k, :], ps_t[:, k // 4, (k % 4) * 128:(k % 4) * 128 + 128], ACT.Gelu,
                            bias=ex.b1[:, bass.ds(e, 1), k])
                    last.then_inc(s_g, 1)

                rolled(act, 0, T, R, gelu)

            @block.vector
            def _(dve):
                v = nc.vector
                if residual is not None:
                    step = Chain(dve, s_ch)
                    step(v.tensor_tensor(residual, residual, pg.XN[:], ALU.add))
                dve.sem_inc(s_xt, 1)
                dve.sem_inc(s_h, 1)
                dve.sem_inc(s_y, 1)
                dve.sem_inc(s_d, R)

                def x_copy(t, r):
                    dve.wait_ge(s_a, t + R + 1)
                    dve.wait_ge(s_b, t + 1)
                    v.tensor_copy(xt[:, r, :, :], ps_x.rearrange("p (k q) -> p k q", k=KD)).then_inc(s_xt, 1)

                def h_copy(t, r):
                    dve.wait_ge(s_b, t + R + 1)
                    dve.wait_ge(s_c, t)
                    for n in range(NB):
                        w = min(512, F)
                        last = v.tensor_copy(hid[:, n * 512:n * 512 + w], ps_h[:, n, 0:w])
                    last.then_inc(s_h, 1)

                def y_copy(t, r):
                    e = v.value_load(ex.owner[0:1, bass.ds(t, 1)], min_val=0, max_val=ex.NE - 1)
                    dve.wait_ge(s_d, t + R + 1)
                    s_st[r].wait(dve, stored16(t, r))
                    v.tensor_tensor(y[:, r, :], ps_y, ex.b2[:, bass.ds(e, 1), :].rearrange("p o d -> p (o d)"),
                                    ALU.add).then_inc(s_y, 1)

                def body(t, r):
                    h_copy(t + 1, (r + 1) % R)
                    x_copy(t + 2, r)
                    y_copy(t - 1, (r + 1) % R)

                dve.sem_inc(s_b, R)
                x_copy(0, 0)
                h_copy(0, 0)
                x_copy(1, 1)
                h_copy(1, 1)
                x_copy(2, 0)
                rolled(dve, 1, T - 2, R, body)
                t = T - 2
                h_copy(t + 1, (t + 1) % R)
                y_copy(t - 1, (t - 1) % R)
                y_copy(t, t % R)
                y_copy(t + 1, (t + 1) % R)



def stage_combine(pg, ex, out=None, x_kept=None):
    nc = pg.nc
    RG = 4
    with ExitStack() as ctx:
        sb = lambda n, s, d=fp32: pg.sb(f"{ex.tag}_{n}", s, d, ctx)
        sem = lambda n: pg.sem(f"{ex.tag}_{n}", ctx)
        g = sb("g", [P, RG, TOP, D])
        xk = sb("xk", [P, RG, TOP, D]) if out is not None else None
        s_g = pg.arrivals(RG, [32 * ((NT - r + RG - 1) // RG) for r in range(RG)])
        s_k = [sem(f"k{r}") for r in range(RG)]
        s_o = [sem(f"o{r}") for r in range(RG)]
        s_sum, s_tick, s_ch = sem("sum"), sem("ctick"), sem("cchain")
        with pg.block() as block:
            @block.gpsimd
            def _(pool):
                pg.clear_used(pool)
                for j in range(NT):
                    r = j % RG
                    if j >= RG:
                        pool.wait_ge(s_sum, j - RG + 1)
                    for c in range(TOP):
                        nc.gpsimd.indirect_dma_start(
                            g[:, r, c, :], None, ex.YS, bass.IndirectOffsetOnAxis(
                                ap=ex.slot_i[:, c * NT + j:c * NT + j + 1], axis=0)).then_inc(s_g[r].sem, 16)

            @block.sync
            def _(sp):
                if out is None:
                    return

                def store(j):
                    sp.wait_ge(s_sum, j + 1)
                    sp.dma_start(out[j * P:(j + 1) * P, :], xk[:, j % RG, 0, :]).then_inc(s_o[j % RG], 16)

                for j in range(NT):
                    r = j % RG
                    if j >= RG:
                        store(j - RG)
                        sp.wait_ge(s_o[r], 16 * (j // RG))
                    rows = slice(j * P, (j + 1) * P)
                    sp.dma_start(xk[:, r, 0, :], x_kept[rows, :]).then_inc(s_k[r], 16)
                    sp.dma_start(xk[:, r, 1, :], ex.YS[rows, :]).then_inc(s_k[r], 16)
                for j in range(NT - RG, NT):
                    store(j)
                for r in range(RG):
                    sp.wait_ge(s_o[r], 16 * ((NT - r + RG - 1) // RG))

            @block.vector
            def _(dve):
                v = nc.vector
                step = Chain(dve, s_ch)
                for j in range(NT):
                    r = j % RG
                    a = pg.X[:, j, :] if out is None else xk[:, r, 0, :]
                    if out is not None:
                        dve.wait_ge(s_k[r], 32 * (j // RG + 1))
                        step(v.tensor_tensor(a, a, xk[:, r, 1, :], ALU.add))
                    s_g[r].wait(dve, 32 * (j // RG + 1))
                    step(v.scalar_tensor_tensor(a, g[:, r, 0, :], ex.gate[:, 0, j:j + 1], a, ALU.mult, ALU.add))
                    v.scalar_tensor_tensor(a, g[:, r, 1, :], ex.gate[:, 1, j:j + 1], a,
                                           ALU.mult, ALU.add).then_inc(s_sum, 1)


class Dense:

    def __init__(self, pg, ctx, tag):
        self.pg = pg
        sb = lambda n, s, d=fp32: pg.sb(f"{tag}_{n}", s, d, ctx)
        sem = lambda n: pg.sem(f"{tag}_{n}", ctx)
        self.st = sb("st", [128, KD, len(CHUNKS), 6])
        self.mv = sb("mv", [128, KD, 2])
        self.std, self.tmp = sb("std", [128, KD]), sb("tmp", [128, KD])
        self.scale, self.shift = sb("scale", [128, 2, KD]), sb("shift", [128, 2, KD])
        self.ring, self.rows = sb("t_ring", [128, U, KD, P]), sb("rows2", [P, U, D])
        self.s_mm, self.s_ev, self.s_bn, self.s_ch, self.s_var, self.s_std, self.s_aff, self.s_relu = (
            sem(n) for n in ("mm", "ev", "bn", "chain", "var", "std", "aff", "relu"))
        self.s_ring, self.s_kept, self.s_tr, self.s_row = (sem(n) for n in ("ringed", "kept", "trd", "row"))
        self.s_st = [sem(f"st{s}") for s in range(U)]
        self.G = KD * len(CHUNKS)

    def product(self, pe, which, weight, src):
        nc, ps = self.pg.nc, self.pg.ps
        for c, (s0, n) in enumerate(CHUNKS):
            if which:
                pe.wait_ge(self.s_relu, KD * (c + 1))
            for fo in range(KD):
                g = which * self.G + c * KD + fo
                if g >= BANKS:
                    pe.wait_ge(self.s_ev, g - BANKS + 1)
                for k in range(KD):
                    last = nc.tensor.matmul(ps[:, g % BANKS, 0:n], weight[:, k, fo * 128:(fo + 1) * 128],
                                            src[:, k, s0:s0 + n], start=(k == 0), stop=(k == KD - 1))
                last.then_inc(self.s_mm, 1)

    def evacuate(self, act, which, dst, bias):
        nc, ps = self.pg.nc, self.pg.ps
        for c, (s0, n) in enumerate(CHUNKS):
            for fo in range(KD):
                g = which * self.G + c * KD + fo
                act.wait_ge(self.s_mm, g + 1)
                nc.scalar.activation(dst[:, fo, s0:s0 + n], ps[:, g % BANKS, 0:n], ACT.Identity,
                                     bias=bias[:, fo:fo + 1]).then_inc(self.s_ev, 1)

    def statistics(self, dve, step, which, src, gamma, beta):
        v = self.pg.nc.vector
        for c, (s0, n) in enumerate(CHUNKS):
            for fo in range(KD):
                g = which * self.G + c * KD + fo
                dve.wait_ge(self.s_ev, g + 1)
                v.bn_stats(self.st[:, fo, c, :], src[:, fo, s0:s0 + n]).then_inc(self.s_bn, 1)
        dve.wait_ge(self.s_bn, (which + 1) * self.G)
        for fo in range(KD):
            step(v.bn_aggr(self.mv[:, fo, :], self.st[:, fo, :, :].rearrange("p c s -> p (c s)")))
        v.tensor_scalar(self.std[:], self.mv[:, :, 1], BN_EPS, None, ALU.add).then_inc(self.s_var, 1)
        dve.wait_ge(self.s_std, which + 1)
        scale, shift = self.scale[:, which, :], self.shift[:, which, :]
        step(v.reciprocal(self.std[:], self.std[:]))
        step(v.tensor_tensor(scale, self.std[:], gamma, ALU.mult))
        step(v.tensor_tensor(self.tmp[:], self.mv[:, :, 0], scale, ALU.mult))
        v.tensor_tensor(shift, beta, self.tmp[:], ALU.subtract).then_inc(self.s_aff, 1)

    def root(self, act, which):
        act.wait_ge(self.s_var, which + 1)
        self.pg.nc.scalar.activation(self.std[:], self.std[:], ACT.Sqrt).then_inc(self.s_std, 1)

    def relu(self, act, which, a):
        act.wait_ge(self.s_aff, which + 1)
        for s0, n in CHUNKS:
            for fo in range(KD):
                self.pg.nc.scalar.activation(
                    a[:, fo, s0:s0 + n], a[:, fo, s0:s0 + n], ACT.Relu,
                    bias=self.shift[:, which, fo:fo + 1],
                    scale=self.scale[:, which, fo:fo + 1]).then_inc(self.s_relu, 1)

    def ring_fill(self, act, src, which):
        nc = self.pg.nc
        if which is not None:
            act.wait_ge(self.s_aff, which + 1)
        with act.Fori(0, NT // U) as i:
            for s in range(U):
                j = i * U + s
                act.wait_ge(self.s_tr, i * U + U)
                act.wait_ge(self.s_kept, i * U + U)
                for k in range(KD):
                    a = src[:, k, bass.ds(j * P, P)]
                    if which is None:
                        last = nc.scalar.copy(self.ring[:, s, k, :], a)
                    else:
                        last = nc.scalar.activation(self.ring[:, s, k, :], a, ACT.Relu,
                                                    bias=self.shift[:, which, k:k + 1],
                                                    scale=self.scale[:, which, k:k + 1])
                last.then_inc(self.s_ring, 1)

    def ring_keep(self, pool, dst):
        pool.sem_inc(self.s_kept, U)
        with pool.Fori(0, NT // U) as i:
            for s in range(U):
                j = i * U + s
                pool.wait_ge(self.s_ring, j + 1)
                self.pg.nc.gpsimd.tensor_copy(dst[:, :, bass.ds(j * P, P)], self.ring[:, s, :, :]).then_inc(self.s_kept, 1)

    def ring_transpose(self, pe):
        nc, ps = self.pg.nc, self.pg.ps
        pe.sem_inc(self.s_tr, U)
        with pe.Fori(0, NT // U) as i:
            for s in range(U):
                j = i * U + s
                pe.wait_ge(self.s_ring, j + 1)
                pe.wait_ge(self.s_row, i * U + U)
                for k in range(KD):
                    last = nc.tensor.transpose(ps[0:P, s, k * 128:(k + 1) * 128], self.ring[:, s, k, :],
                                               self.pg.ident[:])
                last.then_inc(self.s_tr, 1)

    def rows_out(self, dve):
        v, ps = self.pg.nc.vector, self.pg.ps
        dve.sem_inc(self.s_row, U)
        with dve.Fori(0, NT // U) as i:
            for s in range(U):
                j = i * U + s
                dve.wait_ge(self.s_tr, U + 1 + j)
                dve.wait_ge(self.s_st[s], i * 16 + 16)
                v.tensor_copy(self.rows[:, s, :], ps[0:P, s, 0:D]).then_inc(self.s_row, 1)

    def rows_store(self, sp):
        for s in range(U):
            sp.sem_inc(self.s_st[s], 16)
        with sp.Fori(0, NT // U) as i:
            for s in range(U):
                j = i * U + s
                sp.wait_ge(self.s_row, U + 1 + j)
                sp.dma_start(self.pg.H[bass.ds(j * P, P), :], self.rows[:, s, :]).then_inc(self.s_st[s], 16)
        for s in range(U):
            sp.wait_ge(self.s_st[s], 16 * (NT // U) + 16)

    def rows_add(self, dve, X):
        v, ps = self.pg.nc.vector, self.pg.ps
        dve.sem_inc(self.s_row, U)
        with dve.Fori(0, NT // U) as i:
            for s in range(U):
                j = i * U + s
                dve.wait_ge(self.s_tr, U + 1 + j)
                x = X[:, bass.ds(j, 1), :]
                v.tensor_tensor(x, x, ps[0:P, s:s + 1, 0:D], ALU.add).then_inc(self.s_row, 1)


def stage_network(pg, w_in, b_in, w1, b1, g1, be1, w2, b2, g_out, b_out):
    nc = pg.nc
    L = w1.shape[0]
    with ExitStack() as ctx:
        hf, z1, z2 = (pg.sb(n, [128, KD, N], ctx=ctx) for n in ("h_features", "z1", "z2"))
        W = pg.sb("gnn_w", [128, 1 + 2 * L, KD, D], ctx=ctx)
        names = ("b1", "g1", "be1", "b2", "g_out", "b_out")
        par = {n: pg.sb(f"gnn_{n}", [128, L, KD], ctx=ctx) for n in names}
        bi = pg.sb("gnn_b_in", [128, KD], ctx=ctx)
        s_w = pg.sem("gnn_weights")
        loads = 16 * (1 + 2 * L + len(names) + 1)

        with ExitStack() as c:
            norm = Norm(pg, c, "ln2", "features", features=hf)
            d = Dense(pg, c, "in")
            with pg.block() as block:
                @block.sync
                def _(sp):
                    load_weight_chunks(sp, W[:, 0, :, :], w_in, s_w)
                    c.enter_context(nc.allow_non_contiguous_dma(reason="vectors, one value a partition"))
                    sp.dma_start(bi[:], b_in.rearrange("(k p) -> p k", p=128)).then_inc(s_w, 16)
                    for layer in range(L):
                        load_weight_chunks(sp, W[:, 1 + 2 * layer, :, :], w1[layer], s_w)
                        load_weight_chunks(sp, W[:, 2 + 2 * layer, :, :], w2[layer], s_w)
                    for n, a in zip(names, (b1, g1, be1, b2, g_out, b_out)):
                        sp.dma_start(par[n][:], a.rearrange("l (k p) -> p l k", p=128)).then_inc(s_w, 16)
                    d.rows_store(sp)

                @block.gpsimd
                def _(pool):
                    pg.clear_used(pool)
                    d.ring_keep(pool, z1)

                @block.tensor
                def _(pe):
                    norm.tensor(pe)
                    pe.wait_ge(s_w, loads)
                    pe.wait_ge(norm.s_xt, NT + U)
                    d.product(pe, 0, W[:, 0, :, :], hf)
                    d.ring_transpose(pe)

                @block.scalar
                def _(act):
                    norm.scalar(act)
                    act.wait_ge(s_w, loads)
                    d.evacuate(act, 0, z2, bi)
                    act.wait_ge(d.s_ev, d.G)
                    d.ring_fill(act, z2, None)

                @block.vector
                def _(dve):
                    norm.vector(dve)
                    d.rows_out(dve)
        h, spare = z1, hf
        for layer in range(L):
            with ExitStack() as c:
                agg = Aggregate(pg, c, f"agg{layer + 1}", "feature", h)
                with pg.block() as block:
                    block.scalar(agg.scalar)
                    block.gpsimd(agg.gpsimd)
                    block.tensor(agg.tensor)
                    block.vector(agg.vector)
            with ExitStack() as c:
                d = Dense(pg, c, f"layer{layer}")
                p = {n: par[n][:, layer, :] for n in names}
                final = layer == L - 1
                with pg.block() as block:
                    @block.tensor
                    def _(pe):
                        d.product(pe, 0, W[:, 1 + 2 * layer, :, :], h)
                        d.product(pe, 1, W[:, 2 + 2 * layer, :, :], spare)
                        d.ring_transpose(pe)

                    @block.scalar
                    def _(act):
                        d.evacuate(act, 0, spare, p["b1"])
                        d.root(act, 0)
                        d.relu(act, 0, spare)
                        d.evacuate(act, 1, z2, p["b2"])
                        d.root(act, 1)
                        d.ring_fill(act, z2, 1)

                    @block.vector
                    def _(dve):
                        step = Chain(dve, d.s_ch)
                        d.statistics(dve, step, 0, spare, p["g1"], p["be1"])
                        d.statistics(dve, step, 1, z2, p["g_out"], p["b_out"])
                        if final:
                            d.rows_add(dve, pg.X)
                        else:
                            d.rows_out(dve)

                    @block.gpsimd
                    def _(pool):
                        pg.clear_used(pool)
                        if final:
                            pool.sem_inc(d.s_kept, NT + U)
                        else:
                            d.ring_keep(pool, h)

                    @block.sync
                    def _(sp):
                        if not final:
                            d.rows_store(sp)


def run_mixture(pg, ex, load):
    stage_route(pg, ex, load=load)
    stage_experts(pg, ex, residual=pg.X[:])
    stage_combine(pg, ex)


def build(nc, x, src, dst, edge_weight, L0_gnn_W, L0_gnn_bias, L0_ffn_router_w, L0_ffn_w1, L0_ffn_b1,
          L0_ffn_w2, L0_ffn_b2, L1_gnn_W_in, L1_gnn_b_in, L1_gnn_W1, L1_gnn_b1, L1_gnn_g1, L1_gnn_be1,
          L1_gnn_W2, L1_gnn_b2, L1_gnn_g_out, L1_gnn_b_out, L1_ffn_Wr, L1_ffn_W1s, L1_ffn_b1s,
          L1_ffn_W2s, L1_ffn_b2s, L1_ffn_W1p, L1_ffn_b1p, L1_ffn_W2p, L1_ffn_b2p, out):
    with ExitStack() as ctx:
        pg = Program(nc, ctx)
        pg.ps = ctx.enter_context(nc.psum_tensor("ps", [128, 8, 512], fp32))
        pg.X = pg.sb("X", [P, NT, D])
        pg.col = pg.sb("col", [128, 128])
        pg.part = pg.sb("part", [128, 1])
        pg.tiles = pg.sb("tiles", [1, EDGE_PAD])
        pg.ident = pg.sb("ident", [128, 128])
        pg.tri = pg.sb("tri", [128, 128])
        pg.ones = pg.sb("ones", [128, 128])
        pg.prio = pg.sb("prio", [P, NX])
        pg.H = nc.dram_tensor("h_rows", [N, D], fp32).ap()
        pg.pay_dram = nc.dram_tensor("payloads", [128 * EDGE_PAD, 4], fp32).ap()
        pg.XS0 = nc.dram_tensor("expert_rows0", [MOE_TILES * SLOT, D], fp32).ap()
        pg.YS0 = nc.dram_tensor("expert_out0", [MOE_TILES * SLOT, D], fp32).ap()
        pg.x_kept = nc.dram_tensor("x_kept", [N, D], fp32).ap()
        ST = SHARED_TILES + MOE_TILES
        pg.XS1 = nc.dram_tensor("expert_rows1", [ST * SLOT, D], fp32).ap()
        pg.YS1 = nc.dram_tensor("expert_out1", [ST * SLOT, D], fp32).ap()

        edges = ctx.enter_context(ExitStack())
        pg.slots = pg.sb("slots", [128, EDGE_PAD, 4], ctx=edges)
        pg.owner_t = pg.sb("owner_t", [1, EDGE_PAD], int32, ctx=edges)
        pg.owner_n = pg.sb("owner_n", [1, EDGE_PAD], int32, ctx=edges)
        with ExitStack() as c1:
            pg.XN = pg.sb("XN0", [P, NT, D], ctx=c1)
            stage_prepare(pg, x, src, dst, edge_weight, L0_gnn_W, L0_gnn_bias)
        stage_aggregate_nodes(pg)
        with ExitStack() as c1:
            pg.XN = pg.sb("XN1", [P, NT, D], ctx=c1)
            ex = Experts(pg, c1, "moe0", D, 0, pg.XS0, pg.YS0)

            def load0(eng):
                ex.load_weights(eng, lambda k: L0_ffn_router_w.rearrange("e (k p) -> k p e", p=128)[k],
                                L0_ffn_w1, L0_ffn_b1, L0_ffn_w2, L0_ffn_b2)
            run_mixture(pg, ex, load0)
        with ExitStack() as c1:
            pg.XN = pg.sb("XN2", [P, NT, D], ctx=c1)
            stage_network(pg, L1_gnn_W_in, L1_gnn_b_in, L1_gnn_W1, L1_gnn_b1, L1_gnn_g1, L1_gnn_be1,
                          L1_gnn_W2, L1_gnn_b2, L1_gnn_g_out, L1_gnn_b_out)
        edges.close()
        with ExitStack() as c1:
            pg.XN = pg.X
            ex = Experts(pg, c1, "moe1", L1_ffn_W1s.shape[1], SHARED_TILES, pg.XS1, pg.YS1)

            def load1(eng):
                ex.load_weights(eng, lambda k: L1_ffn_Wr[k * 128:(k + 1) * 128, :],
                                L1_ffn_W1p, L1_ffn_b1p, L1_ffn_W2p, L1_ffn_b2p,
                                (L1_ffn_W1s, L1_ffn_b1s, L1_ffn_W2s, L1_ffn_b2s))
            stage_route(pg, ex, keep_x=pg.x_kept, load=load1)
            stage_experts(pg, ex)
            stage_combine(pg, ex, out=out, x_kept=pg.x_kept)


_INS = ['x', 'src', 'dst', 'edge_weight', 'L0_gnn_W', 'L0_gnn_bias', 'L0_ffn_router_w', 'L0_ffn_w1',
        'L0_ffn_b1', 'L0_ffn_w2', 'L0_ffn_b2', 'L1_gnn_W_in', 'L1_gnn_b_in', 'L1_gnn_W1', 'L1_gnn_b1',
        'L1_gnn_g1', 'L1_gnn_be1', 'L1_gnn_W2', 'L1_gnn_b2', 'L1_gnn_g_out', 'L1_gnn_b_out',
        'L1_ffn_Wr', 'L1_ffn_W1s', 'L1_ffn_b1s', 'L1_ffn_W2s', 'L1_ffn_b2s', 'L1_ffn_W1p',
        'L1_ffn_b1p', 'L1_ffn_W2p', 'L1_ffn_b2p']
_OUTS = [((N, D), 'float32')]


def kernel(**inputs):
    import numpy as _np
    import concourse.bacc as _bacc
    from concourse import mybir as _mybir
    from concourse.bass_utils import run_bass_kernel_spmd as _run

    nc = _bacc.Bacc("TRN2", target_bir_lowering=False, num_devices=1)
    arrays, args = {}, []
    for name in _INS:
        a = _np.ascontiguousarray(inputs[name])
        arrays[f"in_{name}_dram"] = a
        args.append(nc.dram_tensor(f"in_{name}_dram", a.shape, _mybir.dt.from_np(a.dtype), kind="ExternalInput").ap())
    for i, (shape, dtype) in enumerate(_OUTS):
        dt = _mybir.dt.from_np(_np.dtype(dtype))
        args.append(nc.dram_tensor(f"out_{i}_dram", shape, dt, kind="ExternalOutput").ap())
    build(nc, *args)
    r = _run(nc, [arrays], core_ids=[0])
    got = tuple(r.results[0][f"out_{i}_dram"] for i in range(len(_OUTS)))
    return got[0]
```

```python
import concourse.bass as bass
from concourse import mybir
from contextlib import ExitStack, contextmanager

fp32 = mybir.dt.float32
fp16 = mybir.dt.float16
int32 = mybir.dt.int32
ALU = mybir.AluOpType
ACT = mybir.ActivationFunctionType
AXIS = mybir.AxisListType

N = 3125
D = 256
P = 125
NT = N // P
KD = D // 128
E = 50000
EJ = E // P
TOP = 2
NX = 8
SLOT = 128
ROUND = 16
HOT = 4
QUAD = 4
HR = 3 * QUAD
EB = 2 * NT
COLD_TILES = (E + NT * (SLOT - 1)) // SLOT
HOT_TILES = (E + NT * (QUAD * SLOT - 1)) // SLOT
EDGE_TILES = (E + NT * ((QUAD + 1) * SLOT - 2)) // SLOT + ROUND - 1
EDGE_PAD = -(-(EDGE_TILES + 2 * HR) // ROUND) * ROUND
COLD_ROUNDS, HOT_ROUNDS = -(-COLD_TILES // ROUND), -(-HOT_TILES // HR)
SORTED = 80
BANKS = 8
MOE_TILES = (TOP * N + NX * (SLOT - 1)) // SLOT
SHARED_TILES = -(-N // SLOT)
LN_EPS = 1e-5
BN_EPS = 1e-5
U = 5
CH = 500
CHUNKS = [(s, min(CH, N - s)) for s in range(0, N, CH)]


class Program:

    def __init__(self, nc, ctx):
        self.nc, self.ctx = nc, ctx
        self.own_sems, self.used_sems = [], []
        self.pool_sems = [self.sem(f"arrived{k}") for k in range(ROUND)]
        self.pool_count = [0] * ROUND

    def sb(self, name, shape, dt=fp32, ctx=None):
        return (ctx or self.ctx).enter_context(self.nc.sbuf_tensor(name, shape, dt))

    def arrivals(self, n, total):
        taken = [Arrival(self.pool_sems[k], self.pool_count[k]) for k in range(n)]
        for k in range(n):
            self.pool_count[k] += total[k] if isinstance(total, list) else total
        return taken

    def sem(self, name, ctx=None):
        handle = (ctx or self.ctx).enter_context(self.nc.semaphore(name))
        if ctx is not None:
            self.own_sems.append(handle.num)
        return handle

    def tiles_at(self, first, n):
        first = self.nc.s_assert_within(first, 0, EDGE_PAD - n, skip_runtime_bounds_check_because=(
            "a list's rounds, and the half round behind them, lie inside the tables for any inputs"))
        return bass.ds(first, n)

    @contextmanager
    def block(self):
        with self.nc.Block() as block:
            yield block
        self.used_sems, self.own_sems = self.own_sems, []

    def clear_used(self, pool):
        nums, self.used_sems = sorted(self.used_sems), []
        while nums:
            n = next((k for k in range(1, len(nums)) if nums[k] != nums[0] + k), len(nums))
            pool.sem_clear(range(nums[0], nums[0] + n))
            nums = nums[n:]


class Arrival:

    def __init__(self, sem, base):
        self.sem, self.base = sem, base

    def wait(self, eng, value):
        eng.wait_ge(self.sem, value + self.base)


class Chain:

    def __init__(self, eng, sem):
        self.eng, self.sem, self.n = eng, sem, 0

    def __call__(self, ins):
        self.n += 1
        ins.then_inc(self.sem, 1)
        self.eng.wait_ge(self.sem, self.n)


def load_weight_chunks(eng, dst, src, sem):
    eng.dma_start(dst, src.rearrange("(k p) m -> p k m", p=128)).then_inc(sem, 16)


def bucket_bases(nc, step, dve, oh, cum, J, B, buf, tot_ready, tot_done, split=None):
    flat = "p b j -> p (b j)"
    step(nc.vector.tensor_tensor_scan(cum.rearrange(flat), oh.rearrange(flat), oh.rearrange(flat),
                                      0.0, ALU.add, ALU.max))
    last = cum[:, :, J - 1]
    before, total = buf["before"], buf["total"]
    step(nc.vector.memset(before[:, 0:1], 0.0))
    step(nc.vector.tensor_copy(before[:, 1:B], last[:, 0:B - 1]))
    nc.vector.tensor_tensor(total[:, 0:B], last, before[:, 0:B], ALU.subtract).then_inc(tot_ready, 1)
    dve.wait_ge(tot_done, 1)
    ti, tf, start, base = buf["ti"], buf["tf"], buf["start"], buf["base"]
    step(nc.vector.tensor_scalar(ti[:, 0:B], buf["ps_all"], float(SLOT - 1), None, ALU.add))
    if split:
        step(nc.vector.tensor_scalar(ti[:, split[0]:B], buf["ps_all"][:, split[0]:B],
                                     float(QUAD * SLOT - 1), None, ALU.add))
    step(nc.vector.tensor_scalar(ti[:, 0:B], ti[:, 0:B], 7, None, ALU.arith_shift_right))
    if split:
        step(nc.vector.tensor_scalar(ti[:, split[0]:B], ti[:, split[0]:B], -QUAD, None, ALU.bitwise_and))
    step(nc.vector.tensor_copy(tf[:, 1:B + 1], ti[:, 0:B]))
    step(nc.vector.memset(tf[:, 0:1], 0.0))
    step(nc.vector.memset(buf["zero"][:, 0:B + 1], 0.0))
    step(nc.vector.tensor_tensor_scan(start[:, 0:B + 1], tf[:, 0:B + 1], buf["zero"][:, 0:B + 1], 0.0,
                                      ALU.add, ALU.add))
    if split:
        b, n = split
        up = ti[:, 0:1]
        step(nc.vector.tensor_scalar(up, start[:, b:b + 1], float(n - 1), None, ALU.add))
        step(nc.vector.tensor_scalar(up, up, -n, None, ALU.bitwise_and))
        step(nc.vector.tensor_copy(tf[:, 0:1], up))
        step(nc.vector.tensor_tensor(tf[:, 0:1], tf[:, 0:1], start[:, b:b + 1], ALU.subtract))
        step(nc.vector.tensor_scalar(start[:, b:B + 1], start[:, b:B + 1], tf[:, 0:1], None, ALU.add))
    step(nc.vector.tensor_scalar(base[:, 0:B], start[0:P, 0:B], float(SLOT), -1.0, ALU.mult, ALU.add))
    step(nc.vector.tensor_tensor(base[:, 0:B], base[:, 0:B], before[:, 0:B], ALU.subtract))
    step(nc.vector.tensor_tensor(base[:, 0:B], base[:, 0:B], buf["ps_pre"], ALU.add))


def bucket_slots(nc, step, dve, oh, cum, J, B, buf, tot_ready, tot_done, slots):
    bucket_bases(nc, step, dve, oh, cum, J, B, buf, tot_ready, tot_done)
    base = buf["base"]
    step(nc.vector.tensor_tensor(cum, cum, base[:, 0:B].unsqueeze(2).to_broadcast([P, B, J]), ALU.add))
    step(nc.vector.tensor_tensor(cum, cum, oh, ALU.mult))
    step(nc.vector.tensor_reduce(slots, cum.rearrange("p b j -> p j b"), AXIS.X, ALU.add))


def slot_buffers(pg, ctx, tag, B):
    sb = lambda n, s, d=fp32: pg.sb(f"{tag}_{n}", s, d, ctx)
    return {"before": sb("before", [P, B]), "total": sb("total", [P, B]),
            "ti": sb("ti", [128, B], int32), "tf": sb("tf", [128, B + 1]), "zero": sb("zero", [128, B + 1]),
            "start": sb("start", [128, B + 1]), "base": sb("base", [P, B]),
            "ps_all": pg.ps[:, 7, 0:B], "ps_pre": pg.ps[0:P, 7, 64:64 + B]}


def bucket_totals(nc, pe, pg, buf, B, tot_ready, tot_done):
    pe.wait_ge(tot_ready, 1)
    nc.tensor.matmul(buf["ps_all"], pg.ones[0:P, :], buf["total"][:, 0:B], start=True, stop=True)
    nc.tensor.matmul(buf["ps_pre"], pg.tri[0:P, 0:P], buf["total"][:, 0:B],
                     start=True, stop=True).then_inc(tot_done, 1)


def owner_table(nc, step, row_t, start, B, count, acc):
    step(nc.vector.memset(acc, 0.0))
    for b in range(1, B):
        step(nc.vector.scalar_tensor_tensor(acc, row_t[0:1, 0:count], start[0:1, b:b + 1], acc,
                                            ALU.is_ge, ALU.add))


class Norm:

    def __init__(self, pg, ctx, tag, use, weight=None, dram=None, features=None, logits=None):
        self.pg, self.use, self.weight, self.dram = pg, use, weight, dram
        self.features, self.logits = features, logits
        sb = lambda n, s, d=fp32: pg.sb(f"{tag}_{n}", s, d, ctx)
        sem = lambda n: pg.sem(f"{tag}_{n}", ctx)
        self.st = sb("stats", [P, NT, 6])
        self.mean, self.var = sb("mean", [P, NT]), sb("var", [P, NT])
        self.dif, self.rstd = sb("dif", [P, NT]), sb("rstd", [P, NT])
        self.ring = sb("xn_ring", [P, U, D])
        self.xt = sb("xn_t", [128, U, KD, P])
        self.rows = sb("rows", [P, U, D]) if use == "rows" else None
        self.s_stat, self.s_var, self.s_std = sem("stat"), sem("var"), sem("std")
        self.s_xn, self.s_ring, self.s_tr, self.s_xt = sem("xn"), sem("ring"), sem("tr"), sem("xt")
        self.s_mm, self.s_out = sem("mm"), sem("out")
        self.s_st = [sem(f"stored{s}") for s in range(U)]
        self.s_ch = sem("chain")

    def vector(self, dve, x_ready=None):
        nc, pg = self.pg.nc, self.pg
        step = Chain(dve, self.s_ch)
        if x_ready is not None:
            dve.wait_ge(*x_ready)
        dve.sem_inc(self.s_xt, U)
        if self.use == "router":
            dve.sem_inc(self.s_out, U)
        with dve.Fori(0, NT) as j:
            nc.vector.bn_stats(self.st[:, bass.ds(j, 1), :], pg.X[:, bass.ds(j, 1), :]).then_inc(self.s_stat, 1)
        dve.wait_ge(self.s_stat, NT)
        st = self.st
        step(nc.vector.tensor_tensor(self.dif[:], st[:, :, 1], st[:, :, 4], ALU.subtract))
        step(nc.vector.tensor_tensor(self.mean[:], st[:, :, 1], st[:, :, 4], ALU.add))
        step(nc.vector.tensor_scalar(self.mean[:], self.mean[:], 0.5, None, ALU.mult))
        step(nc.vector.tensor_tensor(self.var[:], st[:, :, 2], st[:, :, 5], ALU.add))
        step(nc.vector.tensor_scalar(self.var[:], self.var[:], 1.0 / D, LN_EPS, ALU.mult, ALU.add))
        step(nc.vector.tensor_tensor(self.dif[:], self.dif[:], self.dif[:], ALU.mult))
        nc.vector.scalar_tensor_tensor(self.var[:], self.dif[:], 0.25, self.var[:],
                                       ALU.mult, ALU.add).then_inc(self.s_var, 1)
        dve.wait_ge(self.s_std, 1)
        step(nc.vector.reciprocal(self.rstd[:], self.rstd[:]))
        with dve.Fori(0, NT // U) as i:
            for s in range(U):
                j = i * U + s
                nc.vector.tensor_scalar(pg.XN[:, bass.ds(j, 1), :], pg.X[:, bass.ds(j, 1), :],
                                        self.mean[:, bass.ds(j, 1)], self.rstd[:, bass.ds(j, 1)],
                                        ALU.subtract, ALU.mult).then_inc(self.s_xn, 1)
            for s in range(U):
                j = i * U + s
                dve.wait_ge(self.s_tr, U + 1 + j)
                if self.use != "features":
                    dve.wait_ge(self.s_mm, j + 1)
                out = (self.features[:, :, bass.ds(j * P, P)] if self.use == "features"
                       else self.xt[:, s, :, :])
                nc.vector.tensor_copy(out, self.t_psum(s)).then_inc(self.s_xt, 1)
            if self.use == "router":
                for s in range(U):
                    j = i * U + s
                    dve.wait_ge(self.s_mm, U + 1 + j)
                    nc.vector.tensor_copy(self.logits[:, bass.ds(j, 1), :],
                                          pg.ps[0:P, s:s + 1, 256:256 + NX]).then_inc(self.s_out, 1)

    def t_psum(self, s):
        return self.pg.ps[:, s, 0:256].rearrange("p (k q) -> p k q", k=KD)[:, :, 0:P]

    def scalar(self, act):
        nc, pg = self.pg.nc, self.pg
        if self.use == "rows":
            act.sem_inc(self.s_out, U)
            for s in range(U):
                act.sem_inc(self.s_st[s], 16)
        act.wait_ge(self.s_var, 1)
        nc.scalar.activation(self.rstd[:], self.var[:], ACT.Sqrt).then_inc(self.s_std, 1)
        with act.Fori(0, NT // U) as i:
            for s in range(U):
                j = i * U + s
                act.wait_ge(self.s_xn, j + 1)
                act.wait_ge(self.s_tr, i * U + U)
                nc.scalar.copy(self.ring[:, s:s + 1, :], pg.XN[:, bass.ds(j, 1), :]).then_inc(self.s_ring, 1)
            if self.use == "rows":
                for s in range(U):
                    j = i * U + s
                    act.wait_ge(self.s_mm, U + 1 + j)
                    act.wait_ge(self.s_st[s], i * 16 + 16)
                    nc.scalar.copy(self.rows[:, s, :], pg.ps[0:P, s, 256:512]).then_inc(self.s_out, 1)
                for s in range(U):
                    j = i * U + s
                    act.wait_ge(self.s_out, U + 1 + j)
                    act.dma_start(self.dram[bass.ds(j * P, P), :], self.rows[:, s, :]).then_inc(self.s_st[s], 16)
        if self.use == "rows":
            for s in range(U):
                act.wait_ge(self.s_st[s], 16 * (NT // U) + 16)

    def tensor(self, pe, w_ready=None):
        nc, pg = self.pg.nc, self.pg
        if w_ready is not None:
            pe.wait_ge(*w_ready)
        if self.use != "features":
            pe.sem_inc(self.s_mm, U)
        pe.sem_inc(self.s_tr, U)

        def transposes(i, s):
            j = i * U + s
            pe.wait_ge(self.s_ring, j + 1)
            pe.wait_ge(self.s_xt, i * U + U)
            if self.use != "features":
                pe.wait_ge(self.s_out, i * U + U)
            for k in range(KD):
                last = nc.tensor.transpose(pg.ps[:, s, k * 128:k * 128 + P],
                                           self.ring[:, s, k * 128:(k + 1) * 128], pg.ident[0:P, 0:P])
            last.then_inc(self.s_tr, 1)

        def product(i, s):
            pe.wait_ge(self.s_xt, U + 1 + i * U + s)
            width = NX if self.use == "router" else D
            for k in range(KD):
                last = nc.tensor.matmul(pg.ps[0:P, s, 256:256 + width], self.xt[:, s, k, :],
                                        self.weight[:, k, :], start=(k == 0), stop=(k == KD - 1))
            last.then_inc(self.s_mm, 1)

        with pe.Fori(0, NT // U) as i:
            for s in range(U):
                transposes(i, s)
            if self.use != "features":
                for s in range(U):
                    product(i, s)


def stage_prepare(pg, x, src, dst, edge_weight, w_l0, bias_l0):
    nc = pg.nc
    with ExitStack() as ctx:
        sb = lambda n, s, d=fp32: pg.sb(n, s, d, ctx)
        sem = lambda n: pg.sem(n, ctx)
        src_i, dst_i = sb("src_i", [P, EJ], int32), sb("dst_i", [P, EJ], int32)
        src_f, blk = sb("src_f", [P, EJ]), sb("blk", [P, EJ])
        pay = sb("pay", [P, EJ, 4])
        slot_f, row_f = sb("slot_f", [P, EJ]), sb("row_f", [P, EJ])
        slot_i, low_i = sb("slot_i", [P, EJ], int32), sb("low_i", [P, EJ], int32)
        bucket = sb("bucket", [P, EJ], fp16)
        oh = sb("oh", [P, EB, EJ], fp16)
        room = sb("cum_or_xn", [P, EB * EJ // 2])
        cum = room[:].bitcast(fp16).rearrange("p (b j) -> p b j", b=EB)
        pg.XN = room[:, 0:NT * D].rearrange("p (j d) -> p j d", j=NT)
        part = sb("part_slots", [P, EB, SORTED])
        row1 = sb("row1", [1, EDGE_PAD])
        W = sb("w_l0_gnn", [128, KD, D])
        bias = sb("bias_l0", [P, D])
        zero = sb("zero", [128, EDGE_PAD * 4])
        pay_st, idx_st = sb("pay_st", [P, 2, 8, 4]), sb("idx_st", [P, 2, 8], int32)
        owner = sb("owner", [1, EDGE_PAD])
        buf = slot_buffers(pg, ctx, "edges", EB)
        ld_edge, ld_x, ld_w, s_ch, s_const, tri_ok = (sem(n) for n in (
            "ld_edge", "ld_x", "ld_w", "sort_chain", "consts", "tri_ok"))
        tot_ready, tot_done, rows_ok, zeroed, cleared = (sem(n) for n in (
            "tot_ready", "tot_done", "slots_ok", "zeroed", "cleared"))
        s_tick, s_back, s_pool, s_oh = (sem(n) for n in ("tick", "payload_back", "pool_chain", "onehots"))
        staged = [sem(f"staged{h}") for h in range(2)]
        wiped = pg.arrivals(16, 16)
        scat = pg.arrivals(16, 16 * (EJ // 16))
        norm = Norm(pg, ctx, "ln0", "rows", weight=W, dram=pg.H)
        CLEARS = 2

        with pg.block() as block:
            @block.sync
            def _(sp):
                sp.dma_start(src_i[:], src.rearrange("(p j) -> p j", p=P)).then_inc(ld_edge, 16)
                sp.dma_start(dst_i[:], dst.rearrange("(p j) -> p j", p=P)).then_inc(ld_edge, 16)
                sp.dma_start(slot_f[:], edge_weight.rearrange("(p j) -> p j", p=P)).then_inc(ld_edge, 16)
                sp.dma_start(pg.X[:], x.rearrange("(j p) d -> p j d", p=P)).then_inc(ld_x, 16)
                load_weight_chunks(sp, W[:], w_l0, ld_w)
                sp.dma_start(bias[:], bias_l0.partition_broadcast(P)).then_inc(ld_w, 16)
                sp.wait_ge(zeroed, 1)
                for rows, n in ((pg.XS0, MOE_TILES), (pg.XS1, SHARED_TILES + MOE_TILES)):
                    sp.dma_start(rows.rearrange("(t p) d -> p t d", p=128),
                                 zero[:, 0:D].unsqueeze(1).to_broadcast([128, n, D])).then_inc(cleared, 16)
                for q in range(EJ // SORTED):
                    sp.wait_ge(rows_ok, q + 1)
                    with sp.Fori(0, SORTED // 16) as n:
                        i = n + q * (SORTED // 16)
                        for h in range(2):
                            for k in range(8):
                                scat[8 * h + k].wait(sp, 16 * i)
                            cols = bass.ds(i * 16 + 8 * h, 8)
                            sp.dma_start(pay_st[:, h, :, :], pay[:, cols, :]).then_inc(staged[h], 16)
                            sp.dma_start(idx_st[:, h, :], slot_i[:, cols]).then_inc(staged[h], 16)
                for k in range(16):
                    scat[k].wait(sp, 16 * (EJ // 16))
                sp.dma_start(pg.slots[:].rearrange("p c f -> p (c f)"),
                             pg.pay_dram.rearrange("(p c) f -> p (c f)", p=128)).then_inc(s_back, 16)
                sp.wait_ge(s_back, 16)

            @block.gpsimd
            def _(pool):
                pg.clear_used(pool)
                step = Chain(pool, s_pool)
                g = nc.gpsimd
                step(g.memset(zero[:], 0.0))
                pool.sem_inc(zeroed, 1)
                f = {"allow_small_or_imprecise_dtypes": True}
                step(g.iota(pg.col[:], [[1, 128]], base=0, channel_multiplier=0, **f))
                step(g.iota(pg.tiles[:], [[1, EDGE_PAD]], base=0, channel_multiplier=0, **f))
                step(g.iota(pg.part[:], [[1, 1]], base=0, channel_multiplier=1, **f))
                step(g.iota(pg.hot_col[:], [[1, HOT * P]], base=0, channel_multiplier=0, **f))
                step(g.iota(pg.prio[:], [[-1, NX]], base=NX, channel_multiplier=0, **f))
                step(g.memset(pg.ones[:], 1.0))
                pool.sem_inc(s_const, 1)
                piece = 128 // 16
                for k in range(16):
                    rows = slice(k * piece * EDGE_PAD, (k + 1) * piece * EDGE_PAD)
                    pool.dma_start(pg.pay_dram[rows, :].rearrange("(p c) f -> p (c f)", p=piece),
                                   zero[k * piece:(k + 1) * piece, :]).then_inc(wiped[k].sem, 16)
                for k in range(16):
                    wiped[k].wait(pool, 16)
                pool.wait_ge(cleared, 16 * CLEARS)
                with pool.Fori(0, EJ // 16) as i:
                    for h in range(2):
                        pool.wait_ge(staged[h], 32 * i + 32)
                        pool.sem_inc(s_tick, 1)
                        for k in range(8):
                            g.indirect_dma_start(
                                pg.pay_dram, bass.IndirectOffsetOnAxis(ap=idx_st[:, h, k:k + 1], axis=0),
                                pay_st[:, h, k, :], None).then_inc(scat[8 * h + k].sem, 16)

            @block.vector
            def _(dve):
                step = Chain(dve, s_ch)
                v = nc.vector
                dve.wait_ge(s_const, 1)
                step(v.tensor_scalar(pg.ident[:], pg.col[:], pg.part[:, 0:1], None, ALU.is_equal))
                v.tensor_scalar(pg.tri[:], pg.col[:], pg.part[:, 0:1], None, ALU.is_gt).then_inc(tri_ok, 1)
                dve.wait_ge(ld_edge, 48)
                step(v.tensor_copy(src_f[:], src_i[:]))
                step(v.tensor_copy(pay[:, :, 2], dst_i[:]))
                step(v.tensor_copy(pay[:, :, 1], slot_f[:]))
                step(v.memset(pay[:, :, 3], 0.0))
                step(v.tensor_scalar(slot_i[:], src_f[:], 1.0 / P, None, ALU.mult))
                step(v.tensor_copy(blk[:], slot_i[:]))
                step(v.scalar_tensor_tensor(row_f[:], blk[:], -float(P), src_f[:], ALU.mult, ALU.add))
                step(v.scalar_tensor_tensor(blk[:], row_f[:], 0.0, blk[:], ALU.is_ge, ALU.add))
                step(v.scalar_tensor_tensor(blk[:], row_f[:], float(P), blk[:], ALU.is_ge, ALU.add))
                step(v.tensor_scalar(blk[:], blk[:], -1.0, None, ALU.add))
                step(v.scalar_tensor_tensor(pay[:, :, 0], blk[:], -float(P), src_f[:], ALU.mult, ALU.add))
                step(v.tensor_scalar(row_f[:], pay[:, :, 2], float(HOT * P), float(NT), ALU.is_lt, ALU.mult))
                step(v.tensor_tensor(bucket[:], blk[:], row_f[:], ALU.add))
                for b in range(EB):
                    v.tensor_scalar(oh[:, b, :], bucket[:], float(b), None, ALU.is_equal).then_inc(s_oh, 1)
                dve.wait_ge(s_oh, EB)
                bucket_bases(nc, step, dve, oh[:], cum, EJ, EB, buf, tot_ready, tot_done,
                             split=(NT, ROUND))
                for q in range(EJ // SORTED):
                    c = slice(q * SORTED, (q + 1) * SORTED)
                    step(v.tensor_tensor(part[:], cum[:, :, c],
                                         buf["base"][:, 0:EB].unsqueeze(2).to_broadcast([P, EB, SORTED]), ALU.add))
                    step(v.tensor_tensor(part[:], part[:], oh[:, :, c], ALU.mult))
                    step(v.tensor_reduce(slot_f[:, c], part[:].rearrange("p b j -> p j b"), AXIS.X, ALU.add))
                    step(v.tensor_copy(slot_i[:, c], slot_f[:, c]))
                    step(v.tensor_scalar(low_i[:, c], slot_i[:, c], SLOT - 1, None, ALU.bitwise_and))
                    step(v.tensor_scalar(slot_i[:, c], slot_i[:, c], 7, None, ALU.arith_shift_right))
                    step(v.tensor_copy(slot_f[:, c], slot_i[:, c]))
                    step(v.tensor_copy(row_f[:, c], low_i[:, c]))
                    step(v.scalar_tensor_tensor(row_f[:, c], row_f[:, c], float(EDGE_PAD), slot_f[:, c],
                                                ALU.mult, ALU.add))
                    step(v.tensor_copy(slot_i[:, c], row_f[:, c]))
                    dve.sem_inc(rows_ok, 1)
                owner_table(nc, step, pg.tiles, buf["start"], EB, EDGE_PAD, owner[:])
                step(v.tensor_scalar(pg.owner_n[:], owner[:], float(P), None, ALU.mult))
                step(v.tensor_copy(pg.owner_t[:], owner[:]))
                step(v.tensor_scalar(owner[:], owner[:], -float(NT), 0.0, ALU.add, ALU.max))
                step(v.tensor_scalar(pg.owner_h[:], owner[:], float(P), None, ALU.mult))
                first, end = buf["start"][0:1, NT:NT + 1], buf["start"][0:1, EB:EB + 1]
                step(v.tensor_copy(pg.lists[:, 0:1], first))
                step(v.tensor_scalar(pg.lists[:, 1:2], first, 1.0 / ROUND, None, ALU.mult))
                step(v.tensor_tensor(row1[:, 0:1], end, first, ALU.subtract))
                step(v.tensor_scalar(owner[:, 0:HOT_ROUNDS], pg.tiles[:, 0:HOT_ROUNDS], float(HR), row1[:, 0:1],
                                     ALU.mult, ALU.is_lt))
                step(v.tensor_reduce(row1[:, 1:2], owner[:, 0:HOT_ROUNDS], AXIS.X, ALU.add))
                step(v.tensor_copy(pg.lists[:, 2:3], row1[:, 1:2]))
                norm.vector(dve, (ld_x, 16))
                dve.wait_ge(ld_w, 32)
                step(v.tensor_tensor(pg.X[:], pg.X[:], bias[:].unsqueeze(1).to_broadcast([P, NT, D]), ALU.add))

            @block.tensor
            def _(pe):
                pe.wait_ge(s_const, 1)
                pe.wait_ge(tri_ok, 1)
                bucket_totals(nc, pe, pg, buf, EB, tot_ready, tot_done)
                norm.tensor(pe, (ld_w, 32))

            @block.scalar
            def _(act):
                norm.scalar(act)


class Aggregate:
    BANKS = 4

    def __init__(self, pg, ctx, tag, by, acc, room=None):
        self.pg, self.by, self.acc = pg, by, acc
        sb = lambda n, s, d=fp32: pg.sb(f"{tag}_{n}", s, d, ctx)
        sem = lambda n: pg.sem(f"{tag}_{n}", ctx)
        if room is None:
            room = sb("room", [128, ROUND * (D + P)])
        self.G = room[:, 0:ROUND * D].rearrange("p (k d) -> p k d", k=ROUND)
        self.S = room[:, ROUND * D:ROUND * (D + P)].rearrange("p (k q) -> p k q", k=ROUND)
        self.key = sb("key", [128, ROUND, 2])
        self.idx = sb("idx", [128, ROUND], int32)
        self.s_got = [pg.sem(f"{tag}_arrived{q}") for q in range(ROUND // 4)]
        self.s_key, self.s_hot, self.s_mm, self.s_acc, self.s_tick = (
            sem(n) for n in ("key", "hot", "mm", "acc", "tick"))

    def rounds(self, eng, k=1):
        return eng.value_load(self.pg.lists[0:1, k:k + 1], min_val=0,
                              max_val=COLD_ROUNDS if k == 1 else HOT_ROUNDS)

    def stage(self, act, i, h):
        act.wait_ge(self.s_mm, ROUND * i + 8 * (h + 1))
        act.wait_ge(self.s_hot, ROUND * i + 8 * (h + 1))
        cols = self.pg.tiles_at(i * ROUND + 8 * h, 8)
        half = slice(8 * h, 8 * h + 8)
        self.pg.nc.scalar.copy(self.idx[:, half], self.pg.slots[:, cols, 2])
        self.pg.nc.scalar.copy(self.key[:, half, :], self.pg.slots[:, cols, 0:2]).then_inc(self.s_key, 1)

    def stage_round(self, act, n, i):
        for h in range(2):
            self.stage_half(act, n, i, h)

    def stage_half(self, act, n, i, h):
        with act.If(n > i - 1 if h == 0 else n > i):
            self.stage(act, i, h)

    def gather_round(self, pool, n, i):
        with pool.If(n > i):
            for h in range(2):
                pool.wait_ge(self.s_key, 2 * i + h + 1)
                pool.wait_ge(self.s_mm, ROUND * i + 8 * (h + 1))
                pool.sem_inc(self.s_tick, 1)
                for k in range(8 * h, 8 * h + 8):
                    self.pg.nc.gpsimd.indirect_dma_start(
                        self.G[:, k, :], None, self.pg.H,
                        bass.IndirectOffsetOnAxis(ap=self.idx[:, k:k + 1], axis=0)).then_inc(self.s_got[k // 4], 16)

    def target(self, k):
        b = k % self.BANKS
        if self.by == "node":
            return self.pg.ps[0:P, b, 0:D]
        return self.pg.ps[:, b, 0:KD * P].rearrange("p (k q) -> p k q", k=KD)

    def product_round(self, pe, n, i):
        for h in range(2):
            self.product_half(pe, n, i, h)

    def product_half(self, pe, n, i, h):
        nc = self.pg.nc
        with pe.If(n > i):
            for k in range(8 * h, 8 * h + 8):
                if k % 4 == 0:
                    pe.wait_ge(self.s_got[k // 4], 64 * i + 64)
                pe.wait_ge(self.s_hot, ROUND * i + ROUND + k + 1)
                pe.wait_ge(self.s_acc, ROUND * i + k + 1)
                out = self.target(k)
                if self.by == "node":
                    last = nc.tensor.matmul(out, self.S[:, k, :], self.G[:, k, :], start=True, stop=True)
                else:
                    for c in range(KD):
                        last = nc.tensor.matmul(out[:, c, :], self.G[:, k, c * 128:(c + 1) * 128],
                                                self.S[:, k, :], start=True, stop=True)
                last.then_inc(self.s_mm, 1)

    def onehot(self, dve, i, k):
        if k % 8 == 0:
            dve.wait_ge(self.s_key, 2 * i + k // 8 + 1)
        dve.wait_ge(self.s_mm, ROUND * i + k + 1)
        self.pg.nc.vector.tensor_scalar(self.S[:, k, :], self.pg.col[:, 0:P], self.key[:, k, 0:1],
                                        self.key[:, k, 1:2], ALU.is_equal, ALU.mult).then_inc(self.s_hot, 1)

    def owners(self, i, h):
        table = self.pg.owner_t if self.by == "node" else self.pg.owner_n
        _, own = self.pg.nc.values_load_multi_w_load_instructions(
            table[0:1, self.pg.tiles_at(i * ROUND + 8 * h, 8)], engines=(mybir.EngineType.DVE,),
            min_val=0, max_val=NT - 1 if self.by == "node" else N - P)
        return own

    def add(self, dve, i, k, own):
        nc, t = self.pg.nc, ROUND * i + k
        dve.wait_ge(self.s_mm, ROUND + 1 + t)
        dve.wait_ge(self.s_acc, self.BANKS + t)
        if self.by == "node":
            a, p = self.acc[:, bass.ds(own, 1), :], self.target(k).unsqueeze(1)
        else:
            a, p = self.acc[:, :, bass.ds(own, P)], self.target(k)
        nc.vector.tensor_tensor(a, a, p, ALU.add).then_inc(self.s_acc, 1)

    def vector_start(self, dve):
        dve.sem_inc(self.s_hot, ROUND)
        dve.sem_inc(self.s_acc, self.BANKS)
        for k in range(8):
            self.onehot(dve, 0, k)

    def add_round(self, dve, n, i):
        for h in range(2):
            self.add_half(dve, n, i, h)

    def add_half(self, dve, n, i, h):
        with dve.If(n > i):
            own = self.owners(i, h)
            for k in range(8):
                self.add(dve, i, 8 * h + k, own[k])
                self.onehot(dve, i + h, 8 * (1 - h) + k)


def stage_aggregate_nodes(pg):
    nc = pg.nc
    Q = HR // QUAD
    with ExitStack() as ctx:
        agg = Aggregate(pg, ctx, "agg0", "node", pg.X)
        sb = lambda n, s, d=fp32: pg.sb(n, s, d, ctx)
        S, T = sb("hot_sources", [128, HR, P]), sb("hot_targets", [128, HR, HOT * P])
        away = sb("hot_away", [128, QUAD, HOT * P])
        key = sb("hot_key", [128, HR, 3])
        s_key, s_neg, s_away, s_src, s_dst, s_mm, s_add = (pg.sem(f"hot_{n}", ctx) for n in (
            "key", "negated", "away", "sources", "targets", "mm", "add"))
        LOOPS = max(COLD_ROUNDS + 1, HOT_ROUNDS + 1)

        def block_psum(q):
            return pg.ps[0:P, 4 + q, 0:HOT * P].rearrange("p (d q) -> p d q", d=HOT)

        def stage_hot(act, m, first, i):
            with act.If(m > i - 1):
                act.wait_ge(s_src, i * HR + HR)
                act.wait_ge(s_dst, i * HR + HR)
                nc.scalar.copy(key[:, :, 0:2], pg.slots[:, pg.tiles_at(first + i * HR, HR), 0:2]).then_inc(s_key, 1)
                nc.scalar.activation(key[:, :, 2], pg.slots[:, pg.tiles_at(first + i * HR, HR), 2],
                                     ACT.Copy, scale=-1.0).then_inc(s_neg, 1)

        def targets(act, m, i, q):
            with act.If(m > i):
                act.wait_ge(s_neg, i + 1)
                for u in range(QUAD):
                    k = q * QUAD + u
                    act.wait_ge(s_dst, i * HR + (k + HR - QUAD + 1))
                    nc.scalar.activation(away[:, u, :], pg.hot_col[:], ACT.Abs,
                                         bias=key[:, k, 2:3]).then_inc(s_away, 1)
                act.wait_ge(s_mm, i * Q + (q + 1))
                for u in range(QUAD):
                    k = q * QUAD + u
                    act.wait_ge(s_away, i * HR + (k + 1))
                    nc.scalar.activation(T[:, k, :], away[:, u, :], ACT.Relu, bias=pg.ones[:, 0:1],
                                         scale=-1.0).then_inc(s_dst, 1)

        def sources(dve, i, q):
            if q == 0:
                dve.wait_ge(s_key, i + 1)
            dve.wait_ge(s_mm, i * Q + (q + 1))
            for k in range(q * QUAD, (q + 1) * QUAD):
                nc.vector.tensor_scalar(S[:, k, :], pg.col[:, 0:P], key[:, k, 0:1], key[:, k, 1:2],
                                        ALU.is_equal, ALU.mult).then_inc(s_src, 1)

        def quad_product(pe, m, i, q):
            with pe.If(m > i):
                pe.wait_ge(s_add, i * Q + (q + 1))
                pe.wait_ge(s_src, i * HR + (HR + (q + 1) * QUAD))
                pe.wait_ge(s_dst, i * HR + (HR + (q + 1) * QUAD))
                for d in range(HOT):
                    for u in range(QUAD):
                        k = q * QUAD + u
                        last = nc.tensor.matmul(block_psum(q)[:, d, :], T[:, k, d * P:(d + 1) * P], S[:, k, :],
                                                start=(u == 0), stop=(u == QUAD - 1))
                last.then_inc(s_mm, 1)

        def quad_add(dve, m, first, i, q):
            with dve.If(m > i):
                own = dve.value_load(pg.owner_h[0:1, pg.tiles_at(first + (i * HR + q * QUAD), 1)],
                                     min_val=0, max_val=N - P)
                dve.wait_ge(s_mm, i * Q + (Q + q + 1))
                dve.wait_ge(s_add, i * Q + (Q + q))
                a = pg.A[:, :, bass.ds(own, P)]
                nc.vector.tensor_tensor(a, a, block_psum(q), ALU.add).then_inc(s_add, 1)
                sources(dve, i + 1, q)

        with pg.block() as block:
            @block.scalar
            def _(act):
                n, m = agg.rounds(act), agg.rounds(act, 2)
                first = act.value_load(pg.lists[0:1, 0:1], min_val=0, max_val=EDGE_PAD)
                act.sem_inc(s_dst, HR)
                with act.Fori(0, LOOPS) as i:
                    agg.stage_half(act, n, i, 0)
                    stage_hot(act, m, first, i)
                    targets(act, m, i, 0)
                    agg.stage_half(act, n, i, 1)
                    for q in range(1, Q):
                        targets(act, m, i, q)

            @block.gpsimd
            def _(pool):
                pg.clear_used(pool)
                n = agg.rounds(pool)
                with pool.Fori(0, COLD_ROUNDS) as i:
                    agg.gather_round(pool, n, i)

            @block.tensor
            def _(pe):
                n, m = agg.rounds(pe), agg.rounds(pe, 2)
                pe.sem_inc(agg.s_mm, ROUND)
                pe.sem_inc(s_mm, Q)
                with pe.Fori(0, LOOPS) as i:
                    agg.product_half(pe, n, i, 0)
                    quad_product(pe, m, i, 0)
                    agg.product_half(pe, n, i, 1)
                    for q in range(1, Q):
                        quad_product(pe, m, i, q)

            @block.vector
            def _(dve):
                n, m = agg.rounds(dve), agg.rounds(dve, 2)
                first = dve.value_load(pg.lists[0:1, 0:1], min_val=0, max_val=EDGE_PAD)
                nc.vector.memset(pg.A[:], 0.0).then_inc(s_add, Q)
                dve.sem_inc(s_src, HR)
                agg.vector_start(dve)
                for q in range(Q):
                    sources(dve, 0, q)
                with dve.Fori(0, LOOPS) as i:
                    agg.add_half(dve, n, i, 0)
                    quad_add(dve, m, first, i, 0)
                    agg.add_half(dve, n, i, 1)
                    for q in range(1, Q):
                        quad_add(dve, m, first, i, q)

    with ExitStack() as ctx:
        Hh = pg.sb("hot_rows", [P, HOT, D], ctx=ctx)
        s_ld, s_mm, s_add = (pg.sem(f"share_{n}", ctx) for n in ("rows", "mm", "add"))
        with pg.block() as block:
            @block.sync
            def _(sp):
                load_hot_rows(pg, sp, Hh, s_ld)

            @block.gpsimd
            def _(pool):
                pg.clear_used(pool)

            @block.tensor
            def _(pe):
                pe.wait_ge(s_ld, 16)
                for j in range(NT):
                    if j >= BANKS:
                        pe.wait_ge(s_add, j - BANKS + 1)
                    for d in range(HOT):
                        last = nc.tensor.matmul(pg.ps[0:P, j % BANKS, 0:D], pg.A[:, d, j * P:(j + 1) * P],
                                                Hh[:, d, :], start=(d == 0), stop=(d == HOT - 1))
                    last.then_inc(s_mm, 1)

            @block.vector
            def _(dve):
                for j in range(NT):
                    dve.wait_ge(s_mm, j + 1)
                    nc.vector.tensor_tensor(pg.X[:, j, :], pg.X[:, j, :], pg.ps[0:P, j % BANKS, 0:D],
                                            ALU.add).then_inc(s_add, 1)


def load_hot_rows(pg, eng, dst, sem):
    eng.dma_start(dst[:], pg.H[0:HOT * P, :].rearrange("(d p) f -> p d f", p=P)).then_inc(sem, 16)


def stage_aggregate_features(pg, tag, acc, room):
    nc = pg.nc
    W = 2 * P
    PIECES = N // W
    with ExitStack() as ctx:
        agg = Aggregate(pg, ctx, tag, "feature", acc, room)
        Hh = pg.sb(f"{tag}_hot_rows", [P, HOT, D], ctx=ctx)
        s_ld, s_mm, s_add, s_tick = (pg.sem(f"{tag}_share_{n}", ctx) for n in ("rows", "mm", "add", "tick"))
        share = pg.ps[:, 4, :]

        def product(pe, first, width):
            for c in range(KD):
                for d in range(HOT):
                    last = nc.tensor.matmul(share[:, c * W:c * W + width], Hh[:, d, c * 128:(c + 1) * 128],
                                            pg.A[:, d, bass.ds(first, width)], start=(d == 0), stop=(d == HOT - 1))
            last.then_inc(s_mm, 1)

        def add(first, width):
            a = acc[:, :, bass.ds(first, width)]
            nc.vector.tensor_tensor(a, a, share[:, 0:KD * W].rearrange("p (k w) -> p k w", k=KD)[:, :, 0:width],
                                    ALU.add).then_inc(s_add, 1)

        with pg.block() as block:
            @block.sync
            def _(sp):
                load_hot_rows(pg, sp, Hh, s_ld)

            @block.scalar
            def _(act):
                n = agg.rounds(act)
                with act.Fori(0, COLD_ROUNDS + 1) as i:
                    agg.stage_round(act, n, i)

            @block.gpsimd
            def _(pool):
                pg.clear_used(pool)
                n = agg.rounds(pool)
                with pool.Fori(0, COLD_ROUNDS) as i:
                    agg.gather_round(pool, n, i)

            @block.tensor
            def _(pe):
                n = agg.rounds(pe)
                pe.sem_inc(agg.s_mm, ROUND)
                pe.wait_ge(s_ld, 16)
                product(pe, PIECES * W, P)
                with pe.Fori(0, PIECES) as i:
                    agg.product_round(pe, n, i)
                    pe.wait_ge(s_add, i + 1)
                    product(pe, i * W, W)
                with pe.Fori(0, COLD_ROUNDS - PIECES) as i:
                    agg.product_round(pe, n, i + PIECES)

            @block.vector
            def _(dve):
                n = agg.rounds(dve)
                agg.vector_start(dve)
                dve.wait_ge(s_mm, 1)
                add(PIECES * W, P)
                with dve.Fori(0, PIECES) as i:
                    dve.wait_ge(s_add, i + 1)
                    dve.sem_inc(s_tick, 1)
                    agg.add_round(dve, n, i)
                    with dve.If(n > i):
                        dve.wait_ge(agg.s_acc, i * ROUND + (ROUND + agg.BANKS))
                        dve.sem_inc(s_tick, 1)
                    dve.wait_ge(s_mm, i + 2)
                    add(i * W, W)
                dve.wait_ge(s_add, PIECES + 1)
                with dve.Fori(0, COLD_ROUNDS - PIECES) as i:
                    agg.add_round(dve, n, i + PIECES)


def rolled(eng, first, end, unroll, body):
    n = (end - first) // unroll
    if n > 1:
        with eng.Fori(0, n) as i:
            for u in range(unroll):
                body(i * unroll + (first + u), (first + u) % unroll)
    else:
        n = 0
    for t in range(first + n * unroll, end):
        body(t, t % unroll)


class Experts:

    def __init__(self, pg, ctx, tag, F, shared, XS, YS):
        self.pg, self.tag, self.F, self.FK, self.shared, self.XS, self.YS = pg, tag, F, F // 128, shared, XS, YS
        self.T = shared + MOE_TILES
        self.NE = NX + (1 if shared else 0)
        sb = lambda n, s, d=fp32: pg.sb(f"{tag}_{n}", s, d, ctx)
        self.W1 = sb("w1", [128, self.NE, KD, F])
        self.W2 = sb("w2", [128, self.NE, self.FK, D])
        self.b1 = sb("b1", [128, self.NE, self.FK])
        self.b2 = sb("b2", [128, self.NE, D])
        self.wr = sb("wr", [128, KD, NX])
        self.slot_i = sb("slot_i", [P, TOP * NT], int32)
        self.gate = sb("gate", [P, TOP, NT])
        self.owner = sb("owner", [1, self.T], int32)
        self.s_w = pg.sem(f"{tag}_weights")
        self.loads = 16 * (KD + 2 + 2 * NX + (4 if shared else 0))

    def load(self, eng, dst, src):
        with self.pg.nc.allow_non_contiguous_dma(reason="a few vectors, one value a partition"):
            eng.dma_start(dst, src).then_inc(self.s_w, 16)

    def load_weights(self, eng, wr, w1, b1, w2, b2, shared=None):
        for k in range(KD):
            self.load(eng, self.wr[:, k, :], wr(k))
        self.load(eng, self.b1[:, 0:NX, :], b1.rearrange("e (k p) -> p e k", p=128))
        self.load(eng, self.b2[:, 0:NX, :], b2.partition_broadcast(128))
        for e in range(NX):
            self.load(eng, self.W1[:, e, :, :], w1[e].rearrange("(k p) f -> p k f", p=128))
            self.load(eng, self.W2[:, e, :, :], w2[e].rearrange("(k p) f -> p k f", p=128))
        if shared:
            v1, c1, v2, c2 = shared
            self.load(eng, self.W1[:, NX, :, :], v1.rearrange("(k p) f -> p k f", p=128))
            self.load(eng, self.W2[:, NX, :, :], v2.rearrange("(k p) f -> p k f", p=128))
            self.load(eng, self.b1[:, NX, :], c1.rearrange("(k p) -> p k", p=128))
            self.load(eng, self.b2[:, NX, :], c2.partition_broadcast(128))


def stage_route(pg, ex, keep_x=None, load=None):
    nc = pg.nc
    B, J = NX, TOP * NT
    with ExitStack() as ctx:
        sb = lambda n, s, d=fp32: pg.sb(f"{ex.tag}_{n}", s, d, ctx)
        sem = lambda n: pg.sem(f"{ex.tag}_{n}", ctx)
        logit, prob = sb("logit", [P, NT, NX]), sb("prob", [P, NT, NX])
        cand = sb("cand", [P, NT, NX])
        top, best = sb("top", [P, TOP, NT]), sb("best", [P, NT])
        oh, cum = sb("oh", [P, B, J]), sb("cum", [P, B, J])
        slot_f, own = sb("slot_f", [P, J]), sb("own", [1, ex.T])
        buf = slot_buffers(pg, ctx, ex.tag, B)
        s_ch, s_log, s_exp, tot_ready, tot_done, s_kept = (
            sem(n) for n in ("route_chain", "logits", "exp", "tot_ready", "tot_done", "kept"))
        norm = Norm(pg, ctx, ex.tag, "router", weight=ex.wr, logits=logit)
        with pg.block() as block:
            @block.sync
            def _(sp):
                if keep_x is not None:
                    sp.dma_start(keep_x.rearrange("(j p) d -> p j d", p=P), pg.X[:]).then_inc(s_kept, 16)
                if load:
                    load(sp)
                if keep_x is not None:
                    sp.wait_ge(s_kept, 16)

            @block.gpsimd
            def _(pool):
                pg.clear_used(pool)

            @block.tensor
            def _(pe):
                norm.tensor(pe, (ex.s_w, ex.loads))
                bucket_totals(nc, pe, pg, buf, B, tot_ready, tot_done)

            @block.scalar
            def _(act):
                norm.scalar(act)
                act.wait_ge(s_log, 1)
                nc.scalar.activation(prob[:], logit[:], ACT.Exp).then_inc(s_exp, 1)

            @block.vector
            def _(dve):
                v = nc.vector
                step = Chain(dve, s_ch)
                wide = lambda a: a.unsqueeze(2).to_broadcast([P, NT, NX])
                prio = pg.prio[:].unsqueeze(1).to_broadcast([P, NT, NX])
                norm.vector(dve, (s_kept, 16) if keep_x is not None else None)
                dve.wait_ge(norm.s_out, NT + U)
                step(v.tensor_reduce(best[:], logit[:], AXIS.X, ALU.max))
                v.tensor_tensor(logit[:], logit[:], wide(best[:]), ALU.subtract).then_inc(s_log, 1)
                dve.wait_ge(s_exp, 1)
                step(v.tensor_reduce(best[:], prob[:], AXIS.X, ALU.add))
                step(v.reciprocal(best[:], best[:]))
                step(v.tensor_tensor(prob[:], prob[:], wide(best[:]), ALU.mult))
                for c in range(TOP):
                    picked = oh[:, :, c * NT:(c + 1) * NT].rearrange("p e j -> p j e")
                    step(v.tensor_reduce(top[:, c, :], prob[:], AXIS.X, ALU.max))
                    step(v.tensor_tensor(cand[:], prob[:], wide(top[:, c, :]), ALU.is_equal))
                    step(v.tensor_tensor(cand[:], cand[:], prio, ALU.mult))
                    step(v.tensor_reduce(best[:], cand[:], AXIS.X, ALU.max))
                    step(v.tensor_tensor(picked, cand[:], wide(best[:]), ALU.is_equal))
                    if c + 1 < TOP:
                        step(v.scalar_tensor_tensor(prob[:], picked, -2.0, prob[:], ALU.mult, ALU.add))
                step(v.tensor_tensor(best[:], top[:, 0, :], top[:, 1, :], ALU.add))
                step(v.tensor_scalar(best[:], best[:], 1e-12, None, ALU.max))
                step(v.reciprocal(best[:], best[:]))
                for c in range(TOP):
                    step(v.tensor_tensor(ex.gate[:, c, :], top[:, c, :], best[:], ALU.mult))
                bucket_slots(nc, step, dve, oh[:], cum[:], J, B, buf, tot_ready, tot_done, slot_f[:])
                if ex.shared:
                    step(v.tensor_scalar(slot_f[:], slot_f[:], float(ex.shared * SLOT), None, ALU.add))
                    step(v.memset(own[:, 0:ex.shared], float(NX)))
                step(v.tensor_copy(ex.slot_i[:], slot_f[:]))
                owner_table(nc, step, pg.tiles, buf["start"], B, MOE_TILES, own[:, ex.shared:])
                step(v.tensor_copy(ex.owner[:], own[:]))


def stage_experts(pg, ex, residual=None):
    nc = pg.nc
    F, FK, T = ex.F, ex.FK, ex.T
    R = 2
    NB = -(-F // 512)
    with ExitStack() as ctx:
        sb = lambda n, s, d=fp32: pg.sb(f"{ex.tag}_{n}", s, d, ctx)
        sem = lambda n: pg.sem(f"{ex.tag}_{n}", ctx)
        xs, xt = sb("xs", [128, R, D]), sb("xt", [128, R, KD, 128])
        hid, ht = sb("hid", [128, F]), sb("ht", [128, R, FK, 128])
        y = sb("y", [128, R, D])
        s_sh, s_ch, s_tick = sem("shared_rows"), sem("chain2"), sem("tick")
        s_sc, *s_st = pg.arrivals(1 + R, [16 * TOP * NT] + [16 * ((T - r + R - 1) // R) for r in range(R)])
        s_ld = [sem(f"loaded{r}") for r in range(R)]
        s_a, s_xt, s_b, s_h, s_c, s_g, s_d, s_y = (sem(n) for n in (
            "x_transposed", "xt_ok", "fc1", "hid_ok", "h_transposed", "gelu", "fc2", "y_ok"))
        ps_x, ps_h = pg.ps[:, 0, 0:D], pg.ps[:, 1:1 + NB, :]
        ps_t, ps_y = pg.ps[:, 3:3 + NB, :], pg.ps[:, 5, 0:D]
        tile_rows = lambda ap, t: ap[bass.ds(t * SLOT, SLOT), :]

        def times16(t, r):
            return (t - r) * (16 // R) + 16

        def stored16(t, r):
            return (t - r) * (16 // R)

        with pg.block() as block:
            @block.gpsimd
            def _(pool):
                pg.clear_used(pool)
                for c in range(TOP):
                    for j in range(NT):
                        nc.gpsimd.indirect_dma_start(
                            ex.XS, bass.IndirectOffsetOnAxis(ap=ex.slot_i[:, c * NT + j:c * NT + j + 1], axis=0),
                            pg.XN[:, j, :], None).then_inc(s_sc.sem, 16)

                def store(t, r):
                    pool.wait_ge(s_y, t + 2)
                    pool.sem_inc(s_tick, 1)
                    pool.dma_start(tile_rows(ex.YS, t), y[:, r, :]).then_inc(s_st[r].sem, 16)

                rolled(pool, 0, T, R, store)
                for r in range(R):
                    s_st[r].wait(pool, 16 * ((T - r + R - 1) // R))

            @block.sync
            def _(sp):
                def load(t, r):
                    sp.wait_ge(s_a, t + 1)
                    sp.dma_start(xs[:, r, :], tile_rows(ex.XS, t)).then_inc(s_ld[r], 16)

                if ex.shared:
                    sp.dma_start(ex.XS[0:N, :].rearrange("(j p) d -> p j d", p=P), pg.XN[:]).then_inc(s_sh, 16)
                    sp.wait_ge(s_sh, 16)
                    rolled(sp, 0, ex.shared, R, load)
                s_sc.wait(sp, 16 * TOP * NT)
                rolled(sp, ex.shared, T, R, load)

            @block.tensor
            def _(pe):
                pe.sem_inc(s_a, R)
                pe.wait_ge(ex.s_w, ex.loads)

                def expert(t):
                    return nc.tensor.value_load(ex.owner[0:1, bass.ds(t, 1)], min_val=0, max_val=ex.NE - 1)

                def x_transpose(t, r):
                    pe.wait_ge(s_ld[r], times16(t, r))
                    pe.wait_ge(s_xt, t + 1)
                    for k in range(KD):
                        last = nc.tensor.transpose(ps_x[:, k * 128:(k + 1) * 128],
                                                   xs[:, r, k * 128:(k + 1) * 128], pg.ident[:])
                    last.then_inc(s_a, 1)

                def fc1(t, r):
                    e = expert(t)
                    pe.wait_ge(s_xt, t + 2)
                    pe.wait_ge(s_h, t + 1)
                    for n in range(NB):
                        w = min(512, F)
                        for k in range(KD):
                            last = nc.tensor.matmul(ps_h[:, n, 0:w], xt[:, r, k, :],
                                                    ex.W1[:, bass.ds(e, 1), k, n * 512:n * 512 + w]
                                                    .rearrange("p o w -> p (o w)"),
                                                    start=(k == 0), stop=(k == KD - 1))
                    last.then_inc(s_b, 1)

                def h_transpose(t, r):
                    pe.wait_ge(s_h, t + 2)
                    pe.wait_ge(s_g, t + 1)
                    for k in range(FK):
                        last = nc.tensor.transpose(ps_t[:, k // 4, (k % 4) * 128:(k % 4) * 128 + 128],
                                                   hid[:, k * 128:(k + 1) * 128], pg.ident[:])
                    last.then_inc(s_c, 1)

                def fc2(t, r):
                    e = expert(t)
                    pe.wait_ge(s_g, t + 2)
                    pe.wait_ge(s_y, t + 1)
                    for k in range(FK):
                        last = nc.tensor.matmul(ps_y, ht[:, r, k, :], ex.W2[:, bass.ds(e, 1), k, :]
                                                .rearrange("p o w -> p (o w)"),
                                                start=(k == 0), stop=(k == FK - 1))
                    last.then_inc(s_d, 1)

                def body(t, r):
                    fc1(t + 1, (r + 1) % R)
                    h_transpose(t, r)
                    x_transpose(t + 2, r)
                    fc2(t - 1, (r + 1) % R)

                x_transpose(0, 0)
                fc1(0, 0)
                x_transpose(1, 1)
                fc1(1, 1)
                h_transpose(0, 0)
                x_transpose(2, 0)
                rolled(pe, 1, T - 2, R, body)
                t = T - 2
                fc1(t + 1, (t + 1) % R)
                h_transpose(t, t % R)
                fc2(t - 1, (t - 1) % R)
                h_transpose(t + 1, (t + 1) % R)
                fc2(t, t % R)
                fc2(t + 1, (t + 1) % R)

            @block.scalar
            def _(act):
                act.sem_inc(s_g, 1)

                def gelu(t, r):
                    e = nc.scalar.value_load(ex.owner[0:1, bass.ds(t, 1)], min_val=0, max_val=ex.NE - 1)
                    act.wait_ge(s_c, t + 1)
                    act.wait_ge(s_d, t + 1)
                    for k in range(FK):
                        last = nc.scalar.activation(
                            ht[:, r, k, :], ps_t[:, k // 4, (k % 4) * 128:(k % 4) * 128 + 128], ACT.Gelu,
                            bias=ex.b1[:, bass.ds(e, 1), k])
                    last.then_inc(s_g, 1)

                rolled(act, 0, T, R, gelu)

            @block.vector
            def _(dve):
                v = nc.vector
                if residual is not None:
                    step = Chain(dve, s_ch)
                    step(v.tensor_tensor(residual, residual, pg.XN[:], ALU.add))
                dve.sem_inc(s_xt, 1)
                dve.sem_inc(s_h, 1)
                dve.sem_inc(s_y, 1)
                dve.sem_inc(s_d, R)

                def x_copy(t, r):
                    dve.wait_ge(s_a, t + R + 1)
                    dve.wait_ge(s_b, t + 1)
                    v.tensor_copy(xt[:, r, :, :], ps_x.rearrange("p (k q) -> p k q", k=KD)).then_inc(s_xt, 1)

                def h_copy(t, r):
                    dve.wait_ge(s_b, t + R + 1)
                    dve.wait_ge(s_c, t)
                    for n in range(NB):
                        w = min(512, F)
                        last = v.tensor_copy(hid[:, n * 512:n * 512 + w], ps_h[:, n, 0:w])
                    last.then_inc(s_h, 1)

                def y_copy(t, r):
                    e = v.value_load(ex.owner[0:1, bass.ds(t, 1)], min_val=0, max_val=ex.NE - 1)
                    dve.wait_ge(s_d, t + R + 1)
                    s_st[r].wait(dve, stored16(t, r))
                    v.tensor_tensor(y[:, r, :], ps_y, ex.b2[:, bass.ds(e, 1), :].rearrange("p o d -> p (o d)"),
                                    ALU.add).then_inc(s_y, 1)

                def body(t, r):
                    h_copy(t + 1, (r + 1) % R)
                    x_copy(t + 2, r)
                    y_copy(t - 1, (r + 1) % R)

                dve.sem_inc(s_b, R)
                x_copy(0, 0)
                h_copy(0, 0)
                x_copy(1, 1)
                h_copy(1, 1)
                x_copy(2, 0)
                rolled(dve, 1, T - 2, R, body)
                t = T - 2
                h_copy(t + 1, (t + 1) % R)
                y_copy(t - 1, (t - 1) % R)
                y_copy(t, t % R)
                y_copy(t + 1, (t + 1) % R)



def stage_combine(pg, ex, out=None, x_kept=None):
    nc = pg.nc
    RG = 4
    with ExitStack() as ctx:
        sb = lambda n, s, d=fp32: pg.sb(f"{ex.tag}_{n}", s, d, ctx)
        sem = lambda n: pg.sem(f"{ex.tag}_{n}", ctx)
        g = sb("g", [P, RG, TOP, D])
        xk = sb("xk", [P, RG, TOP, D]) if out is not None else None
        s_g = pg.arrivals(RG, [32 * ((NT - r + RG - 1) // RG) for r in range(RG)])
        s_k = [sem(f"k{r}") for r in range(RG)]
        s_o = [sem(f"o{r}") for r in range(RG)]
        s_sum, s_tick, s_ch = sem("sum"), sem("ctick"), sem("cchain")
        with pg.block() as block:
            @block.gpsimd
            def _(pool):
                pg.clear_used(pool)
                for j in range(NT):
                    r = j % RG
                    if j >= RG:
                        pool.wait_ge(s_sum, j - RG + 1)
                    for c in range(TOP):
                        nc.gpsimd.indirect_dma_start(
                            g[:, r, c, :], None, ex.YS, bass.IndirectOffsetOnAxis(
                                ap=ex.slot_i[:, c * NT + j:c * NT + j + 1], axis=0)).then_inc(s_g[r].sem, 16)

            @block.sync
            def _(sp):
                if out is None:
                    return

                def store(j):
                    sp.wait_ge(s_sum, j + 1)
                    sp.dma_start(out[j * P:(j + 1) * P, :], xk[:, j % RG, 0, :]).then_inc(s_o[j % RG], 16)

                for j in range(NT):
                    r = j % RG
                    if j >= RG:
                        store(j - RG)
                        sp.wait_ge(s_o[r], 16 * (j // RG))
                    rows = slice(j * P, (j + 1) * P)
                    sp.dma_start(xk[:, r, 0, :], x_kept[rows, :]).then_inc(s_k[r], 16)
                    sp.dma_start(xk[:, r, 1, :], ex.YS[rows, :]).then_inc(s_k[r], 16)
                for j in range(NT - RG, NT):
                    store(j)
                for r in range(RG):
                    sp.wait_ge(s_o[r], 16 * ((NT - r + RG - 1) // RG))

            @block.vector
            def _(dve):
                v = nc.vector
                step = Chain(dve, s_ch)
                for j in range(NT):
                    r = j % RG
                    a = pg.X[:, j, :] if out is None else xk[:, r, 0, :]
                    if out is not None:
                        dve.wait_ge(s_k[r], 32 * (j // RG + 1))
                        step(v.tensor_tensor(a, a, xk[:, r, 1, :], ALU.add))
                    s_g[r].wait(dve, 32 * (j // RG + 1))
                    step(v.scalar_tensor_tensor(a, g[:, r, 0, :], ex.gate[:, 0, j:j + 1], a, ALU.mult, ALU.add))
                    v.scalar_tensor_tensor(a, g[:, r, 1, :], ex.gate[:, 1, j:j + 1], a,
                                           ALU.mult, ALU.add).then_inc(s_sum, 1)


class Dense:

    def __init__(self, pg, ctx, tag):
        self.pg = pg
        sb = lambda n, s, d=fp32: pg.sb(f"{tag}_{n}", s, d, ctx)
        sem = lambda n: pg.sem(f"{tag}_{n}", ctx)
        self.st = sb("st", [128, KD, len(CHUNKS), 6])
        self.mv = sb("mv", [128, KD, 2])
        self.std, self.tmp = sb("std", [128, KD]), sb("tmp", [128, KD])
        self.scale, self.shift = sb("scale", [128, 2, KD]), sb("shift", [128, 2, KD])
        self.ring, self.rows = sb("t_ring", [128, U, KD, P]), sb("rows2", [P, U, D])
        self.s_mm, self.s_ev, self.s_bn, self.s_ch, self.s_var, self.s_std, self.s_aff, self.s_relu = (
            sem(n) for n in ("mm", "ev", "bn", "chain", "var", "std", "aff", "relu"))
        self.s_ring, self.s_kept, self.s_tr, self.s_row = (sem(n) for n in ("ringed", "kept", "trd", "row"))
        self.s_st = [sem(f"st{s}") for s in range(U)]
        self.G = KD * len(CHUNKS)

    def product(self, pe, which, weight, src):
        nc, ps = self.pg.nc, self.pg.ps
        for c, (s0, n) in enumerate(CHUNKS):
            if which:
                pe.wait_ge(self.s_relu, KD * (c + 1))
            for fo in range(KD):
                g = which * self.G + c * KD + fo
                if g >= BANKS:
                    pe.wait_ge(self.s_ev, g - BANKS + 1)
                for k in range(KD):
                    last = nc.tensor.matmul(ps[:, g % BANKS, 0:n], weight[:, k, fo * 128:(fo + 1) * 128],
                                            src[:, k, s0:s0 + n], start=(k == 0), stop=(k == KD - 1))
                last.then_inc(self.s_mm, 1)

    def evacuate(self, act, which, dst, bias):
        nc, ps = self.pg.nc, self.pg.ps
        for c, (s0, n) in enumerate(CHUNKS):
            for fo in range(KD):
                g = which * self.G + c * KD + fo
                act.wait_ge(self.s_mm, g + 1)
                nc.scalar.activation(dst[:, fo, s0:s0 + n], ps[:, g % BANKS, 0:n], ACT.Identity,
                                     bias=bias[:, fo:fo + 1]).then_inc(self.s_ev, 1)

    def statistics(self, dve, step, which, src, gamma, beta):
        v = self.pg.nc.vector
        for c, (s0, n) in enumerate(CHUNKS):
            for fo in range(KD):
                g = which * self.G + c * KD + fo
                dve.wait_ge(self.s_ev, g + 1)
                v.bn_stats(self.st[:, fo, c, :], src[:, fo, s0:s0 + n]).then_inc(self.s_bn, 1)
        dve.wait_ge(self.s_bn, (which + 1) * self.G)
        for fo in range(KD):
            step(v.bn_aggr(self.mv[:, fo, :], self.st[:, fo, :, :].rearrange("p c s -> p (c s)")))
        v.tensor_scalar(self.std[:], self.mv[:, :, 1], BN_EPS, None, ALU.add).then_inc(self.s_var, 1)
        dve.wait_ge(self.s_std, which + 1)
        scale, shift = self.scale[:, which, :], self.shift[:, which, :]
        step(v.reciprocal(self.std[:], self.std[:]))
        step(v.tensor_tensor(scale, self.std[:], gamma, ALU.mult))
        step(v.tensor_tensor(self.tmp[:], self.mv[:, :, 0], scale, ALU.mult))
        v.tensor_tensor(shift, beta, self.tmp[:], ALU.subtract).then_inc(self.s_aff, 1)

    def root(self, act, which):
        act.wait_ge(self.s_var, which + 1)
        self.pg.nc.scalar.activation(self.std[:], self.std[:], ACT.Sqrt).then_inc(self.s_std, 1)

    def relu(self, act, which, a):
        act.wait_ge(self.s_aff, which + 1)
        for s0, n in CHUNKS:
            for fo in range(KD):
                self.pg.nc.scalar.activation(
                    a[:, fo, s0:s0 + n], a[:, fo, s0:s0 + n], ACT.Relu,
                    bias=self.shift[:, which, fo:fo + 1],
                    scale=self.scale[:, which, fo:fo + 1]).then_inc(self.s_relu, 1)

    def ring_fill(self, act, src, which):
        nc = self.pg.nc
        if which is not None:
            act.wait_ge(self.s_aff, which + 1)
        with act.Fori(0, NT // U) as i:
            for s in range(U):
                j = i * U + s
                act.wait_ge(self.s_tr, i * U + U)
                act.wait_ge(self.s_kept, i * U + U)
                for k in range(KD):
                    a = src[:, k, bass.ds(j * P, P)]
                    if which is None:
                        last = nc.scalar.copy(self.ring[:, s, k, :], a)
                    else:
                        last = nc.scalar.activation(self.ring[:, s, k, :], a, ACT.Relu,
                                                    bias=self.shift[:, which, k:k + 1],
                                                    scale=self.scale[:, which, k:k + 1])
                last.then_inc(self.s_ring, 1)

    def ring_keep(self, pool, dst):
        pool.sem_inc(self.s_kept, U)
        with pool.Fori(0, NT // U) as i:
            for s in range(U):
                j = i * U + s
                pool.wait_ge(self.s_ring, j + 1)
                self.pg.nc.gpsimd.tensor_copy(dst[:, :, bass.ds(j * P, P)], self.ring[:, s, :, :]).then_inc(self.s_kept, 1)

    def ring_transpose(self, pe):
        nc, ps = self.pg.nc, self.pg.ps
        pe.sem_inc(self.s_tr, U)
        with pe.Fori(0, NT // U) as i:
            for s in range(U):
                j = i * U + s
                pe.wait_ge(self.s_ring, j + 1)
                pe.wait_ge(self.s_row, i * U + U)
                for k in range(KD):
                    last = nc.tensor.transpose(ps[0:P, s, k * 128:(k + 1) * 128], self.ring[:, s, k, :],
                                               self.pg.ident[:])
                last.then_inc(self.s_tr, 1)

    def rows_out(self, dve):
        v, ps = self.pg.nc.vector, self.pg.ps
        dve.sem_inc(self.s_row, U)
        with dve.Fori(0, NT // U) as i:
            for s in range(U):
                j = i * U + s
                dve.wait_ge(self.s_tr, U + 1 + j)
                dve.wait_ge(self.s_st[s], i * 16 + 16)
                v.tensor_copy(self.rows[:, s, :], ps[0:P, s, 0:D]).then_inc(self.s_row, 1)

    def rows_store(self, sp):
        for s in range(U):
            sp.sem_inc(self.s_st[s], 16)
        with sp.Fori(0, NT // U) as i:
            for s in range(U):
                j = i * U + s
                sp.wait_ge(self.s_row, U + 1 + j)
                sp.dma_start(self.pg.H[bass.ds(j * P, P), :], self.rows[:, s, :]).then_inc(self.s_st[s], 16)
        for s in range(U):
            sp.wait_ge(self.s_st[s], 16 * (NT // U) + 16)

    def rows_add(self, dve, X):
        v, ps = self.pg.nc.vector, self.pg.ps
        dve.sem_inc(self.s_row, U)
        with dve.Fori(0, NT // U) as i:
            for s in range(U):
                j = i * U + s
                dve.wait_ge(self.s_tr, U + 1 + j)
                x = X[:, bass.ds(j, 1), :]
                v.tensor_tensor(x, x, ps[0:P, s:s + 1, 0:D], ALU.add).then_inc(self.s_row, 1)


def stage_network(pg, w_in, b_in, w1, b1, g1, be1, w2, b2, g_out, b_out):
    nc = pg.nc
    L = w1.shape[0]
    with ExitStack() as ctx:
        hf, z1 = (pg.sb(n, [128, KD, N], ctx=ctx) for n in ("h_features", "z1"))
        room = pg.sb("z2_or_xn", [128, NT * D], ctx=ctx)
        z2 = room[:, 0:KD * N].rearrange("p (k n) -> p k n", k=KD)
        pg.XN = room[0:P, :].rearrange("p (j d) -> p j d", j=NT)
        W = pg.sb("gnn_w", [128, 1 + 2 * L, KD, D], ctx=ctx)
        names = ("b1", "g1", "be1", "b2", "g_out", "b_out")
        par = {n: pg.sb(f"gnn_{n}", [128, L, KD], ctx=ctx) for n in names}
        bi = pg.sb("gnn_b_in", [128, KD], ctx=ctx)
        s_w = pg.sem("gnn_weights")
        loads = 16 * (1 + 2 * L + len(names) + 1)

        with ExitStack() as c:
            norm = Norm(pg, c, "ln2", "features", features=hf)
            d = Dense(pg, c, "in")
            with pg.block() as block:
                @block.sync
                def _(sp):
                    load_weight_chunks(sp, W[:, 0, :, :], w_in, s_w)
                    c.enter_context(nc.allow_non_contiguous_dma(reason="vectors, one value a partition"))
                    sp.dma_start(bi[:], b_in.rearrange("(k p) -> p k", p=128)).then_inc(s_w, 16)
                    for layer in range(L):
                        load_weight_chunks(sp, W[:, 1 + 2 * layer, :, :], w1[layer], s_w)
                        load_weight_chunks(sp, W[:, 2 + 2 * layer, :, :], w2[layer], s_w)
                    for n, a in zip(names, (b1, g1, be1, b2, g_out, b_out)):
                        sp.dma_start(par[n][:], a.rearrange("l (k p) -> p l k", p=128)).then_inc(s_w, 16)
                    d.rows_store(sp)

                @block.gpsimd
                def _(pool):
                    pg.clear_used(pool)
                    d.ring_keep(pool, z1)

                @block.tensor
                def _(pe):
                    norm.tensor(pe)
                    pe.wait_ge(s_w, loads)
                    pe.wait_ge(norm.s_xt, NT + U)
                    d.product(pe, 0, W[:, 0, :, :], hf)
                    d.ring_transpose(pe)

                @block.scalar
                def _(act):
                    norm.scalar(act)
                    act.wait_ge(s_w, loads)
                    d.evacuate(act, 0, z2, bi)
                    act.wait_ge(d.s_ev, d.G)
                    d.ring_fill(act, z2, None)

                @block.vector
                def _(dve):
                    norm.vector(dve)
                    d.rows_out(dve)
        h, spare = z1, hf
        for layer in range(L):
            stage_aggregate_features(pg, f"agg{layer + 1}", h, room)
            with ExitStack() as c:
                d = Dense(pg, c, f"layer{layer}")
                p = {n: par[n][:, layer, :] for n in names}
                final = layer == L - 1
                with pg.block() as block:
                    @block.tensor
                    def _(pe):
                        d.product(pe, 0, W[:, 1 + 2 * layer, :, :], h)
                        d.product(pe, 1, W[:, 2 + 2 * layer, :, :], spare)
                        d.ring_transpose(pe)

                    @block.scalar
                    def _(act):
                        d.evacuate(act, 0, spare, p["b1"])
                        d.root(act, 0)
                        d.relu(act, 0, spare)
                        d.evacuate(act, 1, z2, p["b2"])
                        d.root(act, 1)
                        d.ring_fill(act, z2, 1)

                    @block.vector
                    def _(dve):
                        step = Chain(dve, d.s_ch)
                        d.statistics(dve, step, 0, spare, p["g1"], p["be1"])
                        d.statistics(dve, step, 1, z2, p["g_out"], p["b_out"])
                        if final:
                            d.rows_add(dve, pg.X)
                        else:
                            d.rows_out(dve)

                    @block.gpsimd
                    def _(pool):
                        pg.clear_used(pool)
                        if final:
                            pool.sem_inc(d.s_kept, NT + U)
                        else:
                            d.ring_keep(pool, h)

                    @block.sync
                    def _(sp):
                        if not final:
                            d.rows_store(sp)


def run_mixture(pg, ex, load):
    stage_route(pg, ex, load=load)
    stage_experts(pg, ex, residual=pg.X[:])
    stage_combine(pg, ex)


def build(nc, x, src, dst, edge_weight, L0_gnn_W, L0_gnn_bias, L0_ffn_router_w, L0_ffn_w1, L0_ffn_b1,
          L0_ffn_w2, L0_ffn_b2, L1_gnn_W_in, L1_gnn_b_in, L1_gnn_W1, L1_gnn_b1, L1_gnn_g1, L1_gnn_be1,
          L1_gnn_W2, L1_gnn_b2, L1_gnn_g_out, L1_gnn_b_out, L1_ffn_Wr, L1_ffn_W1s, L1_ffn_b1s,
          L1_ffn_W2s, L1_ffn_b2s, L1_ffn_W1p, L1_ffn_b1p, L1_ffn_W2p, L1_ffn_b2p, out):
    with ExitStack() as ctx:
        pg = Program(nc, ctx)
        pg.ps = ctx.enter_context(nc.psum_tensor("ps", [128, 8, 512], fp32))
        pg.X = pg.sb("X", [P, NT, D])
        pg.col = pg.sb("col", [128, 128])
        pg.part = pg.sb("part", [128, 1])
        pg.tiles = pg.sb("tiles", [1, EDGE_PAD])
        pg.ident = pg.sb("ident", [128, 128])
        pg.tri = pg.sb("tri", [128, 128])
        pg.ones = pg.sb("ones", [128, 128])
        pg.prio = pg.sb("prio", [P, NX])
        pg.H = nc.dram_tensor("h_rows", [N, D], fp32).ap()
        pg.pay_dram = nc.dram_tensor("payloads", [128 * EDGE_PAD, 4], fp32).ap()
        pg.XS0 = nc.dram_tensor("expert_rows0", [MOE_TILES * SLOT, D], fp32).ap()
        pg.YS0 = nc.dram_tensor("expert_out0", [MOE_TILES * SLOT, D], fp32).ap()
        pg.x_kept = nc.dram_tensor("x_kept", [N, D], fp32).ap()
        ST = SHARED_TILES + MOE_TILES
        pg.XS1 = nc.dram_tensor("expert_rows1", [ST * SLOT, D], fp32).ap()
        pg.YS1 = nc.dram_tensor("expert_out1", [ST * SLOT, D], fp32).ap()

        edges = ctx.enter_context(ExitStack())
        pg.slots = pg.sb("slots", [128, EDGE_PAD, 4], ctx=edges)
        pg.owner_t = pg.sb("owner_t", [1, EDGE_PAD], int32, ctx=edges)
        pg.owner_n = pg.sb("owner_n", [1, EDGE_PAD], int32, ctx=edges)
        pg.owner_h = pg.sb("owner_h", [1, EDGE_PAD], int32, ctx=edges)
        pg.lists = pg.sb("lists", [1, 3], int32, ctx=edges)
        pg.hot_col = pg.sb("hot_col", [128, HOT * P], ctx=edges)
        stage_prepare(pg, x, src, dst, edge_weight, L0_gnn_W, L0_gnn_bias)
        pg.A = pg.sb("A_hot", [P, HOT, N], ctx=edges)
        stage_aggregate_nodes(pg)
        with ExitStack() as c1:
            pg.XN = pg.sb("XN1", [P, NT, D], ctx=c1)
            ex = Experts(pg, c1, "moe0", D, 0, pg.XS0, pg.YS0)

            def load0(eng):
                ex.load_weights(eng, lambda k: L0_ffn_router_w.rearrange("e (k p) -> k p e", p=128)[k],
                                L0_ffn_w1, L0_ffn_b1, L0_ffn_w2, L0_ffn_b2)
            run_mixture(pg, ex, load0)
        stage_network(pg, L1_gnn_W_in, L1_gnn_b_in, L1_gnn_W1, L1_gnn_b1, L1_gnn_g1, L1_gnn_be1,
                      L1_gnn_W2, L1_gnn_b2, L1_gnn_g_out, L1_gnn_b_out)
        edges.close()
        with ExitStack() as c1:
            pg.XN = pg.X
            ex = Experts(pg, c1, "moe1", L1_ffn_W1s.shape[1], SHARED_TILES, pg.XS1, pg.YS1)

            def load1(eng):
                ex.load_weights(eng, lambda k: L1_ffn_Wr[k * 128:(k + 1) * 128, :],
                                L1_ffn_W1p, L1_ffn_b1p, L1_ffn_W2p, L1_ffn_b2p,
                                (L1_ffn_W1s, L1_ffn_b1s, L1_ffn_W2s, L1_ffn_b2s))
            stage_route(pg, ex, keep_x=pg.x_kept, load=load1)
            stage_experts(pg, ex)
            stage_combine(pg, ex, out=out, x_kept=pg.x_kept)


_INS = ['x', 'src', 'dst', 'edge_weight', 'L0_gnn_W', 'L0_gnn_bias', 'L0_ffn_router_w', 'L0_ffn_w1',
        'L0_ffn_b1', 'L0_ffn_w2', 'L0_ffn_b2', 'L1_gnn_W_in', 'L1_gnn_b_in', 'L1_gnn_W1', 'L1_gnn_b1',
        'L1_gnn_g1', 'L1_gnn_be1', 'L1_gnn_W2', 'L1_gnn_b2', 'L1_gnn_g_out', 'L1_gnn_b_out',
        'L1_ffn_Wr', 'L1_ffn_W1s', 'L1_ffn_b1s', 'L1_ffn_W2s', 'L1_ffn_b2s', 'L1_ffn_W1p',
        'L1_ffn_b1p', 'L1_ffn_W2p', 'L1_ffn_b2p']
_OUTS = [((N, D), 'float32')]


def kernel(**inputs):
    import numpy as _np
    import concourse.bacc as _bacc
    from concourse import mybir as _mybir
    from concourse.bass_utils import run_bass_kernel_spmd as _run

    nc = _bacc.Bacc("TRN2", target_bir_lowering=False, num_devices=1)
    arrays, args = {}, []
    for name in _INS:
        a = _np.ascontiguousarray(inputs[name])
        arrays[f"in_{name}_dram"] = a
        args.append(nc.dram_tensor(f"in_{name}_dram", a.shape, _mybir.dt.from_np(a.dtype), kind="ExternalInput").ap())
    for i, (shape, dtype) in enumerate(_OUTS):
        dt = _mybir.dt.from_np(_np.dtype(dtype))
        args.append(nc.dram_tensor(f"out_{i}_dram", shape, dt, kind="ExternalOutput").ap())
    build(nc, *args)
    r = _run(nc, [arrays], core_ids=[0])
    got = tuple(r.results[0][f"out_{i}_dram"] for i in range(len(_OUTS)))
    return got[0]
```

```python
import concourse.bass as bass
from concourse import mybir
from contextlib import ExitStack, contextmanager

fp32 = mybir.dt.float32
fp16 = mybir.dt.float16
fp32r = mybir.dt.float32r
int32 = mybir.dt.int32
ALU = mybir.AluOpType
ACT = mybir.ActivationFunctionType
AXIS = mybir.AxisListType

N = 3125
D = 256
P = 125
NT = N // P
KD = D // 128
E = 50000
EJ = E // P
TOP = 2
NX = 8
SLOT = 128
ROUND = 16
HOT = 4
QUAD = 4
HR = 3 * QUAD
EB = 2 * NT
COLD_TILES = (E + NT * (SLOT - 1)) // SLOT
HOT_TILES = (E + NT * (QUAD * SLOT - 1)) // SLOT
EDGE_TILES = (E + NT * ((QUAD + 1) * SLOT - 2)) // SLOT + ROUND - 1
EDGE_PAD = -(-(EDGE_TILES + 2 * HR) // ROUND) * ROUND
COLD_ROUNDS, HOT_ROUNDS = -(-COLD_TILES // ROUND), -(-HOT_TILES // HR)
FIRST, COLD, HOTTER, BOTH, ANY = range(5)
SORTED = ((0, 80), (80, 240), (240, 400))
SCATTERED = 256
PERMUTED = EJ - SCATTERED
PR = 4
BANKS = 8
MOE_TILES = (TOP * N + NX * (SLOT - 1)) // SLOT
SHARED_TILES = -(-N // SLOT)
SHARED_LEAD = 13
LN_EPS = 1e-5
BN_EPS = 1e-5
U = 5
CH = 500
CHUNKS = [(s, min(CH, N - s)) for s in range(0, N, CH)]


class Program:

    def __init__(self, nc, ctx):
        self.nc, self.ctx = nc, ctx
        self.own_sems, self.used_sems = [], []
        self.pool_sems = [self.sem(f"arrived{k}") for k in range(ROUND)]
        self.pool_count = [0] * ROUND

    def sb(self, name, shape, dt=fp32, ctx=None):
        return (ctx or self.ctx).enter_context(self.nc.sbuf_tensor(name, shape, dt))

    def arrivals(self, n, total):
        taken = [Arrival(self.pool_sems[k], self.pool_count[k]) for k in range(n)]
        for k in range(n):
            self.pool_count[k] += total[k] if isinstance(total, list) else total
        return taken

    def sem(self, name, ctx=None):
        handle = (ctx or self.ctx).enter_context(self.nc.semaphore(name))
        if ctx is not None:
            self.own_sems.append(handle.num)
        return handle

    def tiles_at(self, first, n):
        first = self.nc.s_assert_within(first, 0, EDGE_PAD - n, skip_runtime_bounds_check_because=(
            "a list's rounds, and the half round behind them, lie inside the tables for any inputs"))
        return bass.ds(first, n)

    @contextmanager
    def block(self):
        with self.nc.Block() as block:
            yield block
        self.used_sems, self.own_sems = self.own_sems, []

    def clear_used(self, pool):
        nums, self.used_sems = sorted(self.used_sems), []
        while nums:
            n = next((k for k in range(1, len(nums)) if nums[k] != nums[0] + k), len(nums))
            pool.sem_clear(range(nums[0], nums[0] + n))
            nums = nums[n:]


class Arrival:

    def __init__(self, sem, base):
        self.sem, self.base = sem, base

    def wait(self, eng, value):
        eng.wait_ge(self.sem, value + self.base)


class Chain:

    def __init__(self, eng, sem):
        self.eng, self.sem, self.n = eng, sem, 0

    def __call__(self, ins):
        self.n += 1
        ins.then_inc(self.sem, 1)
        self.eng.wait_ge(self.sem, self.n)


def load_weight_chunks(eng, dst, src, sem):
    eng.dma_start(dst, src.rearrange("(k p) m -> p k m", p=128)).then_inc(sem, 16)


def bucket_bases(nc, step, dve, oh, cum, J, B, buf, tot_ready, tot_done, split=None):
    flat = "p b j -> p (b j)"
    step(nc.vector.tensor_tensor_scan(cum.rearrange(flat), oh.rearrange(flat), oh.rearrange(flat),
                                      0.0, ALU.add, ALU.max))
    last = cum[:, :, J - 1]
    before, total = buf["before"], buf["total"]
    step(nc.vector.memset(before[:, 0:1], 0.0))
    step(nc.vector.tensor_copy(before[:, 1:B], last[:, 0:B - 1]))
    nc.vector.tensor_tensor(total[:, 0:B], last, before[:, 0:B], ALU.subtract).then_inc(tot_ready, 1)
    dve.wait_ge(tot_done, 1)
    ti, tf, start, base = buf["ti"], buf["tf"], buf["start"], buf["base"]
    step(nc.vector.tensor_scalar(ti[:, 0:B], buf["ps_all"], float(SLOT - 1), None, ALU.add))
    if split:
        step(nc.vector.tensor_scalar(ti[:, split[0]:B], buf["ps_all"][:, split[0]:B],
                                     float(QUAD * SLOT - 1), None, ALU.add))
    step(nc.vector.tensor_scalar(ti[:, 0:B], ti[:, 0:B], 7, None, ALU.arith_shift_right))
    if split:
        step(nc.vector.tensor_scalar(ti[:, split[0]:B], ti[:, split[0]:B], -QUAD, None, ALU.bitwise_and))
    step(nc.vector.tensor_copy(tf[:, 1:B + 1], ti[:, 0:B]))
    step(nc.vector.memset(tf[:, 0:1], 0.0))
    step(nc.vector.memset(buf["zero"][:, 0:B + 1], 0.0))
    step(nc.vector.tensor_tensor_scan(start[:, 0:B + 1], tf[:, 0:B + 1], buf["zero"][:, 0:B + 1], 0.0,
                                      ALU.add, ALU.add))
    if split:
        b, n = split
        up = ti[:, 0:1]
        step(nc.vector.tensor_scalar(up, start[:, b:b + 1], float(n - 1), None, ALU.add))
        step(nc.vector.tensor_scalar(up, up, -n, None, ALU.bitwise_and))
        step(nc.vector.tensor_copy(tf[:, 0:1], up))
        step(nc.vector.tensor_tensor(tf[:, 0:1], tf[:, 0:1], start[:, b:b + 1], ALU.subtract))
        step(nc.vector.tensor_scalar(start[:, b:B + 1], start[:, b:B + 1], tf[:, 0:1], None, ALU.add))
    step(nc.vector.tensor_scalar(base[:, 0:B], start[0:P, 0:B], float(SLOT), -1.0, ALU.mult, ALU.add))
    step(nc.vector.tensor_tensor(base[:, 0:B], base[:, 0:B], before[:, 0:B], ALU.subtract))
    step(nc.vector.tensor_tensor(base[:, 0:B], base[:, 0:B], buf["ps_pre"], ALU.add))


def bucket_slots(nc, step, dve, oh, cum, J, B, buf, tot_ready, tot_done, slots):
    bucket_bases(nc, step, dve, oh, cum, J, B, buf, tot_ready, tot_done)
    base = buf["base"]
    step(nc.vector.tensor_tensor(cum, cum, base[:, 0:B].unsqueeze(2).to_broadcast([P, B, J]), ALU.add))
    step(nc.vector.tensor_tensor(cum, cum, oh, ALU.mult))
    step(nc.vector.tensor_reduce(slots, cum.rearrange("p b j -> p j b"), AXIS.X, ALU.add))


def slot_buffers(pg, ctx, tag, B):
    sb = lambda n, s, d=fp32: pg.sb(f"{tag}_{n}", s, d, ctx)
    return {"before": sb("before", [P, B]), "total": sb("total", [P, B]),
            "ti": sb("ti", [128, B], int32), "tf": sb("tf", [128, B + 1]), "zero": sb("zero", [128, B + 1]),
            "start": sb("start", [128, B + 1]), "base": sb("base", [P, B]),
            "ps_all": pg.ps[:, 7, 0:B], "ps_pre": pg.ps[0:P, 7, 64:64 + B]}


def bucket_totals(nc, pe, pg, buf, B, tot_ready, tot_done):
    pe.wait_ge(tot_ready, 1)
    nc.tensor.matmul(buf["ps_all"], pg.ones[0:P, :], buf["total"][:, 0:B], start=True, stop=True)
    nc.tensor.matmul(buf["ps_pre"], pg.tri[0:P, 0:P], buf["total"][:, 0:B],
                     start=True, stop=True).then_inc(tot_done, 1)


def owner_table(nc, step, row_t, start, B, count, acc):
    step(nc.vector.memset(acc, 0.0))
    for b in range(1, B):
        step(nc.vector.scalar_tensor_tensor(acc, row_t[0:1, 0:count], start[0:1, b:b + 1], acc,
                                            ALU.is_ge, ALU.add))


def row_stats(pg, dve, j, done):
    for i in ([j - 1] if j else []) + ([j] if j == NT - 1 else []):
        dve.wait_ge(done, i + 1)
        pg.nc.vector.bn_stats(pg.stats[:, i, :], pg.X[:, i, :])


class Norm:
    T_BANKS, M_BANKS = 4, 3
    LAG = 3

    def __init__(self, pg, ctx, tag, use, weight=None, dram=None, features=None, logits=None,
                 room=None):
        self.pg, self.use, self.weight, self.dram = pg, use, weight, dram
        self.features, self.logits = features, logits
        sb = lambda n, s, d=fp32: pg.sb(f"{tag}_{n}", s, d, ctx)
        sem = lambda n: pg.sem(f"{tag}_{n}", ctx)
        self.mean, self.var = sb("mean", [P, NT]), sb("var", [P, NT])
        self.dif, self.rstd = sb("dif", [P, NT]), sb("rstd", [P, NT])
        rows, xt = U * D * (use == "rows"), U * KD * P * (use != "features")
        if room is None and rows + xt:
            room = sb("rings", [128, rows + xt])
        if rows:
            self.rows = room[0:P, 0:rows].rearrange("p (u d) -> p u d", u=U)
            self.s_st = [sem(f"stored{s}") for s in range(U)]
        if xt:
            self.xt = room[:, rows:rows + xt].rearrange("p (u k q) -> p u k q", u=U, k=KD)
        self.s_stat, self.s_var, self.s_std = sem("stat"), sem("var"), sem("std")
        self.s_xn, self.s_tr, self.s_xt = sem("xn"), sem("tr"), sem("xt")
        self.s_mm, self.s_out, self.s_ch = sem("mm"), sem("out"), sem("chain")

    def vector(self, dve, x_ready=None, x_free=None):
        nc, pg = self.pg.nc, self.pg
        step = Chain(dve, self.s_ch)
        if x_ready is not None:
            dve.wait_ge(*x_ready)
            for j in range(NT):
                nc.vector.bn_stats(pg.stats[:, j, :], pg.X[:, j, :]).then_inc(self.s_stat, 1)
            dve.wait_ge(self.s_stat, NT)
        st = pg.stats
        step(nc.vector.tensor_tensor(self.dif[:], st[:, :, 1], st[:, :, 4], ALU.subtract))
        step(nc.vector.tensor_tensor(self.mean[:], st[:, :, 1], st[:, :, 4], ALU.add))
        step(nc.vector.tensor_scalar(self.mean[:], self.mean[:], 0.5, None, ALU.mult))
        step(nc.vector.tensor_tensor(self.var[:], st[:, :, 2], st[:, :, 5], ALU.add))
        step(nc.vector.tensor_scalar(self.var[:], self.var[:], 1.0 / D, LN_EPS, ALU.mult, ALU.add))
        step(nc.vector.tensor_tensor(self.dif[:], self.dif[:], self.dif[:], ALU.mult))
        nc.vector.scalar_tensor_tensor(self.var[:], self.dif[:], 0.25, self.var[:],
                                       ALU.mult, ALU.add).then_inc(self.s_var, 1)
        dve.wait_ge(self.s_std, 1)
        step(nc.vector.reciprocal(self.rstd[:], self.rstd[:]))
        if x_free is not None:
            dve.wait_ge(*x_free)
        for t in range(NT + self.LAG):
            if t < NT:
                nc.vector.tensor_scalar(pg.XN[:, t, :], pg.X[:, t, :], self.mean[:, t:t + 1],
                                        self.rstd[:, t:t + 1], ALU.subtract, ALU.mult).then_inc(self.s_xn, 1)
            j = t - self.LAG
            if j >= 0:
                dve.wait_ge(self.s_tr, j + 1)
                if self.use != "features" and j >= U:
                    dve.wait_ge(self.s_mm, j - U + 1)
                out = (self.features[:, :, j * P:(j + 1) * P] if self.use == "features"
                       else self.xt[:, j % U, :, :])
                nc.vector.tensor_copy(out, self.t_psum(j)).then_inc(self.s_xt, 1)
        if self.use == "router":
            dve.wait_ge(self.s_mm, NT)
            step(nc.vector.tensor_copy(self.logits[:].rearrange("p j e -> p (j e)"),
                                       pg.ps[0:P, self.T_BANKS, 0:NT * NX]))

    def t_psum(self, j):
        return self.pg.ps[:, j % self.T_BANKS, 0:256].rearrange("p (k q) -> p k q", k=KD)[:, :, 0:P]

    def m_psum(self, j):
        if self.use == "router":
            return self.pg.ps[0:P, self.T_BANKS, j * NX:(j + 1) * NX]
        return self.pg.ps[0:P, self.T_BANKS + j % self.M_BANKS, 0:D]

    def scalar(self, act):
        nc = self.pg.nc
        act.wait_ge(self.s_var, 1)
        nc.scalar.activation(self.rstd[:], self.var[:], ACT.Sqrt).then_inc(self.s_std, 1)
        if self.use != "rows":
            return
        for j in range(NT):
            act.wait_ge(self.s_mm, j + 1)
            if j >= U:
                act.wait_ge(self.s_st[j % U], j // U * 16)
            nc.scalar.copy(self.rows[:, j % U, :], self.m_psum(j)).then_inc(self.s_out, 1)
            act.wait_ge(self.s_out, j + 1)
            act.dma_start(self.dram[j * P:(j + 1) * P, :], self.rows[:, j % U, :]).then_inc(self.s_st[j % U], 16)
        for s in range(U):
            act.wait_ge(self.s_st[s], 16 * (NT // U))

    def tensor(self, pe, w_ready=None):
        nc, pg = self.pg.nc, self.pg
        if w_ready is not None:
            pe.wait_ge(*w_ready)

        def transposes(j):
            pe.wait_ge(self.s_xn, j + 1)
            if j >= self.T_BANKS:
                pe.wait_ge(self.s_xt, j - self.T_BANKS + 1)
            for k in range(KD):
                last = nc.tensor.transpose(pg.ps[:, j % self.T_BANKS, k * 128:k * 128 + P],
                                           pg.XN[:, j, k * 128:(k + 1) * 128], pg.ident[0:P, 0:P])
            last.then_inc(self.s_tr, 1)

        def product(j):
            pe.wait_ge(self.s_xt, j + 1)
            if self.use == "rows" and j >= self.M_BANKS:
                pe.wait_ge(self.s_out, j - self.M_BANKS + 1)
            for k in range(KD):
                last = nc.tensor.matmul(self.m_psum(j), self.xt[:, j % U, k, :], self.weight[:, k, :],
                                        start=(k == 0), stop=(k == KD - 1))
            last.then_inc(self.s_mm, 1)

        for j in range(NT):
            transposes(j)
            if self.use != "features" and j:
                product(j - 1)
        if self.use != "features":
            product(NT - 1)


class Permute:

    def __init__(self, pg, ctx, room):
        self.pg = pg
        taken = 0

        def part_of(rows, *shape, dt=fp32):
            nonlocal taken
            size = 1
            for d in shape:
                size *= d
            ap = room[0:rows, taken:taken + size]
            ap = ap if dt == fp32 else ap.bitcast(dt)
            taken += size
            assert taken <= room.shape[1]
            names = "abc"[:len(shape)]
            return ap.rearrange(f"p ({' '.join(names)}) -> p {' '.join(names)}", **dict(zip(names, shape)))

        sem = lambda n: pg.sem(f"perm_{n}", ctx)
        self.tile_row = pg.sb("tile_row", [P, EDGE_PAD], ctx=ctx)
        self.tile = pg.sb("perm_tile", [P, PR, EDGE_PAD], fp32r, ctx=ctx)
        self.place = part_of(P, PR, 128)
        self.weighted = pg.sb("perm_weighted", [P, PR, 4, 128], fp32r, ctx=ctx)
        self.high = part_of(P, 2, PERMUTED, dt=fp32r)
        self.parts = part_of(P, PERMUTED, 4)
        self.got = part_of(128, 2, EDGE_PAD)
        self.got_i = part_of(128, 2, EDGE_PAD, dt=int32)
        self.s_place, self.s_tile, self.s_weighted, self.s_mm = (
            sem(n) for n in ("places", "tiles", "weighted", "mm"))
        self.ps = pg.ps[:, 0:4, 0:EDGE_PAD // 2].rearrange("p (v h) c -> p v h c", v=2)

    def prepare(self, step, pay, first):
        v = self.pg.nc.vector
        c = slice(first, first + PERMUTED)
        parts, high = self.parts, self.high
        step(v.tensor_copy(parts[:, :, 0], pay[:, c, 1]))
        step(v.scalar_tensor_tensor(parts[:, :, 2], pay[:, c, 2], 128.0, pay[:, c, 0], ALU.mult, ALU.add))
        for x in range(2):
            step(v.tensor_copy(high[:, x, :], parts[:, :, 2 * x]))
            step(v.tensor_tensor(parts[:, :, 2 * x + 1], parts[:, :, 2 * x], high[:, x, :].bitcast(fp32),
                                 ALU.subtract))
            step(v.tensor_copy(parts[:, :, 2 * x], high[:, x, :].bitcast(fp32)))

    def vector(self, dve, step, tile, place, first):
        v, pg = self.pg.nc.vector, self.pg
        dve.sem_inc(self.s_place, 1)
        with dve.Fori(0, PERMUTED // PR) as i:
            for u in range(PR):
                c = bass.ds(i * PR + (first + u), 1)
                dve.wait_ge(self.s_mm, i * PR + (u + 1))
                v.tensor_scalar(self.place[:, u, :], pg.col[0:P, :], place[:, c], None,
                                ALU.is_equal).then_inc(self.s_place, 1)
                v.tensor_scalar(self.tile[:, u, :], self.tile_row[:], tile[:, c], None, ALU.is_equal)
                v.tensor_scalar(self.weighted[:, u, 0, :], pg.col[0:P, :], place[:, c],
                                self.parts[:, bass.ds(i * PR + u, 1), 0], ALU.is_equal, ALU.mult
                                ).then_inc(self.s_tile, 1)
        dve.wait_ge(self.s_mm, PERMUTED + PR)
        step(v.tensor_copy(self.got.rearrange("p v (h c) -> p v h c", h=2), self.ps))

    def scalar(self, act):
        long = 4 * PR
        with act.Fori(0, PERMUTED // long) as i:
            for c in range(long):
                u = c % PR
                act.wait_ge(self.s_place, i * long + (c + 2))
                for x in range(1, 4):
                    last = self.pg.nc.scalar.activation(self.weighted[:, u, x, :], self.place[:, u, :], ACT.Copy,
                                                        scale=self.parts[:, bass.ds(i * long + c, 1), x])
                last.then_inc(self.s_weighted, 1)

    def tensor(self, pe):
        nc = self.pg.nc
        pe.sem_inc(self.s_mm, PR)

        def column(c, u, first=False, end=False):
            pe.wait_ge(self.s_weighted, c + 1)
            pe.wait_ge(self.s_tile, c + 1)
            for x in range(4):
                for h in range(2):
                    last = nc.tensor.matmul(
                        self.ps[:, x // 2, h, :], self.weighted[:, u, x, :],
                        self.tile[:, u, h * (EDGE_PAD // 2):(h + 1) * (EDGE_PAD // 2)],
                        start=first and x % 2 == 0, stop=end and x % 2 == 1)
            last.then_inc(self.s_mm, 1)

        for u in range(PR):
            column(u, u, first=u == 0)
        with pe.Fori(0, PERMUTED // PR - 2) as i:
            for u in range(PR):
                column(i * PR + (PR + u), u)
        for u in range(PR):
            column(PERMUTED - PR + u, u, end=u == PR - 1)

    def merge(self, step):
        v, slots, got, got_i = self.pg.nc.vector, self.pg.slots, self.got, self.got_i
        step(v.tensor_tensor(slots[:, :, 1], slots[:, :, 1], got[:, 0, :], ALU.add))
        step(v.tensor_copy(got_i[:, 0, :], got[:, 1, :]))
        step(v.tensor_scalar(got_i[:, 1, :], got_i[:, 0, :], 7, None, ALU.arith_shift_right))
        step(v.tensor_scalar(got_i[:, 0, :], got_i[:, 0, :], 127, None, ALU.bitwise_and))
        step(v.tensor_tensor(slots[:, :, 2], slots[:, :, 2], got_i[:, 1, :], ALU.add))
        step(v.tensor_tensor(slots[:, :, 0], slots[:, :, 0], got_i[:, 0, :], ALU.add))


def stage_prepare(pg, x, src, dst, edge_weight, w_l0, bias_l0):
    nc = pg.nc
    with ExitStack() as ctx:
        sb = lambda n, s, d=fp32: pg.sb(n, s, d, ctx)
        sem = lambda n: pg.sem(n, ctx)
        src_i, dst_i = sb("src_i", [P, EJ], int32), sb("dst_i", [P, EJ], int32)
        src_f, blk = sb("src_f", [P, EJ]), sb("blk", [P, EJ])
        pay = sb("pay", [P, EJ, 4])
        slot_f, row_f = sb("slot_f", [P, EJ]), sb("row_f", [P, EJ])
        slot_i, low_i = sb("slot_i", [P, EJ], int32), sb("low_i", [P, EJ], int32)
        bucket = sb("bucket", [P, EJ], fp16)
        sort_room = sb("oh_or_permute", [128, EB * EJ // 2])
        oh = sort_room[0:P, :].bitcast(fp16).rearrange("p (b j) -> p b j", b=EB)
        room = sb("cum_or_xn", [P, EB * EJ // 2])
        cum = room[:].bitcast(fp16).rearrange("p (b j) -> p b j", b=EB)
        pg.XN = room[:, 0:NT * D].rearrange("p (j d) -> p j d", j=NT)
        widest = max(b - a for a, b in SORTED)
        slot_room = sb("slots_or_rings", [128, EB * widest])
        part = slot_room[0:P, :].rearrange("p (b j) -> p b j", b=EB)
        place_f = sb("place_f", [P, EJ])
        row1 = sb("row1", [1, EDGE_PAD])
        perm = Permute(pg, ctx, sort_room)
        W = sb("w_l0_gnn", [128, KD, D])
        bias = sb("bias_l0", [P, D])
        zero = sb("zero", [128, EDGE_PAD // 2])
        pay_st, idx_st = sb("pay_st", [P, 2, 8, 4]), sb("idx_st", [P, 2, 8], int32)
        owner = sb("owner", [1, EDGE_PAD])
        buf = slot_buffers(pg, ctx, "edges", EB)
        ld_edge, ld_x, ld_w, s_ch, s_const, tri_ok = (sem(n) for n in (
            "ld_edge", "ld_x", "ld_w", "sort_chain", "consts", "tri_ok"))
        tot_ready, tot_done, rows_ok, zeroed, cleared = (sem(n) for n in (
            "tot_ready", "tot_done", "slots_ok", "zeroed", "cleared"))
        s_tick, s_back, s_pool, s_oh = (sem(n) for n in ("tick", "payload_back", "pool_chain", "onehots"))
        staged = [sem(f"staged{h}") for h in range(2)]
        wiped = pg.arrivals(16, 16)
        scat = pg.arrivals(16, 16 * (SCATTERED // 16))
        norm = Norm(pg, ctx, "ln0", "rows", weight=W, dram=pg.H, room=slot_room)
        CLEARS = 2

        with pg.block() as block:
            @block.sync
            def _(sp):
                sp.dma_start(src_i[:], src.rearrange("(p j) -> p j", p=P)).then_inc(ld_edge, 16)
                sp.dma_start(dst_i[:], dst.rearrange("(p j) -> p j", p=P)).then_inc(ld_edge, 16)
                sp.dma_start(slot_f[:], edge_weight.rearrange("(p j) -> p j", p=P)).then_inc(ld_edge, 16)
                sp.dma_start(pg.X[:], x.rearrange("(j p) d -> p j d", p=P)).then_inc(ld_x, 16)
                load_weight_chunks(sp, W[:], w_l0, ld_w)
                sp.dma_start(bias[:], bias_l0.partition_broadcast(P)).then_inc(ld_w, 16)
                sp.wait_ge(zeroed, 1)
                for rows, n in ((pg.XS0, MOE_TILES), (pg.XS1, SHARED_TILES + MOE_TILES)):
                    sp.dma_start(rows.rearrange("(t p) d -> p t d", p=128),
                                 zero[:, 0:D].unsqueeze(1).to_broadcast([128, n, D])).then_inc(cleared, 16)
                for q, (start, end) in enumerate(SORTED):
                    sp.wait_ge(rows_ok, q + 1)
                    with sp.Fori(0, (min(end, SCATTERED) - start) // 16) as n:
                        i = n + start // 16
                        for h in range(2):
                            for k in range(8):
                                scat[8 * h + k].wait(sp, 16 * i)
                            cols = bass.ds(i * 16 + 8 * h, 8)
                            sp.dma_start(pay_st[:, h, :, :], pay[:, cols, :]).then_inc(staged[h], 16)
                            sp.dma_start(idx_st[:, h, :], slot_i[:, cols]).then_inc(staged[h], 16)
                for k in range(16):
                    scat[k].wait(sp, 16 * (SCATTERED // 16))
                sp.dma_start(pg.slots[:].rearrange("p c f -> p (c f)"),
                             pg.pay_dram.rearrange("(p c) f -> p (c f)", p=128)).then_inc(s_back, 16)
                sp.wait_ge(s_back, 16)

            @block.gpsimd
            def _(pool):
                pg.clear_used(pool)
                step = Chain(pool, s_pool)
                g = nc.gpsimd
                step(g.memset(zero[:], 0.0))
                pool.sem_inc(zeroed, 1)
                f = {"allow_small_or_imprecise_dtypes": True}
                step(g.iota(pg.col[:], [[1, 128]], base=0, channel_multiplier=0, **f))
                step(g.iota(pg.moe_tiles[:], [[1, MOE_TILES]], base=0, channel_multiplier=0, **f))
                step(g.iota(pg.tiles[:], [[1, EDGE_PAD]], base=0, channel_multiplier=0, **f))
                step(g.iota(perm.tile_row[:], [[1, EDGE_PAD]], base=0, channel_multiplier=0, **f))
                step(g.iota(pg.part[:], [[1, 1]], base=0, channel_multiplier=1, **f))
                step(g.iota(pg.hot_col[:], [[1, HOT * P]], base=0, channel_multiplier=0, **f))
                step(g.iota(pg.prio[:], [[-1, NX]], base=NX, channel_multiplier=0, **f))
                step(g.memset(pg.ones[:], 1.0))
                pool.sem_inc(s_const, 1)
                piece = 128 // 16
                for k in range(16):
                    rows = slice(k * piece * EDGE_PAD, (k + 1) * piece * EDGE_PAD)
                    pool.dma_start(
                        pg.pay_dram[rows, :].rearrange("(p a c) f -> p a (c f)", p=piece, a=8),
                        zero[k * piece:(k + 1) * piece, :].unsqueeze(1).to_broadcast([piece, 8, EDGE_PAD // 2])
                    ).then_inc(wiped[k].sem, 16)
                for k in range(16):
                    wiped[k].wait(pool, 16)
                pool.wait_ge(cleared, 16 * CLEARS)
                with pool.Fori(0, SCATTERED // 16) as i:
                    for h in range(2):
                        pool.wait_ge(staged[h], 32 * i + 32)
                        pool.sem_inc(s_tick, 1)
                        for k in range(8):
                            g.indirect_dma_start(
                                pg.pay_dram, bass.IndirectOffsetOnAxis(ap=idx_st[:, h, k:k + 1], axis=0),
                                pay_st[:, h, k, :], None).then_inc(scat[8 * h + k].sem, 16)

            @block.vector
            def _(dve):
                step = Chain(dve, s_ch)
                v = nc.vector
                dve.wait_ge(s_const, 1)
                step(v.tensor_scalar(pg.ident[:], pg.col[:], pg.part[:, 0:1], None, ALU.is_equal))
                v.tensor_scalar(pg.tri[:], pg.col[:], pg.part[:, 0:1], None, ALU.is_gt).then_inc(tri_ok, 1)
                dve.wait_ge(ld_edge, 48)
                step(v.tensor_copy(src_f[:], src_i[:]))
                step(v.tensor_copy(pay[:, :, 2], dst_i[:]))
                step(v.tensor_copy(pay[:, :, 1], slot_f[:]))
                step(v.memset(pay[:, :, 3], 0.0))
                step(v.tensor_scalar(slot_i[:], src_f[:], 1.0 / P, None, ALU.mult))
                step(v.tensor_copy(blk[:], slot_i[:]))
                step(v.scalar_tensor_tensor(row_f[:], blk[:], -float(P), src_f[:], ALU.mult, ALU.add))
                step(v.scalar_tensor_tensor(blk[:], row_f[:], 0.0, blk[:], ALU.is_ge, ALU.add))
                step(v.scalar_tensor_tensor(blk[:], row_f[:], float(P), blk[:], ALU.is_ge, ALU.add))
                step(v.tensor_scalar(blk[:], blk[:], -1.0, None, ALU.add))
                step(v.scalar_tensor_tensor(pay[:, :, 0], blk[:], -float(P), src_f[:], ALU.mult, ALU.add))
                step(v.tensor_scalar(row_f[:], pay[:, :, 2], float(HOT * P), float(NT), ALU.is_lt, ALU.mult))
                step(v.tensor_tensor(bucket[:], blk[:], row_f[:], ALU.add))
                for b in range(EB):
                    v.tensor_scalar(oh[:, b, :], bucket[:], float(b), None, ALU.is_equal).then_inc(s_oh, 1)
                count = EB
                dve.wait_ge(s_oh, count)
                bucket_bases(nc, step, dve, oh, cum, EJ, EB, buf, tot_ready, tot_done,
                             split=(NT, ROUND))
                for start, end in SORTED:
                    c, wide = slice(start, end), part[:, :, 0:end - start]
                    for b in range(EB):
                        v.scalar_tensor_tensor(wide[:, b, :], cum[:, b, c], buf["base"][:, b:b + 1], oh[:, b, c],
                                               ALU.add, ALU.mult).then_inc(s_oh, 1)
                    count += EB
                    dve.wait_ge(s_oh, count)
                    step(v.tensor_reduce(slot_f[:, c], wide.rearrange("p b j -> p j b"), AXIS.X, ALU.add))
                    step(v.tensor_copy(slot_i[:, c], slot_f[:, c]))
                    step(v.tensor_scalar(low_i[:, c], slot_i[:, c], SLOT - 1, None, ALU.bitwise_and))
                    step(v.tensor_scalar(slot_i[:, c], slot_i[:, c], 7, None, ALU.arith_shift_right))
                    step(v.tensor_copy(slot_f[:, c], slot_i[:, c]))
                    step(v.tensor_copy(place_f[:, c], low_i[:, c]))
                    step(v.scalar_tensor_tensor(row_f[:, c], place_f[:, c], float(EDGE_PAD), slot_f[:, c],
                                                ALU.mult, ALU.add))
                    step(v.tensor_copy(slot_i[:, c], row_f[:, c]))
                    dve.sem_inc(rows_ok, 1)
                owner_table(nc, step, pg.tiles, buf["start"], EB, EDGE_PAD, owner[:])
                step(v.tensor_scalar(pg.owner_n[:], owner[:], float(P), None, ALU.mult))
                step(v.tensor_copy(pg.owner_t[:], owner[:]))
                step(v.tensor_scalar(owner[:], owner[:], -float(NT), 0.0, ALU.add, ALU.max))
                step(v.tensor_scalar(pg.owner_h[:], owner[:], float(P), None, ALU.mult))
                first, end = buf["start"][0:1, NT:NT + 1], buf["start"][0:1, EB:EB + 1]
                step(v.tensor_copy(pg.lists[:, FIRST:FIRST + 1], first))
                step(v.tensor_scalar(pg.lists[:, COLD:COLD + 1], first, 1.0 / ROUND, None, ALU.mult))
                step(v.tensor_tensor(row1[:, 0:1], end, first, ALU.subtract))
                step(v.tensor_scalar(owner[:, 0:HOT_ROUNDS], pg.tiles[:, 0:HOT_ROUNDS], float(HR), row1[:, 0:1],
                                     ALU.mult, ALU.is_lt))
                step(v.tensor_reduce(row1[:, 1:2], owner[:, 0:HOT_ROUNDS], AXIS.X, ALU.add))
                step(v.tensor_copy(pg.lists[:, HOTTER:HOTTER + 1], row1[:, 1:2]))
                step(v.tensor_copy(row1[:, 2:3], pg.lists[:, COLD:COLD + 1]))
                step(v.tensor_tensor(pg.lists[:, BOTH:BOTH + 1], row1[:, 1:2], row1[:, 2:3], ALU.min))
                step(v.tensor_tensor(pg.lists[:, ANY:ANY + 1], row1[:, 1:2], row1[:, 2:3], ALU.max))
                perm.prepare(step, pay, SCATTERED)
                perm.vector(dve, step, slot_f, place_f, SCATTERED)
                norm.vector(dve, (ld_x, 16))
                dve.wait_ge(ld_w, 32)
                step(v.tensor_tensor(pg.X[:], pg.X[:], bias[:].unsqueeze(1).to_broadcast([P, NT, D]), ALU.add))
                dve.wait_ge(s_back, 16)
                perm.merge(step)

            @block.tensor
            def _(pe):
                pe.wait_ge(s_const, 1)
                pe.wait_ge(tri_ok, 1)
                bucket_totals(nc, pe, pg, buf, EB, tot_ready, tot_done)
                perm.tensor(pe)
                norm.tensor(pe, (ld_w, 32))

            @block.scalar
            def _(act):
                perm.scalar(act)
                norm.scalar(act)


class Aggregate:
    BANKS = 4

    def __init__(self, pg, ctx, tag, by, acc, room=None):
        self.pg, self.by, self.acc = pg, by, acc
        sb = lambda n, s, d=fp32: pg.sb(f"{tag}_{n}", s, d, ctx)
        sem = lambda n: pg.sem(f"{tag}_{n}", ctx)
        if room is None:
            room = sb("room", [128, ROUND * (D + P)])
        self.G = room[:, 0:ROUND * D].rearrange("p (k d) -> p k d", k=ROUND)
        self.S = room[:, ROUND * D:ROUND * (D + P)].rearrange("p (k q) -> p k q", k=ROUND)
        self.key = sb("key", [128, ROUND, 2])
        self.idx = sb("idx", [128, ROUND], int32)
        self.s_got = [pg.sem(f"{tag}_arrived{q}") for q in range(ROUND // 4)]
        self.s_key, self.s_hot, self.s_mm, self.s_acc, self.s_tick = (
            sem(n) for n in ("key", "hot", "mm", "acc", "tick"))

    def rounds(self, eng, k=COLD):
        return eng.value_load(self.pg.lists[0:1, k:k + 1], min_val=0, max_val={
            FIRST: COLD_ROUNDS * ROUND, COLD: COLD_ROUNDS, HOTTER: HOT_ROUNDS,
            BOTH: min(COLD_ROUNDS, HOT_ROUNDS), ANY: max(COLD_ROUNDS, HOT_ROUNDS)}[k])

    def stage(self, act, i, q):
        act.wait_ge(self.s_mm, i * ROUND + 4 * (q + 1))
        act.wait_ge(self.s_hot, i * ROUND + 4 * (q + 1))
        cols = self.pg.tiles_at(i * ROUND + 4 * q, 4)
        four = slice(4 * q, 4 * q + 4)
        self.pg.nc.scalar.copy(self.idx[:, four], self.pg.slots[:, cols, 2])
        self.pg.nc.scalar.copy(self.key[:, four, :], self.pg.slots[:, cols, 0:2]).then_inc(self.s_key, 1)

    def stage_round(self, act, n, i):
        with act.If(n > i - 1):
            self.stage(act, i, 0)
            self.stage(act, i, 1)
        with act.If(n > i):
            self.stage(act, i, 2)
            self.stage(act, i, 3)

    def gather_round(self, pool, n, i):
        with pool.If(n > i):
            for q in range(4):
                pool.wait_ge(self.s_key, 4 * i + q + 1)
                pool.wait_ge(self.s_mm, i * ROUND + 4 * (q + 1))
                pool.sem_inc(self.s_tick, 1)
                for k in range(4 * q, 4 * q + 4):
                    self.pg.nc.gpsimd.indirect_dma_start(
                        self.G[:, k, :], None, self.pg.H,
                        bass.IndirectOffsetOnAxis(ap=self.idx[:, k:k + 1], axis=0)).then_inc(self.s_got[q], 16)

    def target(self, k):
        b = k % self.BANKS
        if self.by == "node":
            return self.pg.ps[0:P, b, 0:D]
        return self.pg.ps[:, b, 0:KD * P].rearrange("p (k q) -> p k q", k=KD)

    def product_round(self, pe, n, i):
        with pe.If(n > i):
            for q in range(4):
                self.product_four(pe, i, q)

    def product_four(self, pe, i, q):
        nc = self.pg.nc
        pe.wait_ge(self.s_got[q], 64 * i + 64)
        for k in range(4 * q, 4 * q + 4):
            pe.wait_ge(self.s_hot, ROUND * i + ROUND + k + 1)
            pe.wait_ge(self.s_acc, ROUND * i + k + 1)
            out = self.target(k)
            if self.by == "node":
                last = nc.tensor.matmul(out, self.S[:, k, :], self.G[:, k, :], start=True, stop=True)
            else:
                for c in range(KD):
                    last = nc.tensor.matmul(out[:, c, :], self.G[:, k, c * 128:(c + 1) * 128],
                                            self.S[:, k, :], start=True, stop=True)
            last.then_inc(self.s_mm, 1)

    def onehot(self, dve, i, k):
        if k % 4 == 0:
            dve.wait_ge(self.s_key, 4 * i + k // 4 + 1)
        dve.wait_ge(self.s_mm, ROUND * i + k + 1)
        self.pg.nc.vector.tensor_scalar(self.S[:, k, :], self.pg.col[:, 0:P], self.key[:, k, 0:1],
                                        self.key[:, k, 1:2], ALU.is_equal, ALU.mult).then_inc(self.s_hot, 1)

    def owners(self, i, h):
        table = self.pg.owner_t if self.by == "node" else self.pg.owner_n
        _, own = self.pg.nc.values_load_multi_w_load_instructions(
            table[0:1, self.pg.tiles_at(i * ROUND + 8 * h, 8)], engines=(mybir.EngineType.DVE,),
            min_val=0, max_val=NT - 1 if self.by == "node" else N - P)
        return own

    def add(self, dve, i, k, own):
        nc, t = self.pg.nc, ROUND * i + k
        dve.wait_ge(self.s_mm, ROUND + 1 + t)
        dve.wait_ge(self.s_acc, self.BANKS + t)
        if self.by == "node":
            a, p = self.acc[:, bass.ds(own, 1), :], self.target(k).unsqueeze(1)
        else:
            a, p = self.acc[:, :, bass.ds(own, P)], self.target(k)
        nc.vector.tensor_tensor(a, a, p, ALU.add).then_inc(self.s_acc, 1)

    def vector_start(self, dve):
        dve.sem_inc(self.s_hot, ROUND)
        dve.sem_inc(self.s_acc, self.BANKS)
        for k in range(8):
            self.onehot(dve, 0, k)

    def add_round(self, dve, n, i):
        with dve.If(n > i):
            for h in range(2):
                own = self.owners(i, h)
                for q in (2 * h, 2 * h + 1):
                    self.add_four(dve, i, q, own)

    def add_four(self, dve, i, q, own):
        for k in range(4 * q, 4 * q + 4):
            self.add(dve, i, k, own[k % 8])
            self.onehot(dve, i + k // 8, (k + 8) % ROUND)


def stage_aggregate_nodes(pg):
    nc = pg.nc
    SPAN = 4
    Q = HR // QUAD
    with ExitStack() as ctx:
        agg = Aggregate(pg, ctx, "agg0", "node", pg.X)
        sb = lambda n, s, d=fp32: pg.sb(n, s, d, ctx)
        S, T = sb("hot_sources", [128, HR, P]), sb("hot_targets", [128, HR, HOT * P])
        away = sb("hot_away", [128, QUAD, HOT * P])
        key = sb("hot_key", [128, HR, 3])
        s_key, s_neg, s_away, s_src, s_dst, s_mm, s_add = (pg.sem(f"hot_{n}", ctx) for n in (
            "key", "negated", "away", "sources", "targets", "mm", "add"))

        def rounds_of_lists(eng, both_lists, either_list):
            both, some = agg.rounds(eng, BOTH), agg.rounds(eng, ANY)
            with eng.Fori(0, -(-(max(COLD_ROUNDS, HOT_ROUNDS) + 1) // SPAN)) as o:
                with eng.If(some > o * SPAN - 1):
                    with eng.Fori(0, SPAN) as s:
                        i = o * SPAN + s
                        with eng.If(both > i):
                            both_lists(i)
                        with eng.Else():
                            either_list(i)

        def block_psum(q):
            return pg.ps[0:P, 4 + q, 0:HOT * P].rearrange("p (d q) -> p d q", d=HOT)

        def stage_hot(act, first, i):
            act.wait_ge(s_src, i * HR + HR)
            act.wait_ge(s_dst, i * HR + HR)
            nc.scalar.copy(key[:, :, 0:2], pg.slots[:, pg.tiles_at(first + i * HR, HR), 0:2]).then_inc(s_key, 1)
            nc.scalar.activation(key[:, :, 2], pg.slots[:, pg.tiles_at(first + i * HR, HR), 2],
                                 ACT.Copy, scale=-1.0).then_inc(s_neg, 1)

        def targets(act, i, q):
            act.wait_ge(s_neg, i + 1)
            for u in range(QUAD):
                k = q * QUAD + u
                act.wait_ge(s_dst, i * HR + (k + HR - QUAD + 1))
                nc.scalar.activation(away[:, u, :], pg.hot_col[:], ACT.Abs,
                                     bias=key[:, k, 2:3]).then_inc(s_away, 1)
            act.wait_ge(s_mm, i * Q + (q + 1))
            for u in range(QUAD):
                k = q * QUAD + u
                act.wait_ge(s_away, i * HR + (k + 1))
                nc.scalar.activation(T[:, k, :], away[:, u, :], ACT.Relu, bias=pg.ones[:, 0:1],
                                     scale=-1.0).then_inc(s_dst, 1)

        def sources(dve, i, q):
            if q == 0:
                dve.wait_ge(s_key, i + 1)
            dve.wait_ge(s_mm, i * Q + (q + 1))
            for k in range(q * QUAD, (q + 1) * QUAD):
                nc.vector.tensor_scalar(S[:, k, :], pg.col[:, 0:P], key[:, k, 0:1], key[:, k, 1:2],
                                        ALU.is_equal, ALU.mult).then_inc(s_src, 1)

        def quad_product(pe, i, q):
            pe.wait_ge(s_add, i * Q + (q + 1))
            pe.wait_ge(s_src, i * HR + (HR + (q + 1) * QUAD))
            pe.wait_ge(s_dst, i * HR + (HR + (q + 1) * QUAD))
            for d in range(HOT):
                for u in range(QUAD):
                    k = q * QUAD + u
                    last = nc.tensor.matmul(block_psum(q)[:, d, :], T[:, k, d * P:(d + 1) * P], S[:, k, :],
                                            start=(u == 0), stop=(u == QUAD - 1))
            last.then_inc(s_mm, 1)

        def quad_add(dve, first, i, q):
            own = dve.value_load(pg.owner_h[0:1, pg.tiles_at(first + (i * HR + q * QUAD), 1)],
                                 min_val=0, max_val=N - P)
            dve.wait_ge(s_mm, i * Q + (Q + q + 1))
            dve.wait_ge(s_add, i * Q + (Q + q))
            a = pg.A[:, :, bass.ds(own, P)]
            nc.vector.tensor_tensor(a, a, block_psum(q), ALU.add).then_inc(s_add, 1)
            sources(dve, i + 1, q)

        with pg.block() as block:
            @block.scalar
            def _(act):
                n, m, first = agg.rounds(act), agg.rounds(act, HOTTER), agg.rounds(act, FIRST)
                act.sem_inc(s_dst, HR)

                def both_lists(i):
                    agg.stage(act, i, 0)
                    stage_hot(act, first, i)
                    for q in range(Q):
                        agg.stage(act, i, q + 1)
                        targets(act, i, q)

                def either_list(i):
                    with act.If(n > i - 1):
                        agg.stage(act, i, 0)
                    with act.If(m > i - 1):
                        stage_hot(act, first, i)
                    with act.If(n > i - 1):
                        agg.stage(act, i, 1)
                    with act.If(n > i):
                        agg.stage(act, i, 2)
                        agg.stage(act, i, 3)
                    with act.If(m > i):
                        for q in range(Q):
                            targets(act, i, q)

                rounds_of_lists(act, both_lists, either_list)

            @block.gpsimd
            def _(pool):
                pg.clear_used(pool)
                n = agg.rounds(pool)
                with pool.Fori(0, COLD_ROUNDS) as i:
                    agg.gather_round(pool, n, i)

            @block.tensor
            def _(pe):
                n, m = agg.rounds(pe), agg.rounds(pe, HOTTER)
                pe.sem_inc(agg.s_mm, ROUND)
                pe.sem_inc(s_mm, Q)

                def both_lists(i):
                    agg.product_four(pe, i, 0)
                    for q in range(Q):
                        quad_product(pe, i, q)
                        agg.product_four(pe, i, q + 1)

                def either_list(i):
                    agg.product_round(pe, n, i)
                    with pe.If(m > i):
                        for q in range(Q):
                            quad_product(pe, i, q)

                rounds_of_lists(pe, both_lists, either_list)

            @block.vector
            def _(dve):
                n, m, first = agg.rounds(dve), agg.rounds(dve, HOTTER), agg.rounds(dve, FIRST)
                dve.sem_inc(s_src, HR)
                agg.vector_start(dve)
                for q in range(Q):
                    sources(dve, 0, q)
                nc.vector.memset(pg.A[:], 0.0).then_inc(s_add, Q)

                def both_lists(i):
                    own = agg.owners(i, 0)
                    agg.add_four(dve, i, 0, own)
                    for q in range(Q):
                        if q == 1:
                            own = agg.owners(i, 1)
                        agg.add_four(dve, i, q + 1, own)
                        quad_add(dve, first, i, q)

                def either_list(i):
                    agg.add_round(dve, n, i)
                    with dve.If(m > i):
                        for q in range(Q):
                            quad_add(dve, first, i, q)

                rounds_of_lists(dve, both_lists, either_list)

    with ExitStack() as ctx:
        Hh = pg.sb("hot_rows", [P, HOT, D], ctx=ctx)
        s_ld, s_mm, s_add = (pg.sem(f"share_{n}", ctx) for n in ("rows", "mm", "add"))
        with pg.block() as block:
            @block.sync
            def _(sp):
                load_hot_rows(pg, sp, Hh, s_ld)

            @block.gpsimd
            def _(pool):
                pg.clear_used(pool)

            @block.tensor
            def _(pe):
                pe.wait_ge(s_ld, 16)
                for j in range(NT):
                    if j >= BANKS:
                        pe.wait_ge(s_add, j - BANKS + 1)
                    for d in range(HOT):
                        last = nc.tensor.matmul(pg.ps[0:P, j % BANKS, 0:D], pg.A[:, d, j * P:(j + 1) * P],
                                                Hh[:, d, :], start=(d == 0), stop=(d == HOT - 1))
                    last.then_inc(s_mm, 1)

            @block.vector
            def _(dve):
                for j in range(NT):
                    dve.wait_ge(s_mm, j + 1)
                    nc.vector.tensor_tensor(pg.X[:, j, :], pg.X[:, j, :], pg.ps[0:P, j % BANKS, 0:D],
                                            ALU.add).then_inc(s_add, 1)
                    row_stats(pg, dve, j, s_add)


def load_hot_rows(pg, eng, dst, sem):
    eng.dma_start(dst[:], pg.H[0:HOT * P, :].rearrange("(d p) f -> p d f", p=P)).then_inc(sem, 16)


def stage_aggregate_features(pg, tag, acc, room):
    nc = pg.nc
    W = 2 * P
    PIECES = N // W
    with ExitStack() as ctx:
        agg = Aggregate(pg, ctx, tag, "feature", acc, room)
        Hh = pg.sb(f"{tag}_hot_rows", [P, HOT, D], ctx=ctx)
        s_ld, s_mm, s_add, s_tick = (pg.sem(f"{tag}_share_{n}", ctx) for n in ("rows", "mm", "add", "tick"))
        def product(pe, c, first, width):
            for d in range(HOT):
                last = nc.tensor.matmul(pg.ps[:, 4 + c, 0:width], Hh[:, d, c * 128:(c + 1) * 128],
                                        pg.A[:, d, bass.ds(first, width)], start=(d == 0), stop=(d == HOT - 1))
            last.then_inc(s_mm, 1)

        def add(c, first, width):
            a = acc[:, c, bass.ds(first, width)]
            nc.vector.tensor_tensor(a, a, pg.ps[:, 4 + c, 0:width], ALU.add).then_inc(s_add, 1)

        with pg.block() as block:
            @block.sync
            def _(sp):
                load_hot_rows(pg, sp, Hh, s_ld)

            @block.scalar
            def _(act):
                n = agg.rounds(act)
                with act.Fori(0, COLD_ROUNDS + 1) as i:
                    agg.stage_round(act, n, i)

            @block.gpsimd
            def _(pool):
                pg.clear_used(pool)
                n = agg.rounds(pool)
                with pool.Fori(0, COLD_ROUNDS) as i:
                    agg.gather_round(pool, n, i)

            @block.tensor
            def _(pe):
                n = agg.rounds(pe)
                pe.sem_inc(agg.s_mm, ROUND)
                pe.wait_ge(s_ld, 16)
                for c in range(KD):
                    product(pe, c, PIECES * W, P)

                def piece(i, c):
                    pe.wait_ge(s_add, i * KD + (c + 1))
                    product(pe, c, i * W, W)

                with pe.Fori(0, PIECES) as i:
                    with pe.If(n > i):
                        for c in range(KD):
                            agg.product_four(pe, i, 2 * c)
                            agg.product_four(pe, i, 2 * c + 1)
                            piece(i, c)
                    with pe.Else():
                        for c in range(KD):
                            piece(i, c)
                with pe.Fori(0, COLD_ROUNDS - PIECES) as i:
                    agg.product_round(pe, n, i + PIECES)

            @block.vector
            def _(dve):
                n = agg.rounds(dve)
                agg.vector_start(dve)
                for c in range(KD):
                    dve.wait_ge(s_mm, c + 1)
                    add(c, PIECES * W, P)

                def piece(i, c):
                    dve.wait_ge(s_mm, i * KD + (KD + c + 1))
                    add(c, i * W, W)

                def four(i, q, own):
                    dve.wait_ge(s_add, i * KD + (KD if q < 3 else KD + 1))
                    dve.sem_inc(s_tick, 1)
                    agg.add_four(dve, i, q, own)

                def additions(i, count):
                    dve.wait_ge(agg.s_acc, i * ROUND + (count + agg.BANKS))
                    dve.sem_inc(s_tick, 1)

                with dve.Fori(0, PIECES) as i:
                    with dve.If(n > i):
                        own = agg.owners(i, 0)
                        four(i, 0, own)
                        four(i, 1, own)
                        own = agg.owners(i, 1)
                        four(i, 2, own)
                        additions(i, 12)
                        piece(i, 0)
                        four(i, 3, own)
                        additions(i, 16)
                        piece(i, 1)
                    with dve.Else():
                        for c in range(KD):
                            piece(i, c)
                dve.wait_ge(s_add, KD * (PIECES + 1))
                with dve.Fori(0, COLD_ROUNDS - PIECES) as i:
                    agg.add_round(dve, n, i + PIECES)


def rolled(eng, first, end, unroll, body):
    n = (end - first) // unroll
    if n > 1:
        with eng.Fori(0, n) as i:
            for u in range(unroll):
                body(i * unroll + (first + u), (first + u) % unroll)
    else:
        n = 0
    for t in range(first + n * unroll, end):
        body(t, t % unroll)


def rolled_owned(pg, eng, engine_type, table, top, first, end, unroll, lo, hi, body):
    def owners(start, n):
        _, regs = pg.nc.values_load_multi_w_load_instructions(
            table[0:1, bass.ds(start, n)], engines=(engine_type,), min_val=0, max_val=top)
        return regs

    n = (end - first) // unroll
    if n > 1:
        with eng.Fori(0, n) as i:
            regs = owners(i * unroll + (first + lo), unroll + hi - lo)
            for u in range(unroll):
                body(i * unroll + (first + u), lambda k, u=u: regs[u + k - lo], (first + u) % 2)
    else:
        n = 0
    done = first + n * unroll
    for t in range(done, end):
        regs = owners(t + lo, 1 + hi - lo)
        body(t, lambda k: regs[k - lo], t % 2)


def shared_rows(rows, first, end):
    cut, gap = SHARED_LEAD * SLOT, MOE_TILES * SLOT
    j, p = cut // P, cut % P
    pieces = []
    for lo, hi, a, b, at in ((first, min(end, j), 0, P, 0), (max(first, j), min(end, j + 1), 0, p, 0),
                             (max(first, j), min(end, j + 1), p, P, gap), (max(first, j + 1), end, 0, P, gap)):
        if lo < hi:
            n = lo * P + a + at
            pieces.append((slice(a, b), slice(lo, hi), rows[n:n + (hi - lo - 1) * P + b - a, :].rearrange(
                "(j p) d -> p j d", j=hi - lo)))
    return pieces


class Experts:

    def __init__(self, pg, ctx, tag, F, shared, XS, YS):
        self.pg, self.tag, self.F, self.FK, self.shared, self.XS, self.YS = pg, tag, F, F // 128, shared, XS, YS
        self.T = shared + MOE_TILES
        self.lead = SHARED_LEAD if shared else 0
        self.NE = NX + (1 if shared else 0)
        sb = lambda n, s, d=fp32: pg.sb(f"{tag}_{n}", s, d, ctx)
        self.W1 = sb("w1", [128, self.NE, KD, F])
        self.W2 = sb("w2", [128, self.NE, self.FK, D])
        self.b1 = sb("b1", [128, self.NE, self.FK])
        self.b2 = sb("b2", [128, self.NE, D])
        self.wr = sb("wr", [128, KD, NX])
        self.slot_i = sb("slot_i", [P, TOP * NT], int32)
        self.gate = sb("gate", [P, TOP, NT])
        self.owner = sb("owner", [1, self.T], int32)
        self.s_wr, self.s_w = pg.sem(f"{tag}_router"), pg.sem(f"{tag}_weights")
        self.loads = 16 * (2 + 2 * NX + (4 if shared else 0))

    def load(self, eng, dst, src, sem=None):
        with self.pg.nc.allow_non_contiguous_dma(reason="a few vectors, one value a partition"):
            eng.dma_start(dst, src).then_inc(sem or self.s_w, 16)

    def load_weights(self, eng, wr, w1, b1, w2, b2, shared=None):
        for k in range(KD):
            self.load(eng, self.wr[:, k, :], wr(k), self.s_wr)
        self.load(eng, self.b1[:, 0:NX, :], b1.rearrange("e (k p) -> p e k", p=128))
        self.load(eng, self.b2[:, 0:NX, :], b2.partition_broadcast(128))
        for e in range(NX):
            self.load(eng, self.W1[:, e, :, :], w1[e].rearrange("(k p) f -> p k f", p=128))
            self.load(eng, self.W2[:, e, :, :], w2[e].rearrange("(k p) f -> p k f", p=128))
        if shared:
            v1, c1, v2, c2 = shared
            self.load(eng, self.W1[:, NX, :, :], v1.rearrange("(k p) f -> p k f", p=128))
            self.load(eng, self.W2[:, NX, :, :], v2.rearrange("(k p) f -> p k f", p=128))
            self.load(eng, self.b1[:, NX, :], c1.rearrange("(k p) -> p k", p=128))
            self.load(eng, self.b2[:, NX, :], c2.partition_broadcast(128))


def stage_route(pg, ex, keep_x=None, load=None):
    nc = pg.nc
    B, J = NX, TOP * NT
    with ExitStack() as ctx:
        sb = lambda n, s, d=fp32: pg.sb(f"{ex.tag}_{n}", s, d, ctx)
        sem = lambda n: pg.sem(f"{ex.tag}_{n}", ctx)
        logit, prob = sb("logit", [P, NT, NX]), sb("prob", [P, NT, NX])
        cand = sb("cand", [P, NT, NX])
        top, best = sb("top", [P, TOP, NT]), sb("best", [P, NT])
        oh, cum = sb("oh", [P, B, J]), sb("cum", [P, B, J])
        slot_f, own = sb("slot_f", [P, J]), sb("own", [1, ex.T])
        buf = slot_buffers(pg, ctx, ex.tag, B)
        s_ch, s_log, s_exp, tot_ready, tot_done, s_kept = (
            sem(n) for n in ("route_chain", "logits", "exp", "tot_ready", "tot_done", "kept"))
        norm = Norm(pg, ctx, ex.tag, "router", weight=ex.wr, logits=logit)
        with pg.block() as block:
            @block.sync
            def _(sp):
                if keep_x is not None:
                    sp.dma_start(keep_x.rearrange("(j p) d -> p j d", p=P), pg.X[:]).then_inc(s_kept, 16)
                if load:
                    load(sp)
                if keep_x is not None:
                    sp.wait_ge(s_kept, 16)

            @block.gpsimd
            def _(pool):
                pg.clear_used(pool)

            @block.tensor
            def _(pe):
                norm.tensor(pe, (ex.s_wr, 16 * KD))
                bucket_totals(nc, pe, pg, buf, B, tot_ready, tot_done)

            @block.scalar
            def _(act):
                norm.scalar(act)
                act.wait_ge(s_log, 1)
                nc.scalar.activation(prob[:], logit[:], ACT.Exp).then_inc(s_exp, 1)

            @block.vector
            def _(dve):
                v = nc.vector
                step = Chain(dve, s_ch)
                wide = lambda a: a.unsqueeze(2).to_broadcast([P, NT, NX])
                prio = pg.prio[:].unsqueeze(1).to_broadcast([P, NT, NX])
                norm.vector(dve, x_free=(s_kept, 16) if keep_x is not None else None)
                step(v.tensor_reduce(best[:], logit[:], AXIS.X, ALU.max))
                v.tensor_tensor(logit[:], logit[:], wide(best[:]), ALU.subtract).then_inc(s_log, 1)
                dve.wait_ge(s_exp, 1)
                step(v.tensor_reduce(best[:], prob[:], AXIS.X, ALU.add))
                step(v.reciprocal(best[:], best[:]))
                step(v.tensor_tensor(prob[:], prob[:], wide(best[:]), ALU.mult))
                for c in range(TOP):
                    picked = oh[:, :, c * NT:(c + 1) * NT].rearrange("p e j -> p j e")
                    step(v.tensor_reduce(top[:, c, :], prob[:], AXIS.X, ALU.max))
                    step(v.tensor_tensor(cand[:], prob[:], wide(top[:, c, :]), ALU.is_equal))
                    step(v.tensor_tensor(cand[:], cand[:], prio, ALU.mult))
                    step(v.tensor_reduce(best[:], cand[:], AXIS.X, ALU.max))
                    step(v.tensor_tensor(picked, cand[:], wide(best[:]), ALU.is_equal))
                    if c + 1 < TOP:
                        step(v.scalar_tensor_tensor(prob[:], picked, -2.0, prob[:], ALU.mult, ALU.add))
                step(v.tensor_tensor(best[:], top[:, 0, :], top[:, 1, :], ALU.add))
                step(v.tensor_scalar(best[:], best[:], 1e-12, None, ALU.max))
                step(v.reciprocal(best[:], best[:]))
                for c in range(TOP):
                    step(v.tensor_tensor(ex.gate[:, c, :], top[:, c, :], best[:], ALU.mult))
                bucket_slots(nc, step, dve, oh[:], cum[:], J, B, buf, tot_ready, tot_done, slot_f[:])
                if ex.shared:
                    step(v.tensor_scalar(slot_f[:], slot_f[:], float(ex.lead * SLOT), None, ALU.add))
                    step(v.memset(own[:], float(NX)))
                step(v.tensor_copy(ex.slot_i[:], slot_f[:]))
                owner_table(nc, step, pg.moe_tiles, buf["start"], B, MOE_TILES,
                            own[:, ex.lead:ex.lead + MOE_TILES])
                step(v.tensor_copy(ex.owner[:], own[:]))


def stage_experts(pg, ex, residual=None, x_kept=None):
    nc = pg.nc
    F, FK, T = ex.F, ex.FK, ex.T
    R = 2
    NB = -(-F // 512)
    with ExitStack() as ctx:
        sb = lambda n, s, d=fp32: pg.sb(f"{ex.tag}_{n}", s, d, ctx)
        sem = lambda n: pg.sem(f"{ex.tag}_{n}", ctx)
        xs, xt = sb("xs", [128, R, D]), sb("xt", [128, R, KD, 128])
        hid, ht = sb("hid", [128, F]), sb("ht", [128, R, FK, 128])
        y = sb("y", [128, R, D])
        s_sh, s_ch, s_tick = sem("shared_rows"), sem("chain2"), sem("tick")
        s_sc, *s_st = pg.arrivals(1 + R, [16 * TOP * NT] + [16 * ((T - r + R - 1) // R) for r in range(R)])
        END = ex.lead + MOE_TILES
        RG = 3
        if ex.shared:
            g = sb("g_tail", [P, RG, TOP, D])
            s_back = pg.arrivals(1 + R + RG, [0] * (1 + R) + [32 * ((NT - r + RG - 1) // RG) for r in range(RG)])[1 + R:]
            s_kept, s_sum, s_gch = sem("kept_back"), sem("tail_sum"), sem("tail_chain")
            group = [range(u * NT // (T - END), (u + 1) * NT // (T - END)) for u in range(T - END)]
        s_ld = [sem(f"loaded{r}") for r in range(R)]
        s_a, s_xt, s_b, s_h, s_c, s_g, s_d, s_y = (sem(n) for n in (
            "x_transposed", "xt_ok", "fc1", "hid_ok", "h_transposed", "gelu", "fc2", "y_ok"))
        ps_x, ps_h = pg.ps[:, 0, 0:D], pg.ps[:, 1:1 + NB, :]
        ps_t, ps_y = pg.ps[:, 3:3 + NB, :], pg.ps[:, 5, 0:D]
        tile_rows = lambda ap, t: ap[bass.ds(t * SLOT, SLOT), :]

        def times16(t, r):
            return (t - r) * (16 // R) + 16

        def stored16(t, r):
            return (t - r) * (16 // R)

        with pg.block() as block:
            @block.gpsimd
            def _(pool):
                pg.clear_used(pool)
                for c in range(TOP):
                    for j in range(NT):
                        nc.gpsimd.indirect_dma_start(
                            ex.XS, bass.IndirectOffsetOnAxis(ap=ex.slot_i[:, c * NT + j:c * NT + j + 1], axis=0),
                            pg.XN[:, j, :], None).then_inc(s_sc.sem, 16)

                def store(t, r):
                    pool.wait_ge(s_y, t + 2)
                    pool.sem_inc(s_tick, 1)
                    pool.dma_start(tile_rows(ex.YS, t), y[:, r, :]).then_inc(s_st[r].sem, 16)

                def gather(j):
                    if j >= RG:
                        pool.wait_ge(s_sum, j - RG + 1)
                        pool.sem_inc(s_tick, 1)
                    for c in range(TOP):
                        nc.gpsimd.indirect_dma_start(
                            g[:, j % RG, c, :], None, ex.YS[0:END * SLOT, :], bass.IndirectOffsetOnAxis(
                                ap=ex.slot_i[:, c * NT + j:c * NT + j + 1], axis=0)
                        ).then_inc(s_back[j % RG].sem, 16)

                rolled(pool, 0, END, R, store)
                if ex.shared:
                    for r in range(R):
                        s_st[r].wait(pool, 16 * ((END - r + R - 1) // R))
                    for u, js in enumerate(group):
                        for j in js:
                            gather(j)
                        store(END + u, (END + u) % R)
                for r in range(R):
                    s_st[r].wait(pool, 16 * ((T - r + R - 1) // R))

            @block.sync
            def _(sp):
                def load(t, r):
                    sp.wait_ge(s_a, t + 1)
                    sp.dma_start(xs[:, r, :], tile_rows(ex.XS, t)).then_inc(s_ld[r], 16)

                if ex.shared:
                    pieces = shared_rows(ex.XS, 0, NT)
                    for p, j, rows in pieces:
                        sp.dma_start(rows, pg.XN[p, j, :]).then_inc(s_sh, 16)
                    sp.wait_ge(s_sh, 16 * len(pieces))
                    rolled(sp, 0, ex.lead, R, load)
                s_sc.wait(sp, 16 * TOP * NT)
                if ex.shared:
                    sp.dma_start(pg.X[:], x_kept.rearrange("(j p) d -> p j d", p=P)).then_inc(s_kept, 16)
                rolled(sp, ex.lead, T, R, load)

            @block.tensor
            def _(pe):
                pe.sem_inc(s_a, R)
                pe.wait_ge(ex.s_w, ex.loads)

                def expert(t):
                    return nc.tensor.value_load(ex.owner[0:1, t:t + 1], min_val=0, max_val=ex.NE - 1)

                def x_transpose(t, r):
                    pe.wait_ge(s_ld[r], times16(t, r))
                    pe.wait_ge(s_xt, t + 1)
                    for k in range(KD):
                        last = nc.tensor.transpose(ps_x[:, k * 128:(k + 1) * 128],
                                                   xs[:, r, k * 128:(k + 1) * 128], pg.ident[:])
                    last.then_inc(s_a, 1)

                def fc1(t, r, e):
                    pe.wait_ge(s_xt, t + 2)
                    pe.wait_ge(s_h, t + 1)
                    for n in range(NB):
                        w = min(512, F)
                        for k in range(KD):
                            last = nc.tensor.matmul(ps_h[:, n, 0:w], xt[:, r, k, :],
                                                    ex.W1[:, bass.ds(e, 1), k, n * 512:n * 512 + w]
                                                    .rearrange("p o w -> p (o w)"),
                                                    start=(k == 0), stop=(k == KD - 1))
                    last.then_inc(s_b, 1)

                def h_transpose(t, r):
                    pe.wait_ge(s_h, t + 2)
                    pe.wait_ge(s_g, t + 1)
                    for k in range(FK):
                        last = nc.tensor.transpose(ps_t[:, k // 4, (k % 4) * 128:(k % 4) * 128 + 128],
                                                   hid[:, k * 128:(k + 1) * 128], pg.ident[:])
                    last.then_inc(s_c, 1)

                def fc2(t, r, e):
                    pe.wait_ge(s_g, t + 2)
                    pe.wait_ge(s_y, t + 1)
                    for k in range(FK):
                        last = nc.tensor.matmul(ps_y, ht[:, r, k, :], ex.W2[:, bass.ds(e, 1), k, :]
                                                .rearrange("p o w -> p (o w)"),
                                                start=(k == 0), stop=(k == FK - 1))
                    last.then_inc(s_d, 1)

                def body(t, own, r):
                    fc1(t + 1, (r + 1) % R, own(1))
                    h_transpose(t, r)
                    x_transpose(t + 2, r)
                    fc2(t - 1, (r + 1) % R, own(-1))

                x_transpose(0, 0)
                fc1(0, 0, expert(0))
                x_transpose(1, 1)
                fc1(1, 1, expert(1))
                h_transpose(0, 0)
                x_transpose(2, 0)
                rolled_owned(pg, pe, mybir.EngineType.PE, ex.owner, ex.NE - 1, 1, T - 2, 4, -1, 1, body)
                t = T - 2
                fc1(t + 1, (t + 1) % R, expert(t + 1))
                h_transpose(t, t % R)
                fc2(t - 1, (t - 1) % R, expert(t - 1))
                h_transpose(t + 1, (t + 1) % R)
                fc2(t, t % R, expert(t))
                fc2(t + 1, (t + 1) % R, expert(t + 1))

            @block.scalar
            def _(act):
                act.sem_inc(s_g, 1)

                def gelu(t, own, r):
                    e = own(0)
                    act.wait_ge(s_c, t + 1)
                    act.wait_ge(s_d, t + 1)
                    for k in range(FK):
                        last = nc.scalar.activation(
                            ht[:, r, k, :], ps_t[:, k // 4, (k % 4) * 128:(k % 4) * 128 + 128], ACT.Gelu,
                            bias=ex.b1[:, bass.ds(e, 1), k])
                    last.then_inc(s_g, 1)

                rolled_owned(pg, act, mybir.EngineType.Activation, ex.owner, ex.NE - 1, 0, T, 8, 0, 0, gelu)

            @block.vector
            def _(dve):
                v = nc.vector
                if residual is not None:
                    step = Chain(dve, s_ch)
                    step(v.tensor_tensor(residual, residual, pg.XN[:], ALU.add))
                dve.sem_inc(s_xt, 1)
                dve.sem_inc(s_h, 1)
                dve.sem_inc(s_y, 1)
                dve.sem_inc(s_d, R)

                def x_copy(t, r):
                    dve.wait_ge(s_a, t + R + 1)
                    dve.wait_ge(s_b, t + 1)
                    v.tensor_copy(xt[:, r, :, :], ps_x.rearrange("p (k q) -> p k q", k=KD)).then_inc(s_xt, 1)

                def h_copy(t, r):
                    dve.wait_ge(s_b, t + R + 1)
                    dve.wait_ge(s_c, t)
                    for n in range(NB):
                        w = min(512, F)
                        last = v.tensor_copy(hid[:, n * 512:n * 512 + w], ps_h[:, n, 0:w])
                    last.then_inc(s_h, 1)

                def expert(t):
                    return v.value_load(ex.owner[0:1, t:t + 1], min_val=0, max_val=ex.NE - 1)

                def y_copy(t, r, e):
                    dve.wait_ge(s_d, t + R + 1)
                    s_st[r].wait(dve, stored16(t, r))
                    v.tensor_tensor(y[:, r, :], ps_y, ex.b2[:, bass.ds(e, 1), :].rearrange("p o d -> p (o d)"),
                                    ALU.add).then_inc(s_y, 1)

                def body(t, own, r):
                    h_copy(t + 1, (r + 1) % R)
                    x_copy(t + 2, r)
                    y_copy(t - 1, (r + 1) % R, own(-1))

                dve.sem_inc(s_b, R)
                x_copy(0, 0)
                h_copy(0, 0)
                x_copy(1, 1)
                h_copy(1, 1)
                x_copy(2, 0)
                def combine(j):
                    s_back[j % RG].wait(dve, 32 * (j // RG + 1))
                    a = pg.X[:, j, :]
                    weighted(v.scalar_tensor_tensor(a, g[:, j % RG, 0, :], ex.gate[:, 0, j:j + 1], a,
                                                    ALU.mult, ALU.add))
                    v.scalar_tensor_tensor(a, g[:, j % RG, 1, :], ex.gate[:, 1, j:j + 1], a,
                                           ALU.mult, ALU.add).then_inc(s_sum, 1)

                rolled_owned(pg, dve, mybir.EngineType.DVE, ex.owner, ex.NE - 1, 1, min(END + 1, T - 2), 4,
                             -1, -1, body)
                if ex.shared:
                    weighted = Chain(dve, s_gch)
                    dve.wait_ge(s_kept, 16)
                    for t in range(END + 1, T - 2):
                        body(t, lambda k: NX, t % R)
                        for j in group[t - END - 1]:
                            combine(j)
                t = T - 2
                h_copy(t + 1, (t + 1) % R)
                for u in (t - 1, t, t + 1):
                    y_copy(u, u % R, NX if ex.shared else expert(u))
                if ex.shared:
                    for js in group[T - END - 3:]:
                        for j in js:
                            combine(j)


def stage_combine(pg, ex):
    nc = pg.nc
    RG = 4
    with ExitStack() as ctx:
        sem = lambda n: pg.sem(f"{ex.tag}_{n}", ctx)
        g = pg.sb(f"{ex.tag}_g", [P, RG, TOP, D], ctx=ctx)
        s_g = pg.arrivals(RG, [32 * ((NT - r + RG - 1) // RG) for r in range(RG)])
        s_sum, s_ch = sem("sum"), sem("cchain")
        with pg.block() as block:
            @block.gpsimd
            def _(pool):
                pg.clear_used(pool)
                for j in range(NT):
                    r = j % RG
                    if j >= RG:
                        pool.wait_ge(s_sum, j - RG + 1)
                    for c in range(TOP):
                        nc.gpsimd.indirect_dma_start(
                            g[:, r, c, :], None, ex.YS, bass.IndirectOffsetOnAxis(
                                ap=ex.slot_i[:, c * NT + j:c * NT + j + 1], axis=0)).then_inc(s_g[r].sem, 16)

            @block.vector
            def _(dve):
                v = nc.vector
                step = Chain(dve, s_ch)
                for j in range(NT):
                    r, a = j % RG, pg.X[:, j, :]
                    s_g[r].wait(dve, 32 * (j // RG + 1))
                    step(v.scalar_tensor_tensor(a, g[:, r, 0, :], ex.gate[:, 0, j:j + 1], a, ALU.mult, ALU.add))
                    v.scalar_tensor_tensor(a, g[:, r, 1, :], ex.gate[:, 1, j:j + 1], a,
                                           ALU.mult, ALU.add).then_inc(s_sum, 1)
                    row_stats(pg, dve, j, s_sum)


def stage_finish(pg, ex, out):
    nc = pg.nc
    with ExitStack() as ctx:
        got = ex.W1[0:P].rearrange("p e k f -> p (e k f)")[:, 0:NT * D].rearrange("p (j d) -> p j d", j=NT)
        groups = range(0, NT, U)
        s_ld = [pg.sem(f"shared{j}", ctx) for j in groups]
        s_sum, s_out = pg.sem("finish_sum", ctx), pg.sem("finish_out", ctx)
        with pg.block() as block:
            @block.gpsimd
            def _(pool):
                pg.clear_used(pool)

            @block.sync
            def _(sp):
                for q, first in enumerate(groups):
                    for p, j, rows in shared_rows(ex.YS, first, first + U):
                        sp.dma_start(got[p, j, :], rows).then_inc(s_ld[q], 16)

            @block.vector
            def _(dve):
                for q, first in enumerate(groups):
                    dve.wait_ge(s_ld[q], 16 * len(shared_rows(ex.YS, first, first + U)))
                    j = slice(first, first + U)
                    nc.vector.tensor_tensor(pg.X[:, j, :], pg.X[:, j, :], got[:, j, :], ALU.add).then_inc(s_sum, 1)

            @block.scalar
            def _(act):
                for q, first in enumerate(groups):
                    act.wait_ge(s_sum, q + 1)
                    act.dma_start(out[first * P:(first + U) * P, :].rearrange("(j p) d -> p j d", p=P),
                                  pg.X[:, first:first + U, :]).then_inc(s_out, 16)
                act.wait_ge(s_out, 16 * len(groups))


class Dense:

    def __init__(self, pg, ctx, tag):
        self.pg = pg
        sb = lambda n, s, d=fp32: pg.sb(f"{tag}_{n}", s, d, ctx)
        sem = lambda n: pg.sem(f"{tag}_{n}", ctx)
        self.st = sb("st", [128, KD, len(CHUNKS), 6])
        self.mv = sb("mv", [128, KD, 2])
        self.std, self.tmp = sb("std", [128, KD]), sb("tmp", [128, KD])
        self.scale, self.shift = sb("scale", [128, 2, KD]), sb("shift", [128, 2, KD])
        self.rows = sb("rows2", [P, U, D])
        self.s_mm, self.s_ev, self.s_bn, self.s_ch, self.s_var, self.s_std, self.s_aff, self.s_relu = (
            sem(n) for n in ("mm", "ev", "bn", "chain", "var", "std", "aff", "relu"))
        self.s_out, self.s_tr, self.s_row = (sem(n) for n in ("relu_out", "trd", "row"))
        self.s_st = [sem(f"st{s}") for s in range(U)]
        self.G = KD * len(CHUNKS)

    def product(self, pe, which, weight, src):
        nc, ps = self.pg.nc, self.pg.ps
        for c, (s0, n) in enumerate(CHUNKS):
            if which:
                pe.wait_ge(self.s_relu, KD * (c + 1))
            for fo in range(KD):
                g = which * self.G + c * KD + fo
                if g >= BANKS:
                    pe.wait_ge(self.s_ev, g - BANKS + 1)
                for k in range(KD):
                    last = nc.tensor.matmul(ps[:, g % BANKS, 0:n], weight[:, k, fo * 128:(fo + 1) * 128],
                                            src[:, k, s0:s0 + n], start=(k == 0), stop=(k == KD - 1))
                last.then_inc(self.s_mm, 1)

    def evacuate(self, act, which, dst, bias):
        nc, ps = self.pg.nc, self.pg.ps
        for c, (s0, n) in enumerate(CHUNKS):
            for fo in range(KD):
                g = which * self.G + c * KD + fo
                act.wait_ge(self.s_mm, g + 1)
                nc.scalar.activation(dst[:, fo, s0:s0 + n], ps[:, g % BANKS, 0:n], ACT.Identity,
                                     bias=bias[:, fo:fo + 1]).then_inc(self.s_ev, 1)

    def statistics(self, dve, step, which, src, gamma, beta):
        v = self.pg.nc.vector
        for c, (s0, n) in enumerate(CHUNKS):
            for fo in range(KD):
                g = which * self.G + c * KD + fo
                dve.wait_ge(self.s_ev, g + 1)
                v.bn_stats(self.st[:, fo, c, :], src[:, fo, s0:s0 + n]).then_inc(self.s_bn, 1)
        dve.wait_ge(self.s_bn, (which + 1) * self.G)
        for fo in range(KD):
            step(v.bn_aggr(self.mv[:, fo, :], self.st[:, fo, :, :].rearrange("p c s -> p (c s)")))
        v.tensor_scalar(self.std[:], self.mv[:, :, 1], BN_EPS, None, ALU.add).then_inc(self.s_var, 1)
        dve.wait_ge(self.s_std, which + 1)
        scale, shift = self.scale[:, which, :], self.shift[:, which, :]
        step(v.reciprocal(self.std[:], self.std[:]))
        step(v.tensor_tensor(scale, self.std[:], gamma, ALU.mult))
        step(v.tensor_tensor(self.tmp[:], self.mv[:, :, 0], scale, ALU.mult))
        v.tensor_tensor(shift, beta, self.tmp[:], ALU.subtract).then_inc(self.s_aff, 1)

    def root(self, act, which):
        act.wait_ge(self.s_var, which + 1)
        self.pg.nc.scalar.activation(self.std[:], self.std[:], ACT.Sqrt).then_inc(self.s_std, 1)

    def relu(self, act, which, a):
        act.wait_ge(self.s_aff, which + 1)
        for s0, n in CHUNKS:
            for fo in range(KD):
                self.pg.nc.scalar.activation(
                    a[:, fo, s0:s0 + n], a[:, fo, s0:s0 + n], ACT.Relu,
                    bias=self.shift[:, which, fo:fo + 1],
                    scale=self.scale[:, which, fo:fo + 1]).then_inc(self.s_relu, 1)

    def relu_out(self, act, which, src, dst):
        act.wait_ge(self.s_aff, which + 1)
        for s0, n in CHUNKS:
            for fo in range(KD):
                self.pg.nc.scalar.activation(
                    dst[:, fo, s0:s0 + n], src[:, fo, s0:s0 + n], ACT.Relu,
                    bias=self.shift[:, which, fo:fo + 1],
                    scale=self.scale[:, which, fo:fo + 1]).then_inc(self.s_out, 1)

    def transposes(self, pe, src, ready):
        for j in range(NT):
            if j * P % CH == 0:
                pe.wait_ge(ready, KD * (j * P // CH + 1))
            if j >= BANKS:
                pe.wait_ge(self.s_row, j - BANKS + 1)
            for k in range(KD):
                last = self.pg.nc.tensor.transpose(self.pg.ps[0:P, j % BANKS, k * 128:(k + 1) * 128],
                                                   src[:, k, j * P:(j + 1) * P], self.pg.ident[:])
            last.then_inc(self.s_tr, 1)

    def rows_out(self, dve):
        for j in range(NT):
            dve.wait_ge(self.s_tr, j + 1)
            if j >= U:
                dve.wait_ge(self.s_st[j % U], 16 * (j // U))
            self.pg.nc.vector.tensor_copy(self.rows[:, j % U, :], self.pg.ps[0:P, j % BANKS, 0:D]
                                          ).then_inc(self.s_row, 1)

    def rows_store(self, sp):
        for j in range(NT):
            sp.wait_ge(self.s_row, j + 1)
            sp.dma_start(self.pg.H[j * P:(j + 1) * P, :], self.rows[:, j % U, :]).then_inc(self.s_st[j % U], 16)
        for s in range(U):
            sp.wait_ge(self.s_st[s], 16 * (NT // U))

    def rows_add(self, dve, X):
        for j in range(NT):
            dve.wait_ge(self.s_tr, j + 1)
            self.pg.nc.vector.tensor_tensor(X[:, j, :], X[:, j, :], self.pg.ps[0:P, j % BANKS, 0:D],
                                            ALU.add).then_inc(self.s_row, 1)
            row_stats(self.pg, dve, j, self.s_row)


def stage_network(pg, w_in, b_in, w1, b1, g1, be1, w2, b2, g_out, b_out):
    nc = pg.nc
    L = w1.shape[0]
    with ExitStack() as ctx:
        hf, z1 = (pg.sb(n, [128, KD, N], ctx=ctx) for n in ("h_features", "z1"))
        room = pg.sb("z2_or_xn", [128, NT * D], ctx=ctx)
        z2 = room[:, 0:KD * N].rearrange("p (k n) -> p k n", k=KD)
        pg.XN = room[0:P, :].rearrange("p (j d) -> p j d", j=NT)
        W = pg.sb("gnn_w", [128, 1 + 2 * L, KD, D], ctx=ctx)
        names = ("b1", "g1", "be1", "b2", "g_out", "b_out")
        par = {n: pg.sb(f"gnn_{n}", [128, L, KD], ctx=ctx) for n in names}
        bi = pg.sb("gnn_b_in", [128, KD], ctx=ctx)
        s_w = pg.sem("gnn_weights")
        loads = 16 * (1 + 2 * L + len(names) + 1)

        with ExitStack() as c:
            norm = Norm(pg, c, "ln2", "features", features=hf)
            d = Dense(pg, c, "in")
            with pg.block() as block:
                @block.sync
                def _(sp):
                    load_weight_chunks(sp, W[:, 0, :, :], w_in, s_w)
                    c.enter_context(nc.allow_non_contiguous_dma(reason="vectors, one value a partition"))
                    sp.dma_start(bi[:], b_in.rearrange("(k p) -> p k", p=128)).then_inc(s_w, 16)
                    for layer in range(L):
                        load_weight_chunks(sp, W[:, 1 + 2 * layer, :, :], w1[layer], s_w)
                        load_weight_chunks(sp, W[:, 2 + 2 * layer, :, :], w2[layer], s_w)
                    for n, a in zip(names, (b1, g1, be1, b2, g_out, b_out)):
                        sp.dma_start(par[n][:], a.rearrange("l (k p) -> p l k", p=128)).then_inc(s_w, 16)
                    d.rows_store(sp)

                @block.gpsimd
                def _(pool):
                    pg.clear_used(pool)

                @block.tensor
                def _(pe):
                    norm.tensor(pe)
                    pe.wait_ge(s_w, loads)
                    pe.wait_ge(norm.s_xt, NT)
                    d.product(pe, 0, W[:, 0, :, :], hf)
                    pe.wait_ge(d.s_ev, d.G)
                    d.transposes(pe, z1, d.s_ev)

                @block.scalar
                def _(act):
                    norm.scalar(act)
                    act.wait_ge(s_w, loads)
                    d.evacuate(act, 0, z1, bi)

                @block.vector
                def _(dve):
                    norm.vector(dve)
                    d.rows_out(dve)
        h, spare = z1, hf
        for layer in range(L):
            stage_aggregate_features(pg, f"agg{layer + 1}", h, room)
            with ExitStack() as c:
                d = Dense(pg, c, f"layer{layer}")
                p = {n: par[n][:, layer, :] for n in names}
                final = layer == L - 1
                with pg.block() as block:
                    @block.tensor
                    def _(pe):
                        d.product(pe, 0, W[:, 1 + 2 * layer, :, :], h)
                        d.product(pe, 1, W[:, 2 + 2 * layer, :, :], spare)
                        d.transposes(pe, z2 if final else h, d.s_out)

                    @block.scalar
                    def _(act):
                        d.evacuate(act, 0, spare, p["b1"])
                        d.root(act, 0)
                        d.relu(act, 0, spare)
                        d.evacuate(act, 1, z2, p["b2"])
                        d.root(act, 1)
                        d.relu_out(act, 1, z2, z2 if final else h)

                    @block.vector
                    def _(dve):
                        step = Chain(dve, d.s_ch)
                        d.statistics(dve, step, 0, spare, p["g1"], p["be1"])
                        d.statistics(dve, step, 1, z2, p["g_out"], p["b_out"])
                        if final:
                            d.rows_add(dve, pg.X)
                        else:
                            d.rows_out(dve)

                    @block.gpsimd
                    def _(pool):
                        pg.clear_used(pool)

                    @block.sync
                    def _(sp):
                        if not final:
                            d.rows_store(sp)


def run_mixture(pg, ex, load):
    stage_route(pg, ex, load=load)
    stage_experts(pg, ex, residual=pg.X[:])
    stage_combine(pg, ex)


def build(nc, x, src, dst, edge_weight, L0_gnn_W, L0_gnn_bias, L0_ffn_router_w, L0_ffn_w1, L0_ffn_b1,
          L0_ffn_w2, L0_ffn_b2, L1_gnn_W_in, L1_gnn_b_in, L1_gnn_W1, L1_gnn_b1, L1_gnn_g1, L1_gnn_be1,
          L1_gnn_W2, L1_gnn_b2, L1_gnn_g_out, L1_gnn_b_out, L1_ffn_Wr, L1_ffn_W1s, L1_ffn_b1s,
          L1_ffn_W2s, L1_ffn_b2s, L1_ffn_W1p, L1_ffn_b1p, L1_ffn_W2p, L1_ffn_b2p, out):
    with ExitStack() as ctx:
        pg = Program(nc, ctx)
        pg.ps = ctx.enter_context(nc.psum_tensor("ps", [128, 8, 512], fp32))
        pg.X = pg.sb("X", [P, NT, D])
        pg.stats = pg.sb("stats", [P, NT, 6])
        pg.col = pg.sb("col", [128, 128])
        pg.part = pg.sb("part", [128, 1])
        pg.moe_tiles = pg.sb("moe_tiles", [1, MOE_TILES])
        pg.ident = pg.sb("ident", [128, 128])
        pg.tri = pg.sb("tri", [128, 128])
        pg.ones = pg.sb("ones", [128, 128])
        pg.prio = pg.sb("prio", [P, NX])
        pg.H = nc.dram_tensor("h_rows", [N, D], fp32).ap()
        pg.pay_dram = nc.dram_tensor("payloads", [128 * EDGE_PAD, 4], fp32).ap()
        pg.XS0 = nc.dram_tensor("expert_rows0", [MOE_TILES * SLOT, D], fp32).ap()
        pg.YS0 = nc.dram_tensor("expert_out0", [MOE_TILES * SLOT, D], fp32).ap()
        pg.x_kept = nc.dram_tensor("x_kept", [N, D], fp32).ap()
        ST = SHARED_TILES + MOE_TILES
        pg.XS1 = nc.dram_tensor("expert_rows1", [ST * SLOT, D], fp32).ap()
        pg.YS1 = nc.dram_tensor("expert_out1", [ST * SLOT, D], fp32).ap()

        edges = ctx.enter_context(ExitStack())
        pg.slots = pg.sb("slots", [128, EDGE_PAD, 4], ctx=edges)
        pg.owner_t = pg.sb("owner_t", [1, EDGE_PAD], int32, ctx=edges)
        pg.owner_n = pg.sb("owner_n", [1, EDGE_PAD], int32, ctx=edges)
        pg.owner_h = pg.sb("owner_h", [1, EDGE_PAD], int32, ctx=edges)
        pg.lists = pg.sb("lists", [1, 5], int32, ctx=edges)
        pg.tiles = pg.sb("tiles", [1, EDGE_PAD], ctx=edges)
        pg.hot_col = pg.sb("hot_col", [128, HOT * P], ctx=edges)
        stage_prepare(pg, x, src, dst, edge_weight, L0_gnn_W, L0_gnn_bias)
        pg.A = pg.sb("A_hot", [P, HOT, N], ctx=edges)
        stage_aggregate_nodes(pg)
        with ExitStack() as c1:
            pg.XN = pg.sb("XN1", [P, NT, D], ctx=c1)
            ex = Experts(pg, c1, "moe0", D, 0, pg.XS0, pg.YS0)

            def load0(eng):
                ex.load_weights(eng, lambda k: L0_ffn_router_w.rearrange("e (k p) -> k p e", p=128)[k],
                                L0_ffn_w1, L0_ffn_b1, L0_ffn_w2, L0_ffn_b2)
            run_mixture(pg, ex, load0)
        stage_network(pg, L1_gnn_W_in, L1_gnn_b_in, L1_gnn_W1, L1_gnn_b1, L1_gnn_g1, L1_gnn_be1,
                      L1_gnn_W2, L1_gnn_b2, L1_gnn_g_out, L1_gnn_b_out)
        edges.close()
        with ExitStack() as c1:
            pg.XN = pg.X
            ex = Experts(pg, c1, "moe1", L1_ffn_W1s.shape[1], SHARED_TILES, pg.XS1, pg.YS1)

            def load1(eng):
                ex.load_weights(eng, lambda k: L1_ffn_Wr[k * 128:(k + 1) * 128, :],
                                L1_ffn_W1p, L1_ffn_b1p, L1_ffn_W2p, L1_ffn_b2p,
                                (L1_ffn_W1s, L1_ffn_b1s, L1_ffn_W2s, L1_ffn_b2s))
            stage_route(pg, ex, keep_x=pg.x_kept, load=load1)
            stage_experts(pg, ex, x_kept=pg.x_kept)
            stage_finish(pg, ex, out)


_INS = ['x', 'src', 'dst', 'edge_weight', 'L0_gnn_W', 'L0_gnn_bias', 'L0_ffn_router_w', 'L0_ffn_w1',
        'L0_ffn_b1', 'L0_ffn_w2', 'L0_ffn_b2', 'L1_gnn_W_in', 'L1_gnn_b_in', 'L1_gnn_W1', 'L1_gnn_b1',
        'L1_gnn_g1', 'L1_gnn_be1', 'L1_gnn_W2', 'L1_gnn_b2', 'L1_gnn_g_out', 'L1_gnn_b_out',
        'L1_ffn_Wr', 'L1_ffn_W1s', 'L1_ffn_b1s', 'L1_ffn_W2s', 'L1_ffn_b2s', 'L1_ffn_W1p',
        'L1_ffn_b1p', 'L1_ffn_W2p', 'L1_ffn_b2p']
_OUTS = [((N, D), 'float32')]


def kernel(**inputs):
    import numpy as _np
    import concourse.bacc as _bacc
    from concourse import mybir as _mybir
    from concourse.bass_utils import run_bass_kernel_spmd as _run

    nc = _bacc.Bacc("TRN2", target_bir_lowering=False, num_devices=1)
    arrays, args = {}, []
    for name in _INS:
        a = _np.ascontiguousarray(inputs[name])
        arrays[f"in_{name}_dram"] = a
        args.append(nc.dram_tensor(f"in_{name}_dram", a.shape, _mybir.dt.from_np(a.dtype), kind="ExternalInput").ap())
    for i, (shape, dtype) in enumerate(_OUTS):
        dt = _mybir.dt.from_np(_np.dtype(dtype))
        args.append(nc.dram_tensor(f"out_{i}_dram", shape, dt, kind="ExternalOutput").ap())
    build(nc, *args)
    r = _run(nc, [arrays], core_ids=[0])
    got = tuple(r.results[0][f"out_{i}_dram"] for i in range(len(_OUTS)))
    return got[0]
```
